# Optimizing a Trainium2 kernel written in Bass

```python
import numpy as np
import jax
import jax.numpy as jnp

def _softmax(x, axis=-1):
    return jax.nn.softmax(x, axis=axis)

def _gelu(x):
    return jax.nn.gelu(x, approximate=True)

def _silu(x):
    return jax.nn.silu(x)

def _sigmoid(x):
    return jax.nn.sigmoid(x)

def _layernorm(x, axis=-1, eps=1e-05):
    m = jnp.mean(x, axis=axis, keepdims=True)
    v = jnp.var(x, axis=axis, keepdims=True)
    return (x - m) / jnp.sqrt(v + eps)

def _scatter_add(tgt, idx, src, axis=0):
    return tgt.at[idx].add(src)

def _segment_sum(src, seg, n):
    return jax.ops.segment_sum(src, seg, n)
kernel_name = 'mk_xattn_ffn_d4_seqx_r8_13dc83'

def setup_inputs(seed: int=0):
    np.random.seed(seed)
    _w = jnp.asarray

    def _rec_inputs():
        import jax
        import jax.numpy as jnp
        _rk = jax.random.key(seed)
        x = 7.22e-05 + 1 * jax.random.normal(jax.random.fold_in(_rk, 1), (16, 64, 128), jnp.float32)
        _lenS = 64 - jax.random.randint(jax.random.fold_in(_rk, 7), (16,), 0, max(1, 64 // 4) + 1, jnp.int32)
        _lenS2 = 64 - jax.random.randint(jax.random.fold_in(_rk, 8), (16,), 0, max(1, 64 // 4) + 1, jnp.int32)
        _ctx_1024P = jax.random.normal(jax.random.fold_in(_rk, 11), (16, 16, 128), jnp.float32)
        _ctx_1024c = jax.random.dirichlet(jax.random.fold_in(_rk, 511), 0.3 * jnp.ones((16,), jnp.float32), (16, 64))
        _ctx_1024t = jnp.einsum('bsk,bkd->bsd', _ctx_1024c, _ctx_1024P)
        _ctx_1024t = _ctx_1024t * jax.lax.rsqrt(jnp.mean(jnp.square(_ctx_1024t)) + 1e-12) * 0.953939
        ctx_1024 = 4.13588e-05 + 0.999923 * (_ctx_1024t + 0.3 * jax.random.normal(jax.random.fold_in(_rk, 611), (16, 64, 128), jnp.float32))
        _validS = jnp.arange(64)[None, :] < _lenS[:, None]
        _validS2 = jnp.arange(64)[None, :] < _lenS2[:, None]
        _causal = jnp.tril(jnp.ones((64, 64), dtype=bool))
        mask_BxSxS2_ik0 = jnp.where(jnp.broadcast_to(_validS2[:, None, :], (16, 64, 64)), 0, 1).astype(jnp.int32)
        return (x, ctx_1024, mask_BxSxS2_ik0)
    x, ctx_1024, mask_BxSxS2_ik0 = _rec_inputs()

    def _L0_xattn_setup():
        import jax, jax.numpy as jnp
        import numpy as np
        NUM_HEADS = 16
        key = jax.random.key(seed)
        kq, kk, kv = jax.random.split(key, 3)
        B, S, E = (4, 256, 128)
        Q = jax.random.normal(kq, (B, S, E), dtype=jnp.float32)
        K = jax.random.normal(kk, (B, S, E), dtype=jnp.float32)
        V = jax.random.normal(kv, (B, S, E), dtype=jnp.float32)
        return {'Q': Q, 'K': K, 'V': V}
    _L0_xattn_all = _L0_xattn_setup()
    _L0_xattn_in = {k: v for k, v in _L0_xattn_all.items() if k in ()}
    del _L0_xattn_all

    def _L0_ffn_setup():
        import jax, jax.numpy as jnp
        import numpy as np
        MICRO_BATCHES = 2
        TOP_K = 2
        NUM_EXPERTS = 8
        B, S, D = (4, 512, 128)
        H = 4 * D
        key = jax.random.key(seed)
        ks = jax.random.split(key, 8)
        s = 0.02
        return {'x': jax.random.normal(ks[0], (B, S, D), jnp.float32), 'ln_scale': jnp.ones((D,), jnp.float32), 'ln_bias': jnp.zeros((D,), jnp.float32), 'attn_w': jax.random.normal(ks[1], (D, D), jnp.float32) * s, 'attn_b': jnp.zeros((D,), jnp.float32), 'gate_w': jax.random.normal(ks[2], (NUM_EXPERTS, D), jnp.float32) * s, 'w1': jax.random.normal(ks[3], (NUM_EXPERTS, D, H), jnp.float32) * s, 'b1': jnp.zeros((NUM_EXPERTS, H), jnp.float32), 'w2': jax.random.normal(ks[4], (NUM_EXPERTS, H, D), jnp.float32) * s, 'b2': jnp.zeros((NUM_EXPERTS, D), jnp.float32), 'next_w': jax.random.normal(ks[5], (D, D), jnp.float32) * s, 'next_b': jnp.zeros((D,), jnp.float32)}
    _L0_ffn_all = _L0_ffn_setup()
    _L0_ffn_in = {k: v for k, v in _L0_ffn_all.items() if k in ('ln_scale', 'ln_bias', 'attn_w', 'attn_b', 'gate_w', 'w1', 'b1', 'w2', 'b2', 'next_w', 'next_b')}
    del _L0_ffn_all

    def _L1_xattn_setup():
        import jax, jax.numpy as jnp
        import numpy as np
        D_MODEL = 128
        NUM_HEADS = 16
        HEAD_DIM = D_MODEL // NUM_HEADS
        SEQ = 512
        BATCH = 1
        ROPE_BASE = 10000.0

        def _rope_cos_sin(seq_len, head_dim, dtype):
            inv_freq = 1.0 / ROPE_BASE ** (jnp.arange(0, head_dim, 2, dtype=jnp.float32) / head_dim)
            pos = jnp.arange(seq_len, dtype=jnp.float32)
            freqs = pos[:, None] * inv_freq[None, :]
            emb = jnp.concatenate([freqs, freqs], axis=-1)
            return (jnp.cos(emb).astype(dtype), jnp.sin(emb).astype(dtype))

        def _rotate_half(x):
            d = x.shape[-1] // 2
            return jnp.concatenate([-x[..., d:], x[..., :d]], axis=-1)
        key = jax.random.key(seed)
        ks = jax.random.split(key, 11)
        s = 1.0 / np.sqrt(D_MODEL)
        return {'query': jax.random.normal(ks[0], (BATCH, SEQ, D_MODEL), jnp.float32), 'key': jax.random.normal(ks[1], (BATCH, SEQ, D_MODEL), jnp.float32), 'value': jax.random.normal(ks[2], (BATCH, SEQ, D_MODEL), jnp.float32), 'Wq': jax.random.normal(ks[3], (D_MODEL, D_MODEL), jnp.float32) * s, 'bq': jnp.zeros((D_MODEL,), jnp.float32), 'Wk': jax.random.normal(ks[4], (D_MODEL, D_MODEL), jnp.float32) * s, 'bk': jnp.zeros((D_MODEL,), jnp.float32), 'Wv': jax.random.normal(ks[5], (D_MODEL, D_MODEL), jnp.float32) * s, 'bv': jnp.zeros((D_MODEL,), jnp.float32), 'Wo': jax.random.normal(ks[6], (D_MODEL, D_MODEL), jnp.float32) * s, 'bo': jnp.zeros((D_MODEL,), jnp.float32)}
    _L1_xattn_all = _L1_xattn_setup()
    _L1_xattn_in = {k: v for k, v in _L1_xattn_all.items() if k in ('Wq', 'bq', 'Wk', 'bk', 'Wv', 'bv', 'Wo', 'bo')}
    del _L1_xattn_all

    def _L1_ffn_setup():
        import jax, jax.numpy as jnp
        import numpy as np
        B, S, H = (2, 128, 128)
        E, F = (16, 64)
        G, TOPK_G, TOPK = (4, 2, 4)
        N_SHARED = 2
        ROUTE_SCALE = 1.0
        FS = N_SHARED * F

        def _gate(x, w_gate):
            T = x.shape[0]
            scores = jax.nn.sigmoid(x @ w_gate.T)
            sv = scores.reshape(T, G, E // G)
            group_scores = jax.lax.top_k(sv, 2)[0].sum(-1)
            top_groups = jax.lax.top_k(group_scores, TOPK_G)[1]
            allowed = jnp.zeros((T, G), dtype=bool).at[jnp.arange(T)[:, None], top_groups].set(True)
            masked = jnp.where(allowed[:, :, None], sv, -jnp.inf).reshape(T, E)
            _, idx = jax.lax.top_k(masked, TOPK)
            w = jnp.take_along_axis(scores, idx, axis=1)
            w = w / (w.sum(-1, keepdims=True) + 1e-06) * ROUTE_SCALE
            return (w, idx)

        def _swiglu(x, w1, w3, w2):
            return jax.nn.silu(x @ w1.T) * (x @ w3.T) @ w2.T
        key = jax.random.key(seed)
        ks = jax.random.split(key, 8)
        scale = 0.02
        return {'hidden_states': jax.random.normal(ks[0], (B, S, H), dtype=jnp.float32), 'w_gate': jax.random.normal(ks[1], (E, H), dtype=jnp.float32) * scale, 'w1_e': jax.random.normal(ks[2], (E, F, H), dtype=jnp.float32) * scale, 'w3_e': jax.random.normal(ks[3], (E, F, H), dtype=jnp.float32) * scale, 'w2_e': jax.random.normal(ks[4], (E, H, F), dtype=jnp.float32) * scale, 'w1_s': jax.random.normal(ks[5], (FS, H), dtype=jnp.float32) * scale, 'w3_s': jax.random.normal(ks[6], (FS, H), dtype=jnp.float32) * scale, 'w2_s': jax.random.normal(ks[7], (H, FS), dtype=jnp.float32) * scale}
    _L1_ffn_all = _L1_ffn_setup()
    _L1_ffn_in = {k: v for k, v in _L1_ffn_all.items() if k in ('w_gate', 'w1_e', 'w3_e', 'w2_e', 'w1_s', 'w3_s', 'w2_s')}
    del _L1_ffn_all

    def _L2_xattn_setup():
        import jax, jax.numpy as jnp
        import numpy as np
        key = jax.random.key(seed)
        kq, kk, kv = jax.random.split(key, 3)
        bs, s, d = (16, 256, 128)
        return {'query': jax.random.normal(kq, (bs, s, d), dtype=jnp.float32), 'key': jax.random.normal(kk, (bs, s, d), dtype=jnp.float32), 'value': jax.random.normal(kv, (bs, s, d), dtype=jnp.float32)}
    _L2_xattn_all = _L2_xattn_setup()
    _L2_xattn_in = {k: v for k, v in _L2_xattn_all.items() if k in ()}
    del _L2_xattn_all

    def _L2_ffn_setup():
        import jax, jax.numpy as jnp
        import numpy as np
        D, H, P, E, K, F = (128, 16, 64, 8, 2, 512)
        B, S = (2, 256)
        NROT = 32
        BASE = 10000.0
        EPS = 1e-05

        def _ln(x, g, b):
            m = jnp.mean(x, -1, keepdims=True)
            v = jnp.mean(jnp.square(x - m), -1, keepdims=True)
            return (x - m) * jax.lax.rsqrt(v + EPS) * g + b

        def _rope(x):
            xr, xp = (x[..., :NROT], x[..., NROT:])
            half = NROT // 2
            inv = BASE ** (-jnp.arange(half, dtype=jnp.float32) / half)
            ang = jnp.arange(x.shape[2], dtype=jnp.float32)[:, None] * inv[None, :]
            cos, sin = (jnp.cos(ang), jnp.sin(ang))
            x1, x2 = (xr[..., :half], xr[..., half:])
            xr = jnp.concatenate([x1 * cos - x2 * sin, x1 * sin + x2 * cos], -1)
            return jnp.concatenate([xr, xp], -1)

        def _gate(x, Wsel):
            s = jax.nn.sigmoid(jnp.einsum('bsd,hed->bhse', x, Wsel))
            _, idx = jax.lax.top_k(s, K)
            mask = jax.nn.one_hot(idx, E, dtype=s.dtype).sum(-2)
            return s * mask

        def _moe_attn(x, Wq, Wk, Wv, Wo, Wsel_v, Wsel_o):
            q = _rope(jnp.einsum('bsd,hdp->bhsp', x, Wq))
            k = _rope(jnp.einsum('bsd,hdp->bhsp', x, Wk))
            gv = _gate(x, Wsel_v)
            v = jnp.einsum('bsd,bhse,hedp->bhsp', x, gv, Wv)
            att = jax.nn.softmax(jnp.einsum('bhsp,bhtp->bhst', q, k) / np.sqrt(P), axis=-1)
            o = jnp.einsum('bhst,bhtp->bhsp', att, v)
            go = _gate(x, Wsel_o)
            return jnp.einsum('bhsp,bhse,hepd->bsd', o, go, Wo)
        key = jax.random.key(seed)
        ks = jax.random.split(key, 10)
        f = lambda k, sh: jax.random.normal(k, sh, jnp.float32) * 0.02
        return dict(src=jax.random.normal(ks[0], (B, S, D), jnp.float32), Wq=f(ks[1], (H, D, P)), Wk=f(ks[2], (H, D, P)), Wv=f(ks[3], (H, E, D, P)), Wo=f(ks[4], (H, E, P, D)), Wsel_v=f(ks[5], (H, E, D)), Wsel_o=f(ks[6], (H, E, D)), ln1_g=jnp.ones(D, jnp.float32), ln1_b=jnp.zeros(D, jnp.float32), ln2_g=jnp.ones(D, jnp.float32), ln2_b=jnp.zeros(D, jnp.float32), W1=f(ks[7], (D, F)), b1=jnp.zeros(F, jnp.float32), W2=f(ks[8], (F, D)), b2=jnp.zeros(D, jnp.float32))
    _L2_ffn_all = _L2_ffn_setup()
    _L2_ffn_in = {k: v for k, v in _L2_ffn_all.items() if k in ('Wq', 'Wk', 'Wv', 'Wo', 'Wsel_v', 'Wsel_o', 'ln1_g', 'ln1_b', 'ln2_g', 'ln2_b', 'W1', 'b1', 'W2', 'b2')}
    del _L2_ffn_all

    def _L3_xattn_setup():
        import jax, jax.numpy as jnp
        import numpy as np
        B, NKV, NQ, D, H = (4, 256, 128, 128, 16)
        HD = D // H
        key = jax.random.key(seed)
        ks = jax.random.split(key, 9)
        s = 0.02
        return {'x': jax.random.normal(ks[0], (B, NKV, D), jnp.float32), 'y': jax.random.normal(ks[1], (B, NQ, D), jnp.float32), 'mask': jax.random.randint(ks[2], (B, NQ, NKV), 0, 2, jnp.int32), 'W_kv': jax.random.normal(ks[3], (D, 2 * D), jnp.float32) * s, 'b_kv': jnp.zeros((2 * D,), jnp.float32), 'W_q': jax.random.normal(ks[4], (D, D), jnp.float32) * s, 'b_q': jnp.zeros((D,), jnp.float32), 'W_o': jax.random.normal(ks[5], (D, D), jnp.float32) * s, 'b_o': jnp.zeros((D,), jnp.float32)}
    _L3_xattn_all = _L3_xattn_setup()
    _L3_xattn_in = {k: v for k, v in _L3_xattn_all.items() if k in ('W_kv', 'b_kv', 'W_q', 'b_q', 'W_o', 'b_o')}
    del _L3_xattn_all

    def _L3_ffn_setup():
        import jax, jax.numpy as jnp
        import numpy as np
        K = 32
        key = jax.random.key(seed)
        ks = jax.random.split(key, 9)
        B, S, D, O, E = (8, 256, 128, 128, 16)

        def xavier(k_, shape):
            fan_in, fan_out = (shape[-2], shape[-1])
            lim = (6.0 / (fan_in + fan_out)) ** 0.5
            return jax.random.uniform(k_, shape, jnp.float32, -lim, lim)
        return {'x': jax.random.normal(ks[0], (B, S, D), jnp.float32), 'Wg': xavier(ks[1], (D, E)), 'bg': jnp.zeros((E,), jnp.float32), 'w1': xavier(ks[2], (E, D, O)), 'b1': xavier(ks[3], (E, 1)), 'w2': xavier(ks[4], (E, O, O)), 'b2': xavier(ks[5], (E, 1)), 'w3': xavier(ks[6], (E, O, O)), 'b3': xavier(ks[7], (E, 1))}
    _L3_ffn_all = _L3_ffn_setup()
    _L3_ffn_in = {k: v for k, v in _L3_ffn_all.items() if k in ('Wg', 'bg', 'w1', 'b1', 'w2', 'b2', 'w3', 'b3')}
    del _L3_ffn_all
    return {'x': x, 'ctx_1024': ctx_1024, 'mask_BxSxS2_ik0': mask_BxSxS2_ik0, 'L0_ffn_ln_scale': _L0_ffn_in['ln_scale'], 'L0_ffn_ln_bias': _L0_ffn_in['ln_bias'], 'L0_ffn_attn_w': _L0_ffn_in['attn_w'], 'L0_ffn_attn_b': _L0_ffn_in['attn_b'], 'L0_ffn_gate_w': _L0_ffn_in['gate_w'], 'L0_ffn_w1': _L0_ffn_in['w1'], 'L0_ffn_b1': _L0_ffn_in['b1'], 'L0_ffn_w2': _L0_ffn_in['w2'], 'L0_ffn_b2': _L0_ffn_in['b2'], 'L0_ffn_next_w': _L0_ffn_in['next_w'], 'L0_ffn_next_b': _L0_ffn_in['next_b'], 'L1_xattn_Wq': _L1_xattn_in['Wq'], 'L1_xattn_bq': _L1_xattn_in['bq'], 'L1_xattn_Wk': _L1_xattn_in['Wk'], 'L1_xattn_bk': _L1_xattn_in['bk'], 'L1_xattn_Wv': _L1_xattn_in['Wv'], 'L1_xattn_bv': _L1_xattn_in['bv'], 'L1_xattn_Wo': _L1_xattn_in['Wo'], 'L1_xattn_bo': _L1_xattn_in['bo'], 'L1_ffn_w_gate': _L1_ffn_in['w_gate'], 'L1_ffn_w1_e': _L1_ffn_in['w1_e'], 'L1_ffn_w3_e': _L1_ffn_in['w3_e'], 'L1_ffn_w2_e': _L1_ffn_in['w2_e'], 'L1_ffn_w1_s': _L1_ffn_in['w1_s'], 'L1_ffn_w3_s': _L1_ffn_in['w3_s'], 'L1_ffn_w2_s': _L1_ffn_in['w2_s'], 'L2_ffn_Wq': _L2_ffn_in['Wq'], 'L2_ffn_Wk': _L2_ffn_in['Wk'], 'L2_ffn_Wv': _L2_ffn_in['Wv'], 'L2_ffn_Wo': _L2_ffn_in['Wo'], 'L2_ffn_Wsel_v': _L2_ffn_in['Wsel_v'], 'L2_ffn_Wsel_o': _L2_ffn_in['Wsel_o'], 'L2_ffn_ln1_g': _L2_ffn_in['ln1_g'], 'L2_ffn_ln1_b': _L2_ffn_in['ln1_b'], 'L2_ffn_ln2_g': _L2_ffn_in['ln2_g'], 'L2_ffn_ln2_b': _L2_ffn_in['ln2_b'], 'L2_ffn_W1': _L2_ffn_in['W1'], 'L2_ffn_b1': _L2_ffn_in['b1'], 'L2_ffn_W2': _L2_ffn_in['W2'], 'L2_ffn_b2': _L2_ffn_in['b2'], 'L3_xattn_W_kv': _L3_xattn_in['W_kv'], 'L3_xattn_b_kv': _L3_xattn_in['b_kv'], 'L3_xattn_W_q': _L3_xattn_in['W_q'], 'L3_xattn_b_q': _L3_xattn_in['b_q'], 'L3_xattn_W_o': _L3_xattn_in['W_o'], 'L3_xattn_b_o': _L3_xattn_in['b_o'], 'L3_ffn_Wg': _L3_ffn_in['Wg'], 'L3_ffn_bg': _L3_ffn_in['bg'], 'L3_ffn_w1': _L3_ffn_in['w1'], 'L3_ffn_b1': _L3_ffn_in['b1'], 'L3_ffn_w2': _L3_ffn_in['w2'], 'L3_ffn_b2': _L3_ffn_in['b2'], 'L3_ffn_w3': _L3_ffn_in['w3'], 'L3_ffn_b3': _L3_ffn_in['b3']}

def reference(x, ctx_1024, mask_BxSxS2_ik0, L0_ffn_ln_scale, L0_ffn_ln_bias, L0_ffn_attn_w, L0_ffn_attn_b, L0_ffn_gate_w, L0_ffn_w1, L0_ffn_b1, L0_ffn_w2, L0_ffn_b2, L0_ffn_next_w, L0_ffn_next_b, L1_xattn_Wq, L1_xattn_bq, L1_xattn_Wk, L1_xattn_bk, L1_xattn_Wv, L1_xattn_bv, L1_xattn_Wo, L1_xattn_bo, L1_ffn_w_gate, L1_ffn_w1_e, L1_ffn_w3_e, L1_ffn_w2_e, L1_ffn_w1_s, L1_ffn_w3_s, L1_ffn_w2_s, L2_ffn_Wq, L2_ffn_Wk, L2_ffn_Wv, L2_ffn_Wo, L2_ffn_Wsel_v, L2_ffn_Wsel_o, L2_ffn_ln1_g, L2_ffn_ln1_b, L2_ffn_ln2_g, L2_ffn_ln2_b, L2_ffn_W1, L2_ffn_b1, L2_ffn_W2, L2_ffn_b2, L3_xattn_W_kv, L3_xattn_b_kv, L3_xattn_W_q, L3_xattn_b_q, L3_xattn_W_o, L3_xattn_b_o, L3_ffn_Wg, L3_ffn_bg, L3_ffn_w1, L3_ffn_b1, L3_ffn_w2, L3_ffn_b2, L3_ffn_w3, L3_ffn_b3):
    import jax
    import jax.numpy as jnp

    def _L0_xattn_ref(Q, K, V):
        import jax, jax.numpy as jnp
        import numpy as np
        NUM_HEADS = 16
        B, S, E = Q.shape
        H = NUM_HEADS
        d_k = E // H
        q = Q.reshape(B, S, H, d_k).transpose(0, 2, 1, 3)
        k = K.reshape(B, S, H, d_k).transpose(0, 2, 1, 3)
        v = V.reshape(B, S, H, d_k).transpose(0, 2, 1, 3)
        scale = 1.0 / np.sqrt(d_k).astype(np.float32)
        scores = jnp.einsum('bhqd,bhkd->bhqk', q, k) * scale
        causal_mask = jnp.tril(jnp.ones((S, S), dtype=bool))
        scores = jnp.where(causal_mask, scores, jnp.finfo(scores.dtype).min)
        attn = jax.nn.softmax(scores, axis=-1)
        out = jnp.einsum('bhqk,bhkd->bhqd', attn, v)
        return out.transpose(0, 2, 1, 3).reshape(B, S, E)

    def _L0_ffn_ref(x, ln_scale, ln_bias, attn_w, attn_b, gate_w, w1, b1, w2, b2, next_w, next_b):
        import jax, jax.numpy as jnp
        import numpy as np
        MICRO_BATCHES = 2
        TOP_K = 2
        NUM_EXPERTS = 8
        B, S, D = (4, 512, 128)
        H = 4 * D
        b, s, d = x.shape
        flat = x.reshape(b * s, d)
        mu = jnp.mean(flat, axis=-1, keepdims=True)
        var = jnp.mean((flat - mu) ** 2, axis=-1, keepdims=True)
        xn = (flat - mu) * jax.lax.rsqrt(var + 1e-05) * ln_scale + ln_bias
        x_attn = xn @ attn_w.T + attn_b + flat
        logits = x_attn @ gate_w.T
        _vals, _idx = jax.lax.top_k(logits, TOP_K)
        e = w1.shape[0]
        n = b * s // (MICRO_BATCHES * e)
        xe = x_attn.reshape(MICRO_BATCHES, e, n, d)
        h = jax.nn.gelu(jnp.einsum('mend,edh->menh', xe, w1) + b1[None, :, None, :], approximate=False)
        eo = jnp.einsum('menh,ehd->mend', h, w2) + b2[None, :, None, :]
        eo = eo.reshape(b * s, d)
        out = jax.nn.gelu(eo @ next_w.T + next_b, approximate=False)
        return out.reshape(b, s, d)

    def _L1_xattn_ref(query, key, value, Wq, bq, Wk, bk, Wv, bv, Wo, bo):
        import jax, jax.numpy as jnp
        import numpy as np
        D_MODEL = 128
        NUM_HEADS = 16
        HEAD_DIM = D_MODEL // NUM_HEADS
        SEQ = 512
        BATCH = 1
        ROPE_BASE = 10000.0

        def _rope_cos_sin(seq_len, head_dim, dtype):
            inv_freq = 1.0 / ROPE_BASE ** (jnp.arange(0, head_dim, 2, dtype=jnp.float32) / head_dim)
            pos = jnp.arange(seq_len, dtype=jnp.float32)
            freqs = pos[:, None] * inv_freq[None, :]
            emb = jnp.concatenate([freqs, freqs], axis=-1)
            return (jnp.cos(emb).astype(dtype), jnp.sin(emb).astype(dtype))

        def _rotate_half(x):
            d = x.shape[-1] // 2
            return jnp.concatenate([-x[..., d:], x[..., :d]], axis=-1)
        B, Sq, _ = query.shape
        Skv = key.shape[1]
        H, Dh = (NUM_HEADS, HEAD_DIM)
        q = (query @ Wq.T + bq).reshape(B, Sq, H, Dh)
        k = (key @ Wk.T + bk).reshape(B, Skv, H, Dh)
        v = (value @ Wv.T + bv).reshape(B, Skv, H, Dh)
        cos, sin = _rope_cos_sin(max(Sq, Skv), Dh, query.dtype)
        cq, sq_ = (cos[None, :Sq, None, :], sin[None, :Sq, None, :])
        ck, sk_ = (cos[None, :Skv, None, :], sin[None, :Skv, None, :])
        q = q * cq + _rotate_half(q) * sq_
        k = k * ck + _rotate_half(k) * sk_
        scale = 1.0 / np.sqrt(Dh)
        scores = jnp.einsum('bqhd,bkhd->bhqk', q, k) * scale
        probs = jax.nn.softmax(scores, axis=-1)
        ctx = jnp.einsum('bhqk,bkhd->bqhd', probs, v).reshape(B, Sq, H * Dh)
        return ctx @ Wo.T + bo

    def _L1_ffn_ref(hidden_states, w_gate, w1_e, w3_e, w2_e, w1_s, w3_s, w2_s):
        import jax, jax.numpy as jnp
        import numpy as np
        B, S, H = (2, 128, 128)
        E, F = (16, 64)
        G, TOPK_G, TOPK = (4, 2, 4)
        N_SHARED = 2
        ROUTE_SCALE = 1.0
        FS = N_SHARED * F

        def _gate(x, w_gate):
            T = x.shape[0]
            scores = jax.nn.sigmoid(x @ w_gate.T)
            sv = scores.reshape(T, G, E // G)
            group_scores = jax.lax.top_k(sv, 2)[0].sum(-1)
            top_groups = jax.lax.top_k(group_scores, TOPK_G)[1]
            allowed = jnp.zeros((T, G), dtype=bool).at[jnp.arange(T)[:, None], top_groups].set(True)
            masked = jnp.where(allowed[:, :, None], sv, -jnp.inf).reshape(T, E)
            _, idx = jax.lax.top_k(masked, TOPK)
            w = jnp.take_along_axis(scores, idx, axis=1)
            w = w / (w.sum(-1, keepdims=True) + 1e-06) * ROUTE_SCALE
            return (w, idx)

        def _swiglu(x, w1, w3, w2):
            return jax.nn.silu(x @ w1.T) * (x @ w3.T) @ w2.T
        shape = hidden_states.shape
        x = hidden_states.reshape(-1, H)
        weights, idx = _gate(x, w_gate)
        combine = (jax.nn.one_hot(idx, E, dtype=x.dtype) * weights[..., None]).sum(1)
        g = jax.nn.silu(jnp.einsum('th,efh->tef', x, w1_e))
        u = jnp.einsum('th,efh->tef', x, w3_e)
        routed = jnp.einsum('tef,ehf,te->th', g * u, w2_e, combine)
        shared = _swiglu(x, w1_s, w3_s, w2_s)
        return (routed + shared).reshape(shape)

    def _L2_xattn_ref(query, key, value):
        import jax, jax.numpy as jnp
        import numpy as np
        scale = jnp.asarray(query.shape[-1], query.dtype) ** 0.5
        scores = jnp.einsum('bqd,bkd->bqk', query, key) / scale
        attn = jax.nn.softmax(scores, axis=-1)
        return jnp.einsum('bqk,bkd->bqd', attn, value)

    def _L2_ffn_ref(src, Wq, Wk, Wv, Wo, Wsel_v, Wsel_o, ln1_g, ln1_b, ln2_g, ln2_b, W1, b1, W2, b2):
        import jax, jax.numpy as jnp
        import numpy as np
        D, H, P, E, K, F = (128, 16, 64, 8, 2, 512)
        B, S = (2, 256)
        NROT = 32
        BASE = 10000.0
        EPS = 1e-05

        def _ln(x, g, b):
            m = jnp.mean(x, -1, keepdims=True)
            v = jnp.mean(jnp.square(x - m), -1, keepdims=True)
            return (x - m) * jax.lax.rsqrt(v + EPS) * g + b

        def _rope(x):
            xr, xp = (x[..., :NROT], x[..., NROT:])
            half = NROT // 2
            inv = BASE ** (-jnp.arange(half, dtype=jnp.float32) / half)
            ang = jnp.arange(x.shape[2], dtype=jnp.float32)[:, None] * inv[None, :]
            cos, sin = (jnp.cos(ang), jnp.sin(ang))
            x1, x2 = (xr[..., :half], xr[..., half:])
            xr = jnp.concatenate([x1 * cos - x2 * sin, x1 * sin + x2 * cos], -1)
            return jnp.concatenate([xr, xp], -1)

        def _gate(x, Wsel):
            s = jax.nn.sigmoid(jnp.einsum('bsd,hed->bhse', x, Wsel))
            _, idx = jax.lax.top_k(s, K)
            mask = jax.nn.one_hot(idx, E, dtype=s.dtype).sum(-2)
            return s * mask

        def _moe_attn(x, Wq, Wk, Wv, Wo, Wsel_v, Wsel_o):
            q = _rope(jnp.einsum('bsd,hdp->bhsp', x, Wq))
            k = _rope(jnp.einsum('bsd,hdp->bhsp', x, Wk))
            gv = _gate(x, Wsel_v)
            v = jnp.einsum('bsd,bhse,hedp->bhsp', x, gv, Wv)
            att = jax.nn.softmax(jnp.einsum('bhsp,bhtp->bhst', q, k) / np.sqrt(P), axis=-1)
            o = jnp.einsum('bhst,bhtp->bhsp', att, v)
            go = _gate(x, Wsel_o)
            return jnp.einsum('bhsp,bhse,hepd->bsd', o, go, Wo)
        src2 = _moe_attn(src, Wq, Wk, Wv, Wo, Wsel_v, Wsel_o)
        src = src + src2
        src = _ln(src, ln1_g, ln1_b)
        src2 = jax.nn.relu(src @ W1 + b1) @ W2 + b2
        src = src + src2
        return _ln(src, ln2_g, ln2_b)

    def _L3_xattn_ref(x, y, mask, W_kv, b_kv, W_q, b_q, W_o, b_o):
        import jax, jax.numpy as jnp
        import numpy as np
        B, NKV, NQ, D, H = (4, 256, 128, 128, 16)
        HD = D // H
        b, nkv, _ = x.shape
        nq = y.shape[1]
        kv = x @ W_kv + b_kv
        q = y @ W_q + b_q
        kv = kv.reshape(b, nkv, H, 2 * HD).transpose(0, 2, 1, 3)
        q = q.reshape(b, nq, H, HD).transpose(0, 2, 1, 3)
        k, v = (kv[..., :HD], kv[..., HD:])
        scores = jnp.einsum('bhqd,bhkd->bhqk', q, k) / jnp.sqrt(jnp.float32(HD))
        scores = jnp.where(mask[:, None, :, :] == 0, jnp.float32(-1e+20), scores)
        attn = jax.nn.softmax(scores, axis=-1)
        vals = jnp.einsum('bhqk,bhkd->bhqd', attn, v)
        vals = vals.transpose(0, 2, 1, 3).reshape(b, nq, D)
        return vals @ W_o + b_o

    def _L3_ffn_ref(x, Wg, bg, w1, b1, w2, b2, w3, b3):
        import jax, jax.numpy as jnp
        import numpy as np
        K = 32
        B, S, D = x.shape
        E, _, O = w1.shape
        logits = jnp.einsum('bsd,de->bse', x, Wg) + bg
        probs = jax.nn.softmax(logits, axis=-2)
        pv = jnp.transpose(probs, (0, 2, 1))
        vals, idx = jax.lax.top_k(pv, K)
        bidx = jnp.arange(B)[:, None, None]
        tok = x[bidx, idx]
        b1b = b1[None, :, None, :]
        b2b = b2[None, :, None, :]
        b3b = b3[None, :, None, :]
        h = jax.nn.relu(jnp.einsum('bekd,edo->beko', tok, w1) + b1b)
        h = jax.nn.relu(jnp.einsum('bekd,edo->beko', h, w2) + b2b)
        h = jnp.einsum('bekd,edo->beko', h, w3) + b3b
        out = h * vals[..., None]
        outputs = jnp.zeros((B, S, O), x.dtype).at[bidx, idx].add(out)
        return outputs
    x = x + _L0_xattn_ref(_layernorm(x, axis=-1), ctx_1024, ctx_1024)
    x = x + _L0_ffn_ref(_layernorm(x, axis=-1), L0_ffn_ln_scale, L0_ffn_ln_bias, L0_ffn_attn_w, L0_ffn_attn_b, L0_ffn_gate_w, L0_ffn_w1, L0_ffn_b1, L0_ffn_w2, L0_ffn_b2, L0_ffn_next_w, L0_ffn_next_b)
    x = x + _L1_xattn_ref(_layernorm(x, axis=-1), ctx_1024, ctx_1024, L1_xattn_Wq, L1_xattn_bq, L1_xattn_Wk, L1_xattn_bk, L1_xattn_Wv, L1_xattn_bv, L1_xattn_Wo, L1_xattn_bo)
    x = x + _L1_ffn_ref(_layernorm(x, axis=-1), L1_ffn_w_gate, L1_ffn_w1_e, L1_ffn_w3_e, L1_ffn_w2_e, L1_ffn_w1_s, L1_ffn_w3_s, L1_ffn_w2_s)
    x = x + _L2_xattn_ref(_layernorm(x, axis=-1), ctx_1024, ctx_1024)
    x = x + _L2_ffn_ref(_layernorm(x, axis=-1), L2_ffn_Wq, L2_ffn_Wk, L2_ffn_Wv, L2_ffn_Wo, L2_ffn_Wsel_v, L2_ffn_Wsel_o, L2_ffn_ln1_g, L2_ffn_ln1_b, L2_ffn_ln2_g, L2_ffn_ln2_b, L2_ffn_W1, L2_ffn_b1, L2_ffn_W2, L2_ffn_b2)
    x = x + _L3_xattn_ref(ctx_1024, _layernorm(x, axis=-1), mask_BxSxS2_ik0, L3_xattn_W_kv, L3_xattn_b_kv, L3_xattn_W_q, L3_xattn_b_q, L3_xattn_W_o, L3_xattn_b_o)
    x = x + _L3_ffn_ref(_layernorm(x, axis=-1), L3_ffn_Wg, L3_ffn_bg, L3_ffn_w1, L3_ffn_b1, L3_ffn_w2, L3_ffn_b2, L3_ffn_w3, L3_ffn_b3)
    return x

_drawn_inputs = setup_inputs


def setup_inputs(seed=0):
    import zlib

    import numpy as np

    out = dict(_drawn_inputs(seed))
    spreads = {'L0_ffn_ln_scale': (1.0, 0.6),
     'L0_ffn_ln_bias': (0.0, 0.8),
     'L0_ffn_attn_b': (0.0, 0.8),
     'L0_ffn_b1': (0.0, 0.8),
     'L0_ffn_b2': (0.0, 0.8),
     'L0_ffn_next_b': (0.0, 0.8),
     'L1_xattn_bq': (0.0, 2.0),
     'L1_xattn_bk': (0.0, 2.0),
     'L1_xattn_bv': (0.0, 0.721),
     'L1_xattn_bo': (0.0, 0.796),
     'L2_ffn_ln1_g': (1.0, 0.6),
     'L2_ffn_ln1_b': (0.0, 0.8),
     'L2_ffn_ln2_g': (1.0, 0.6),
     'L2_ffn_ln2_b': (0.0, 0.8),
     'L2_ffn_b1': (0.0, 2.0),
     'L2_ffn_b2': (0.0, 0.8),
     'L3_xattn_b_kv': (0.0, 0.8),
     'L3_xattn_b_q': (0.0, 2.0),
     'L3_xattn_b_o': (0.0, 0.8),
     'L3_ffn_bg': (0.0, 2.0)}
    factors = {'L0_ffn_attn_w': 8.0,
     'L0_ffn_w1': 8.0,
     'L0_ffn_w2': 8.0,
     'L0_ffn_next_w': 7.398,
     'L1_ffn_w_gate': 8.0,
     'L1_ffn_w1_e': 8.0,
     'L1_ffn_w3_e': 8.0,
     'L1_ffn_w2_e': 8.0,
     'L1_ffn_w1_s': 8.0,
     'L1_ffn_w3_s': 8.0,
     'L1_ffn_w2_s': 8.0,
     'L2_ffn_Wq': 8.0,
     'L2_ffn_Wk': 8.0,
     'L2_ffn_Wv': 3.892,
     'L2_ffn_Wo': 3.797,
     'L2_ffn_Wsel_v': 5.471,
     'L2_ffn_Wsel_o': 4.424,
     'L3_xattn_W_kv': 5.389,
     'L3_xattn_W_q': 8.0,
     'L3_xattn_W_o': 4.112,
     'L3_ffn_w1': 3.865,
     'L3_ffn_b1': 7.689,
     'L3_ffn_w2': 3.132,
     'L3_ffn_b2': 60.792,
     'L3_ffn_b3': 38.581,
     'L1_xattn_Wq': 3.085,
     'L1_xattn_Wk': 2.814,
     'L2_ffn_W1': 8.0,
     'L2_ffn_W2': 4.073}
    for name, (base, spread) in spreads.items():
        noise = np.random.default_rng([zlib.crc32(name.encode()), seed]).standard_normal(out[name].shape)
        drawn = base * np.exp(spread * noise) if base else spread * noise
        out[name] = jnp.asarray(drawn.astype(out[name].dtype))
    for name, factor in factors.items():
        out[name] = (out[name] * factor).astype(out[name].dtype)
    return out
```

```python
from contextlib import ExitStack

import concourse.bass as bass
from concourse import mybir

F32 = mybir.dt.float32
BF16 = mybir.dt.bfloat16
I32 = mybir.dt.int32
ALU = mybir.AluOpType
ACT = mybir.ActivationFunctionType
AX = mybir.AxisListType

P = 128
T = 8
S = 64
TOK = 1024
H = 16
HP = H // 2
E0 = 8
EPS = 1e-5
MASKED = -1.0e30
HIDDEN = -1.0e20 * 8.0 ** 0.5

COLS = dict(ln_scale=1, ln_bias=1, attn_b=1, b1_0=32, b2_0=8, bq1=1, bq1p=1, bk1=1, bk1p=1,
            bk3=1, bq3=1, ln1_g=1, ln1_b=1, b1_2=4, bg=1)
ROWS = dict(next_b=128, bv1=128, bo1=128, ln1_gr=128, ln1_br=128, b2_2=128, ln2_g=128, ln2_b=128,
            bv3=128, bo3=128, b1_3=16, b2_3=16, b3_3=16)
CONSTS = dict(ident=128, cos1=64, sin1=64, cos2=64, sin2=64, lt4=16, lt16=256, prefer=8, headof=16)
WB = dict(wq1=128, wq1p=128, wk1=128, wk1p=128, wv1=128, wo1=128, wk3=128, wv3=128, wq3=128, wo3=128,
          w_gate=16, wsel=256, W1=512, W2=512, wg_pad=240)
SEL_PAIR, SEL_DUO, SEL_ONE, NSEL = 0, 16, 24, 40


def offsets(sizes):
    at, out = 0, {}
    for name, n in sizes.items():
        out[name] = (at, n)
        at += n
    return out, at


COL_AT, NCOL = offsets(COLS)
ROW_AT, NROW = offsets(ROWS)
CONST_AT, NCONST = offsets(CONSTS)
WB_AT, NWB = offsets(WB)

L0W = 2 * 4096 + 2 * 128
L1W = 3 * 9 * 128
L2W = 512 + 1024 + 1024
L3W = 3 * 16 * 128
L1_AT = 2 * L2W
STAGE = max(L0W, L1_AT + L1W, L3W)

ATT = {0: 0, 1: 1, 3: 2}
LN_ROWS = [0, 1, 0, 1, 0, 1, 0, 1, 1, 0, 1]
COLUMNS_OF = [0, 2, 3, 4, 5, 6, 7, 9, 10]

ACC_COUNT = {}
_n = 0
for _name, _k in (("att0", T), ("eo", T), ("att1", T), ("l1", 9), ("l2", 64), ("ff", 2), ("att3", T), ("l3", 16)):
    ACC_COUNT[_name] = _n
    _n += _k


def psum_plan():
    jobs = []

    def job(name, banks=2, reads=2):
        jobs.append((name, banks, reads))

    def attention(i):
        for t in range(T + 1):
            if t < T:
                job(f"s{i}.{t}", 2, 1)
            if t >= 1:
                job(f"p{i}.{t - 1}")

    job("x.0")
    attention(0)
    job("k1a")
    job("k1b")
    job("v1.0", 2, 4)
    job("v1.1", 2, 4)
    job("x.1")
    job("xa")
    for t in range(T):
        job(f"h.{t}", 1, 1)
    job("nx")
    job("x.2")
    job("qa")
    job("qb")
    attention(1)
    job("ot1")
    job("out1")
    job("x.3")
    job("rt", 1, 1)
    for c in range(9):
        job(f"G.{c}")
        job(f"U.{c}", 2, 1)
        if c == 0:
            job("gt1", 1, 1)
        if c < 8:
            job(f"E1.{c}", 2, 1)
    job("x.4")
    job("s2", 2, 1)
    job("p2")
    job("o2")
    job("x.5")
    job("gs.0", 2, 1)
    job("gs.1", 2, 1)
    for m in "qk":
        for n in "ab":
            job(f"{m}{n}.0", 2, 1)
    for hp in range(HP):
        job(f"s.{hp}", 2, 1)
        for t in range(T):
            job(f"y.{hp}.{t}", 2, 1)
        if hp == 0:
            for g in range(4):
                job(f"gt2.{g}", 1, 1)
        job(f"pt.{hp}")
        job(f"o.{hp}")
        for e in range(E0):
            job(f"E2.{hp}.{e}", 2, 1)
            if hp < HP - 1 and e % 2 == 1:
                job(f"{'qk'[e // 4]}{'ab'[e // 2 % 2]}.{hp + 1}", 2, 1)
    job("k3")
    job("v3.0", 2, 4)
    job("v3.1", 2, 4)
    job("x.6")
    for c in range(4):
        job(f"f.{c}", 2, 1)
    job("x.7")
    job("q3")
    attention(3)
    job("ot3")
    job("out3")
    job("x.8")
    job("lg", 1, 1)
    job("h1.0", 2, 1)
    job("vt", 1, 1)
    job("gt3", 1, 1)
    for e in range(16):
        if e > 0:
            job(f"h1.{e}", 2, 1)
        job(f"h2.{e}", 2, 1)
        job(f"E3.{e}", 2, 1)
    return jobs


def build(nc, io):
    with ExitStack() as ctx:
        def sb(name, shape, dt=F32):
            return ctx.enter_context(nc.sbuf_tensor(name, shape, dt))

        def sem(name):
            return ctx.enter_context(nc.semaphore(name))

        X = sb("X", [P, T, P])
        XN = [sb(f"XN{i}", [P, T, P]) for i in range(2)]
        XT = [sb(f"XT{i}", [P, TOK]) for i in range(2)]
        ctxT = sb("ctxT_sb", [P, TOK])
        ctxR = sb("ctxR_sb", [P, T, P])
        KX = [sb(f"KX{i}", [P, 2, H, S]) for i in range(2)]
        VX = [sb(f"VX{i}", [P, 2 * T, HP, 2, 9]) for i in range(2)]
        KT = sb("KT", [P, TOK])
        QT = sb("QT", [P, TOK])
        PB = sb("PB", [P, 3, TOK])
        PT = [sb(f"PT{i}", [P, TOK]) for i in range(2)]
        ON = sb("ON", [P, T, P])
        OC = sb("OC", [P, TOK])
        stage = sb("stage", [P, STAGE])
        wb = sb("wb_sb", [P, NWB])
        cols = sb("cols_sb", [P, NCOL])
        rows = sb("rows_sb", [P, NROW])
        consts = sb("consts_sb", [P, NCONST])
        sel = sb("sel_sb", [96, NSEL, P], BF16)
        bmask = sb("bmask_sb", [P, 64 + 128 + 128], BF16)
        stats = sb("stats", [P, T, 6])
        meanvar = sb("meanvar", [P, T, 2])
        vareps = sb("vareps", [P, T])
        rstd = sb("rstd", [P, T])
        minus_half = sb("minus_half", [P, T])
        mx2 = sb("mx", [P, 2, 16])
        rsum2 = sb("rsum", [P, 2, 16])
        SC = sb("SC", [P, T, 16])
        small = sb("small", [P, 1024])
        G3 = sb("G3", [P, T, 96], BF16)
        GT = sb("GT", [96, TOK], BF16)
        GTh = sb("GTh", [96, 4, TOK], BF16)
        maskB = sb("maskB", [P, T, S], BF16)
        big = sb("big", [P, 6, TOK])
        psum = ctx.enter_context(nc.psum_tensor("psum", [P, 4, 1024], F32))
        ACC = psum[:, 3, :]
        mx, rsum = mx2[:, 0, :], rsum2[:, 0, :]

        def col(name, i=0, n=1):
            at = COL_AT[name][0]
            return cols[:, at + i:at + i + n]

        def row(name):
            at, n = ROW_AT[name]
            return rows[:, at:at + n]

        def const(name):
            at, n = CONST_AT[name]
            return consts[:, at:at + n]

        def weight(name):
            at, n = WB_AT[name]
            return wb[:, at:at + n]

        def half(x, p):
            return x[:, 512 * p:512 * p + 512]

        def over(x, n, at=1):
            shape = list(x.shape)
            shape.insert(at, n)
            return x.unsqueeze(at).broadcast_to(shape)

        ident = const("ident")
        causal = bmask[:, 0:64]
        blocks = bmask[:, 64:192]
        identb = bmask[:, 192:320]
        w1_0 = stage[:, 0:4096].rearrange("p (t n) -> p t n", t=T)
        w2_0 = stage[:, 4096:8192].rearrange("p (t c n) -> p t c n", t=T, c=4)
        attn_w = stage[:, 8192:8320]
        next_w = stage[:, 8320:8448]
        XAT = big[:, 5, :]
        w_l1 = stage[:, L1_AT:L1_AT + L1W].rearrange("p (m c n) -> p m c n", m=3, c=9)
        w_l2 = [stage[:, i * L2W:(i + 1) * L2W] for i in range(2)]
        GVO = big[:, 0:2, :].rearrange("p a (t v g) -> p (a t) v g", t=4, v=2)
        YG = [big[:, 2, :], big[:, 3, :]]
        AT = [big[:, 4, :], big[:, 5, :]]
        ROTQ = XT[0][:, :]
        ROTK = ON[:, :, :].rearrange("p t n -> p (t n)")
        V2 = XN[1][:, :, :].rearrange("p t (j v) -> p t j v", j=2)
        G3h = big[:, 4:6, :].rearrange("p a n -> p (a n)").bitcast(BF16)[:, 0:T * HP * 48]\
            .rearrange("p (t h g) -> p t h g", t=T, h=HP)
        w_l3 = stage[:, 0:L3W].rearrange("p (m e n) -> p m e n", m=3, e=16)
        ctxV = big[:, 0, :].rearrange("p (b h d) -> p b h d", b=2 * T, h=HP)
        maskI = big[:, 1, 0:512].bitcast(I32).rearrange("p (t k) -> p t k", t=T)

        ld_x = sem("ld_x")
        ld_small = sem("ld_small")
        ld_ctxT = sem("ld_ctxT")
        ld_ctxR = sem("ld_ctxR")
        ld_ctxV = sem("ld_ctxV")
        ld_rows = sem("ld_rows")
        ld_wb = sem("ld_wb")
        ld_sel = sem("ld_sel")
        ld_mask = sem("ld_mask")
        ld_l0 = sem("ld_l0")
        ld_l1 = sem("ld_l1")
        ld_l2 = [sem(f"ld_l2_{i}") for i in range(2)]
        ld_l3 = sem("ld_l3")
        stored = sem("stored")
        cleared = sem("cleared")
        slot_full = [sem(f"slot_full{i}") for i in range(3)]
        slot_read = [sem(f"slot_read{i}") for i in range(3)]
        acc_full = sem("acc_full")
        acc_read = sem("acc_read")
        dve_step = sem("dve_step")
        pool_step = sem("pool_step")
        ln_var = sem("ln_var")
        ln_rstd = sem("ln_rstd")
        xn_ready = sem("xn_ready")
        kx_ready = sem("kx_ready")
        vx_ready = sem("vx_ready")
        k_ready = sem("k_ready")
        q_ready = sem("q_ready")
        at_exp = sem("at_exp")
        at_out = sem("at_out")
        x_added = sem("x_added")
        mask_ready = sem("mask_ready")
        nx_gelu = sem("nx_gelu")
        gates_ready = sem("gates_ready")
        roped = sem("roped")
        v_ready = sem("v_ready")
        s_exp = sem("s_exp")
        s_recip = sem("s_recip")
        s_norm = sem("s_norm")
        y1_ready = sem("y1_ready")
        l3_shift = sem("l3_shift")
        l3_exp = sem("l3_exp")
        l3_val = sem("l3_val")
        x_final = sem("x_final")

        slot_of, full_before, read_before = {}, {}, {}
        filled, emptied = [0, 0, 0], [0, 0, 0]
        for n, (name, banks, reads) in enumerate(psum_plan()):
            s = n % 3
            slot_of[name], full_before[name], read_before[name] = s, filled[s], emptied[s]
            filled[s] += banks
            emptied[s] += reads

        def slot(name):
            return psum[:, slot_of[name], :]

        def take(pe, name):
            if read_before[name]:
                pe.wait_ge(slot_read[slot_of[name]], read_before[name])
            return slot(name)

        def full(name):
            return slot_full[slot_of[name]]

        def read(name):
            return slot_read[slot_of[name]]

        def wait_full(eng, name, banks=2):
            eng.wait_ge(slot_full[slot_of[name]], full_before[name] + banks)

        def wait_read(eng, name, reads=1):
            eng.wait_ge(slot_read[slot_of[name]], read_before[name] + reads)

        block = ctx.enter_context(nc.Block())

        @block.sync
        def _(sp):
            for bb in range(2):
                sp.dma_start(X[64 * bb:64 * bb + 64, :, :], io["x"][8 * bb:8 * bb + 8].rearrange("t s d -> s t d"))\
                    .then_inc(ld_x, 16)
            sp.dma_start(consts[:, :], io["consts"]).then_inc(ld_small, 16)
            sp.dma_start(bmask[:, :], io["bmask"]).then_inc(ld_small, 16)
            sp.dma_start(cols[:, :], io["cols"]).then_inc(ld_small, 16)
            sp.dma_start(wb[:, :], io["wb"]).then_inc(ld_wb, 16)
            sp.dma_start(sel[:, :, :], io["sel"]).then_inc(ld_sel, 16)
            wait_read(sp, "nx", 2)
            sp.dma_start(stage[:, L1_AT:L1_AT + L1W], io["w_l1"]).then_inc(ld_l1, 16)
            for hp in range(HP):
                if hp >= 2:
                    sp.wait_ge(acc_full, ACC_COUNT["l2"] + 8 * (hp - 1))
                sp.dma_start(w_l2[hp % 2], io["w_l2"][hp]).then_inc(ld_l2[hp % 2], 16)
            sp.wait_ge(acc_full, ACC_COUNT["l2"] + 64)
            sp.dma_start(stage[:, 0:L3W], io["w_l3"]).then_inc(ld_l3, 16)
            sp.wait_ge(x_final, 1)
            for bb in range(2):
                sp.dma_start(io["y"][8 * bb:8 * bb + 8].rearrange("t s d -> s t d"), X[64 * bb:64 * bb + 64, :, :])\
                    .then_inc(stored, 16)
            sp.wait_ge(stored, 32)

        @block.gpsimd
        def _(pool):
            steps = [0]

            def settle(ins):
                steps[0] += 1
                ins.then_inc(pool_step, 1)
                pool.wait_ge(pool_step, steps[0])

            def rsqrt(l):
                for p in range(2):
                    q = slice(4 * p, 4 * p + 4)
                    pool.wait_ge(ln_var, 2 * l + p + 1)
                    pool.tensor_tensor(rstd[:, q], vareps[:, q], minus_half[:, q], ALU.pow).then_inc(ln_rstd, 1)

            def add_row(l, name):
                pool.wait_ge(xn_ready, 2 * l + 2)
                pool.tensor_tensor(X[:, :, :], X[:, :, :], over(row(name), T), ALU.add).then_inc(x_added, 1)

            def keys(i, t):
                n = 8 * ATT[i] + t
                if t >= 2:
                    wait_read(pool, f"s{i}.{t - 2}")
                src = (ctxT if i == 0 else KT)[:, 128 * t:128 * t + 128].rearrange("p (b k) -> p b k", b=2)
                pool.tensor_tensor(KX[t % 2][:, :, :, :], over(src, H, 2),
                                   over(over(const("headof"), S, 2), 2, 1), ALU.mult).then_inc(kx_ready, 1)

            def attention_keys(i):
                for t in range(2, T):
                    keys(i, t)

            pool.memset(minus_half[:, :], -0.5).then_inc(cleared, 1)
            pool.wait_ge(cleared, 1)
            rsqrt(0)
            pool.wait_ge(ld_small, 48)
            pool.wait_ge(ld_ctxT, 16)
            keys(0, 0)
            keys(0, 1)
            for v in VX:
                pool.memset(v[:, :, :, :, :], 0.0).then_inc(cleared, 1)
            pool.memset(G3[:, :, :], 0.0).then_inc(cleared, 1)
            pool.wait_ge(cleared, 4)
            for v in VX:
                for j in range(2):
                    pool.memset(v[64 * j:64 * j + 64, :, :, j, 8:9], 1.0).then_inc(cleared, 1)
            for t in range(2, T + 2):
                if t < T:
                    keys(0, t)
                u = t - 2
                pool.wait_ge(at_out, u + 1)
                pool.tensor_tensor(X[:, u, :], X[:, u, :], ON[:, u, :], ALU.add).then_inc(x_added, 1)
            rsqrt(1)
            rsqrt(2)
            for p in range(2):
                q = slice(4 * p, 4 * p + 4)
                pool.wait_ge(nx_gelu, p + 1)
                pool.tensor_tensor(X[:, q, :], X[:, q, :], ON[:, q, :], ALU.add).then_inc(x_added, 1)
            rsqrt(3)
            pool.wait_ge(k_ready, 2)
            keys(1, 0)
            keys(1, 1)
            pool.wait_ge(ld_rows, 16)
            add_row(3, "bo1")
            attention_keys(1)
            rsqrt(4)
            rsqrt(5)
            rsqrt(6)
            add_row(6, "ln2_b")
            for hp in range(HP):
                if hp == 0:
                    for m in range(2):
                        wait_read(pool, f"{'qk'[m]}a.0")
                        wait_read(pool, f"{'qk'[m]}b.0")
                        dst, rot = (QT[:, :], ROTQ) if m == 0 else (KT[:, :], ROTK)
                        pool.tensor_tensor(dst, dst, rot, ALU.add).then_inc(roped, 1)
                pool.wait_ge(s_recip, hp + 1)
                pb = PB[:, hp % 2, :].rearrange("p (g k) -> p g k", g=16)
                pool.tensor_tensor(pb, pb, over(rsum2[:, hp % 2, :], 64, 2), ALU.mult).then_inc(s_norm, 1)
                for t in range(T):
                    wait_read(pool, f"y.{hp}.{t}")
                    yb = YG[t % 2].rearrange("p (j e v) -> p j e v", j=2, e=E0)
                    settle(pool.tensor_tensor(yb[:, :, 0:4, :], yb[:, :, 0:4, :], yb[:, :, 4:8, :], ALU.add))
                    settle(pool.tensor_tensor(yb[:, :, 0:2, :], yb[:, :, 0:2, :], yb[:, :, 2:4, :], ALU.add))
                    if t == 0 and hp >= 1:
                        wait_full(pool, f"o.{hp - 1}")
                    pool.tensor_tensor(V2[:, t, :, :], yb[:, :, 0, :], yb[:, :, 1, :], ALU.add).then_inc(v_ready, 1)
                if hp < HP - 1:
                    for m in range(2):
                        wait_read(pool, f"{'qk'[m]}a.{hp + 1}")
                        wait_read(pool, f"{'qk'[m]}b.{hp + 1}")
                        dst, rot = (QT[:, :], ROTQ) if m == 0 else (KT[:, :], ROTK)
                        pool.tensor_tensor(dst, dst, rot, ALU.add).then_inc(roped, 1)
            rsqrt(7)
            pool.wait_ge(xn_ready, 16)
            settle(pool.tensor_tensor(XN[0][:, :, :], XN[1][:, :, :], over(row("ln1_gr"), T), ALU.mult))
            settle(pool.tensor_tensor(XN[0][:, :, :], XN[0][:, :, :], over(row("ln1_br"), T), ALU.add))
            pool.tensor_tensor(XN[0][:, :, :], XN[0][:, :, :], over(row("b2_2"), T), ALU.add).then_inc(y1_ready, 1)
            wait_read(pool, "k3", 2)
            keys(3, 0)
            keys(3, 1)
            rsqrt(8)
            rsqrt(9)
            add_row(9, "bo3")
            attention_keys(3)
            rsqrt(10)

        @block.scalar
        def _(act):
            act.dma_start(ctxT[:, :], io["ctxT"]).then_inc(ld_ctxT, 16)
            act.dma_start(ctxV, io["ctxV"]).then_inc(ld_ctxV, 16)
            act.dma_start(rows[:, :], io["rows"].partition_broadcast(P)).then_inc(ld_rows, 16)
            for bb in range(2):
                act.dma_start(maskI[64 * bb:64 * bb + 64, :, :],
                              io["mask"][8 * bb:8 * bb + 8].rearrange("t q k -> q t k")).then_inc(ld_mask, 16)
            act.dma_start(stage[:, 0:L0W], io["w_l0"]).then_inc(ld_l0, 16)
            for bb in range(2):
                act.dma_start(ctxR[64 * bb:64 * bb + 64, :, :],
                              io["ctx"][8 * bb:8 * bb + 8].rearrange("t s d -> s t d")).then_inc(ld_ctxR, 16)

            def columns(n, scale=None, bias=None):
                for p in range(2):
                    wait_full(act, f"x.{n}", p + 1)
                    out, src = half(XT[n % 2], p), half(slot(f"x.{n}"), p)
                    if scale is None:
                        act.activation(out, src, ACT.Copy).then_inc(read(f"x.{n}"), 1)
                    else:
                        act.activation(out, src, ACT.Identity, scale=scale, bias=bias).then_inc(read(f"x.{n}"), 1)

            def attention(i):
                for t in range(T + 1):
                    if t < T:
                        wait_read(act, f"s{i}.{t}")
                        act.activation(PB[:, t % 3, :], PB[:, t % 3, :], ACT.Exp, scale=8.0 ** -0.5)\
                            .then_inc(at_exp, 1)
                    if t >= 1:
                        u = t - 1
                        if u >= 2:
                            act.wait_ge(acc_full, ACC_COUNT[f"att{i}"] + u - 1)
                        for p in range(2):
                            wait_full(act, f"p{i}.{u}", p + 1)
                            act.activation(half(PT[u % 2], p), half(slot(f"p{i}.{u}"), p), ACT.Copy)\
                                .then_inc(read(f"p{i}.{u}"), 1)

            def out_columns(i):
                for p in range(2):
                    wait_full(act, f"ot{i}", p + 1)
                    act.activation(half(OC, p), half(slot(f"ot{i}"), p), ACT.Copy).then_inc(read(f"ot{i}"), 1)

            def gate_columns(name, out):
                wait_full(act, name, 1)
                act.activation(out, slot(name)[0:96, 0:512].bitcast(BF16), ACT.Copy).then_inc(read(name), 1)

            columns(0)
            attention(0)
            act.wait_ge(ld_small, 48)
            columns(1, col("ln_scale"), col("ln_bias"))
            for p in range(2):
                wait_full(act, "xa", p + 1)
                act.activation(half(XAT, p), half(slot("xa"), p), ACT.Identity, bias=col("attn_b"))\
                    .then_inc(read("xa"), 1)
            act.wait_ge(vx_ready, 1)
            for t in range(T):
                wait_full(act, f"h.{t}", 1)
                if t >= 2:
                    act.wait_ge(acc_full, ACC_COUNT["eo"] + t - 1)
                for c in range(4):
                    f = slice(128 * c, 128 * c + 128)
                    ins = act.activation(big[:, 2 + t % 2, f], slot(f"h.{t}")[:, f], ACT.Gelu,
                                         bias=col("b1_0", 4 * t + c))
                ins.then_inc(read(f"h.{t}"), 1)
            for p in range(2):
                q = slice(4 * p, 4 * p + 4)
                wait_read(act, "nx", p + 1)
                act.activation(ON[:, q, :], ON[:, q, :], ACT.Gelu).then_inc(nx_gelu, 1)
            columns(2)
            attention(1)
            out_columns(1)
            columns(3)
            wait_full(act, "rt", 1)
            act.activation(SC[:, :, :], slot("rt")[:, 0:128].rearrange("p (t e) -> p t e", t=T),
                           ACT.Sigmoid).then_inc(read("rt"), 1)
            for c in range(9):
                if c >= 2:
                    wait_read(act, f"U.{c - 2}")
                for p in range(2):
                    wait_full(act, f"G.{c}", p + 1)
                    act.activation(half(big[:, c % 2, :], p), half(slot(f"G.{c}"), p), ACT.Silu)\
                        .then_inc(read(f"G.{c}"), 1)
                if c == 0:
                    gate_columns("gt1", GT[:, :])
            columns(4)
            wait_read(act, "s2")
            act.activation(PB[:, 0, :], PB[:, 0, :], ACT.Exp, scale=128.0 ** -0.5).then_inc(at_exp, 1)
            for p in range(2):
                wait_full(act, "p2", p + 1)
                act.activation(half(PT[0], p), half(slot("p2"), p), ACT.Copy).then_inc(read("p2"), 1)
            columns(5)
            for g in range(2):
                wait_full(act, f"gs.{g}")
                act.activation(big[:, g, :], slot(f"gs.{g}"), ACT.Sigmoid).then_inc(read(f"gs.{g}"), 1)
            for hp in range(HP):
                wait_read(act, f"s.{hp}")
                act.activation(PB[:, hp % 2, :], PB[:, hp % 2, :], ACT.Exp, scale=64.0 ** -0.5).then_inc(s_exp, 1)
                if hp == 0:
                    for g in range(4):
                        gate_columns(f"gt2.{g}", GTh[:, g, :])
                for p in range(2):
                    wait_full(act, f"pt.{hp}", p + 1)
                    act.activation(half(PT[0], p), half(slot(f"pt.{hp}"), p), ACT.Copy).then_inc(read(f"pt.{hp}"), 1)
                if hp >= 1:
                    wait_read(act, f"E2.{hp - 1}.7")
                for b in range(2):
                    wait_full(act, f"o.{hp}", b + 1)
                    act.activation(OC[:, :].rearrange("p (t b q) -> p t b q", t=T, b=2)[:, :, b, :],
                                   half(slot(f"o.{hp}"), b).rearrange("p (t q) -> p t q", t=T), ACT.Copy)\
                        .then_inc(read(f"o.{hp}"), 1)
            for p in range(2):
                wait_full(act, "k3", p + 1)
                act.activation(half(KT, p), half(slot("k3"), p), ACT.Identity, bias=col("bk3"))\
                    .then_inc(read("k3"), 1)
            columns(6, col("ln1_g"), col("ln1_b"))
            for c in range(4):
                wait_full(act, f"f.{c}")
                act.activation(big[:, c, :], slot(f"f.{c}"), ACT.Relu, bias=col("b1_2", c)).then_inc(read(f"f.{c}"), 1)
            columns(7)
            for p in range(2):
                wait_full(act, "q3", p + 1)
                act.activation(half(QT, p), half(slot("q3"), p), ACT.Identity, bias=col("bq3"))\
                    .then_inc(read("q3"), 1)
            attention(3)
            out_columns(3)
            columns(8)

            def relu(m, e):
                name = f"h{m}.{e}"
                wait_full(act, name)
                if m == 2 and e >= 2:
                    wait_read(act, f"E3.{e - 2}")
                act.activation(big[:, 2 * (m - 1) + e % 2, :], slot(name), ACT.Relu,
                               bias=row(f"b{m}_3")[:, e:e + 1]).then_inc(read(name), 1)

            act.wait_ge(l3_shift, 1)
            act.activation(small[:, 0:128], small[:, 0:128], ACT.Exp).then_inc(l3_exp, 1)
            relu(1, 0)
            gate_columns("gt3", GT[:, :])
            for e in range(16):
                if e > 0:
                    relu(1, e)
                relu(2, e)

        @block.vector
        def _(dve):
            steps = [0]

            def settle(ins):
                steps[0] += 1
                ins.then_inc(dve_step, 1)
                dve.wait_ge(dve_step, steps[0])

            def norm(l, src, wait=None):
                dst = XN[LN_ROWS[l]]
                for p in range(2):
                    q = slice(4 * p, 4 * p + 4)
                    for t in range(4 * p, 4 * p + 4):
                        if wait is not None:
                            wait(t)
                        ins = dve.bn_stats(stats[:, t, :], src[:, t, :])
                    settle(ins)
                    for t in range(4 * p, 4 * p + 4):
                        ins = dve.bn_aggr(meanvar[:, t, :], stats[:, t, :])
                    settle(ins)
                    dve.tensor_scalar(vareps[:, q], meanvar[:, q, 1], EPS, None, ALU.add).then_inc(ln_var, 1)
                for p in range(2):
                    dve.wait_ge(ln_rstd, 2 * l + p + 1)
                    for t in range(4 * p, 4 * p + 4):
                        ins = dve.tensor_scalar(dst[:, t, :], src[:, t, :], meanvar[:, t, 0:1], rstd[:, t:t + 1],
                                                ALU.subtract, ALU.mult)
                    ins.then_inc(xn_ready, 1)
                dve.wait_ge(xn_ready, 2 * l + 2)

            def attention(i):
                for t in range(T + 2):
                    if t < T:
                        name = f"s{i}.{t}"
                        wait_full(dve, name)
                        if t >= 3:
                            wait_full(dve, f"p{i}.{t - 3}")
                        sc = slot(name).rearrange("p (h k) -> p h k", h=H)
                        m = mx2[:, t % 2, :]
                        settle(dve.tensor_reduce(m, sc, AX.X, ALU.max))
                        dve.tensor_tensor(PB[:, t % 3, :].rearrange("p (h k) -> p h k", h=H), sc,
                                          over(m, S, 2), ALU.subtract).then_inc(read(name), 1)
                    if t >= 2:
                        u = t - 2
                        dve.wait_ge(acc_full, ACC_COUNT[f"att{i}"] + u + 1)
                        o = ACC[:, 512 * (u % 2):512 * (u % 2) + 144].rearrange("p (h d) -> p h d", h=H)
                        r = rsum2[:, u % 2, :]
                        settle(dve.reciprocal(r, o[:, :, 8]))
                        dve.tensor_tensor(ON[:, u, :].rearrange("p (h d) -> p h d", h=H), o[:, :, 0:8],
                                          over(r, 8, 2), ALU.mult).then_inc(at_out, 1)

            def values(i, bias, v):
                for n in range(2):
                    name = f"v{i}.{n}"
                    for m in range(2):
                        wait_full(dve, name, m + 1)
                        for j in range(2):
                            rows_j = slice(64 * j, 64 * j + 64)
                            dve.tensor_tensor(
                                VX[v][rows_j, 8 * n + 4 * m:8 * n + 4 * m + 4, :, j, 0:8],
                                half(slot(name), m)[rows_j].rearrange("p (b h j d) -> p b h j d", b=4, h=HP, j=2)[:, :, :, j, :],
                                over(bias[rows_j].rearrange("p (h j d) -> p h j d", h=HP, j=2)[:, :, j, :], 4),
                                ALU.add).then_inc(read(name), 1)

            def rope1(a, b, bias_a, bias_b, out, done):
                for p in range(2):
                    wait_full(dve, a, p + 1)
                    v = lambda x: half(x, p).rearrange("p (b k) -> p b k", k=S)
                    dve.scalar_tensor_tensor(out=v(out), in0=v(slot(a)), scalar=bias_a, in1=over(const("cos1"), 8),
                                             op0=ALU.add, op1=ALU.mult).then_inc(read(a), 1)
                    wait_full(dve, b, p + 1)
                    dve.scalar_tensor_tensor(out=v(PB[:, 0, :]), in0=v(slot(b)), scalar=bias_b,
                                             in1=over(const("sin1"), 8), op0=ALU.add, op1=ALU.mult)\
                        .then_inc(read(b), 1)
                    wait_read(dve, b, p + 1)
                    dve.tensor_tensor(half(out, p), half(out, p), half(PB[:, 0, :], p), ALU.add).then_inc(done, 1)

            def add_out(name):
                for p in range(2):
                    q = slice(4 * p, 4 * p + 4)
                    wait_full(dve, name, p + 1)
                    dve.tensor_tensor(X[:, q, :], X[:, q, :], half(slot(name), p).rearrange("p (t n) -> p t n", t=4),
                                      ALU.add).then_inc(read(name), 1)
                wait_read(dve, name, 2)

            def three_parts(gates, dst, n, rest):
                settle(dve.tensor_copy(dst(0), gates))
                settle(dve.tensor_tensor(rest, gates, dst(0), ALU.subtract))
                settle(dve.tensor_copy(dst(1), rest))
                settle(dve.tensor_tensor(rest, rest, dst(1), ALU.subtract))
                dve.tensor_copy(dst(2), rest).then_inc(gates_ready, 1)

            def ranks(v, n, lt, work, work2, out):
                a, b = over(v, n, 2), over(v, n, 3)
                settle(dve.tensor_tensor(work, a, b, ALU.is_equal))
                settle(dve.tensor_tensor(work, work, over(lt, T), ALU.mult))
                settle(dve.tensor_tensor(work2, a, b, ALU.is_gt))
                settle(dve.tensor_tensor(work, work, work2, ALU.add))
                settle(dve.tensor_reduce(out, work, AX.X, ALU.add))

            dve.wait_ge(ld_x, 32)
            norm(0, X)
            dve.wait_ge(ld_ctxV, 16)
            dve.wait_ge(cleared, 8)
            for j in range(2):
                r = slice(64 * j, 64 * j + 64)
                ins = dve.tensor_copy(VX[0][r, :, :, j, 0:8], ctxV[r])
            ins.then_inc(vx_ready, 1)
            attention(0)
            norm(1, X, lambda t: dve.wait_ge(x_added, t + 1))
            norm(2, XN[1])
            dve.wait_ge(ld_small, 48)
            rope1("k1a", "k1b", col("bk1"), col("bk1p"), KT, k_ready)
            dve.wait_ge(ld_rows, 16)
            values(1, row("bv1"), 1)
            dve.wait_ge(ld_mask, 32)
            dve.tensor_scalar(maskB[:, :, :], maskI, 0.0, HIDDEN, ALU.is_equal, ALU.mult).then_inc(mask_ready, 1)
            for p in range(2):
                dve.wait_ge(acc_full, ACC_COUNT["eo"] + 4 * p + 4)
                dve.tensor_tensor(half(OC, p).rearrange("p (t n) -> p t n", t=4),
                                  half(ACC, p).rearrange("p (t n) -> p t n", t=4),
                                  over(col("b2_0", 4 * p, 4), P, 2), ALU.add).then_inc(acc_read, 1)
            for p in range(2):
                q = slice(4 * p, 4 * p + 4)
                wait_full(dve, "nx", p + 1)
                dve.tensor_tensor(ON[:, q, :], half(slot("nx"), p).rearrange("p (t n) -> p t n", t=4),
                                  over(row("next_b"), 4), ALU.add).then_inc(read("nx"), 1)
            norm(3, X, lambda t: dve.wait_ge(x_added, 8 + t // 4 + 1))
            rope1("qa", "qb", col("bq1"), col("bq1p"), QT, q_ready)
            attention(1)
            dve.wait_ge(x_added, 11)
            add_out("out1")
            norm(4, X)
            wait_read(dve, "rt")
            s4 = SC[:, :, :].rearrange("p t (g e) -> p (t g) e", g=4)
            pairs = small[:, 0:192].rearrange("p (g n) -> p g n", n=6)
            gsum = small[:, 192:224].rearrange("p (t g) -> p t g", t=T)
            grank = small[:, 224:256].rearrange("p (t g) -> p t g", t=T)
            masked = small[:, 256:384].rearrange("p (t e) -> p t e", t=T)
            erank = small[:, 384:512].rearrange("p (t e) -> p t e", t=T)
            wsum = small[:, 512:520]
            rest = small[:, 640:768].rearrange("p (t e) -> p t e", t=T)
            w4 = [small[:, 768 + 128 * i:896 + 128 * i].rearrange("p (t a b) -> p t a b", t=T, a=4) for i in range(2)]
            w16 = [big[:, 4:6, :], PB[:, 0:2, :]]
            w16 = [w.rearrange("p a (t x y) -> p (a t) x y", t=4, x=16) for w in w16]
            dve.tensor_tensor(pairs[:, :, 0:3], s4[:, :, 0:3], s4[:, :, 1:4], ALU.add)
            dve.tensor_tensor(pairs[:, :, 3:5], s4[:, :, 0:2], s4[:, :, 2:4], ALU.add)
            settle(dve.tensor_tensor(pairs[:, :, 5:6], s4[:, :, 0:1], s4[:, :, 3:4], ALU.add))
            settle(dve.tensor_reduce(small[:, 192:224], pairs, AX.X, ALU.max))
            ranks(gsum, 4, const("lt4").rearrange("p (a b) -> p a b", a=4), w4[0], w4[1], grank)
            settle(dve.tensor_scalar(grank, grank, 2.0, 2.0, ALU.is_lt, ALU.mult))
            settle(dve.tensor_scalar(grank, grank, -2.0, None, ALU.add))
            settle(dve.tensor_tensor(masked.rearrange("p t (g e) -> p (t g) e", g=4), s4,
                                     over(small[:, 224:256], 4, 2), ALU.add))
            ranks(masked, 16, const("lt16").rearrange("p (a b) -> p a b", a=16), w16[0], w16[1], erank)
            settle(dve.scalar_tensor_tensor(out=erank, in0=erank, scalar=4.0, in1=SC[:, :, :],
                                            op0=ALU.is_lt, op1=ALU.mult))
            settle(dve.tensor_reduce(wsum, erank, AX.X, ALU.add))
            settle(dve.tensor_scalar(wsum, wsum, 1e-6, None, ALU.add))
            settle(dve.reciprocal(wsum, wsum))
            settle(dve.tensor_tensor(erank, erank, over(wsum, 16, 2), ALU.mult))
            three_parts(erank, lambda i: G3[:, :, 16 * i:16 * i + 16], 16, rest)
            for c in range(9):
                wait_read(dve, f"G.{c}", 2)
                wait_full(dve, f"U.{c}")
                if c >= 2:
                    dve.wait_ge(acc_full, ACC_COUNT["l1"] + c - 1)
                hid = big[:, 2 + c % 2, :]
                dve.tensor_tensor(hid, big[:, c % 2, :], slot(f"U.{c}"), ALU.mult).then_inc(read(f"U.{c}"), 1)
                if c < 8:
                    wait_full(dve, f"E1.{c}")
                    wait_read(dve, f"U.{c}")
                    dve.tensor_tensor(hid, hid, slot(f"E1.{c}"), ALU.mult).then_inc(read(f"E1.{c}"), 1)
            dve.wait_ge(acc_full, ACC_COUNT["l1"] + 9)
            settle(dve.tensor_tensor(X[:, :, :], X[:, :, :], ACC.rearrange("p (t n) -> p t n", t=T), ALU.add))
            norm(5, X)
            wait_full(dve, "s2")
            s2 = slot("s2").rearrange("p (t k) -> p t k", t=T)
            p2 = PB[:, 0, :].rearrange("p (t k) -> p t k", t=T)
            settle(dve.tensor_reduce(mx[:, 0:8], s2, AX.X, ALU.max))
            dve.tensor_tensor(p2, s2, over(mx[:, 0:8], P, 2), ALU.subtract).then_inc(read("s2"), 1)
            dve.wait_ge(at_exp, 17)
            settle(dve.tensor_reduce(rsum[:, 0:8], p2, AX.X, ALU.add))
            settle(dve.reciprocal(rsum[:, 0:8], rsum[:, 0:8]))
            for t in range(T):
                wait_full(dve, "o2", t // 4 + 1)
                ins = dve.scalar_tensor_tensor(out=X[:, t, :], in0=slot("o2")[:, 128 * t:128 * t + 128],
                                               scalar=rsum[:, t:t + 1], in1=X[:, t, :], op0=ALU.mult, op1=ALU.add)
                if t % 4 == 3:
                    ins.then_inc(read("o2"), 1)
            wait_read(dve, "o2", 2)
            norm(6, X)

            def rope2_product(hp, k):
                m, n = k // 2, k % 2
                name = f"{'qk'[m]}{'ab'[n]}.{hp}"
                wait_full(dve, name)
                if hp >= 1:
                    dve.wait_ge(roped, 2 * hp)
                dst = ((QT[:, :], ROTQ), (KT[:, :], ROTK))[m][n]
                v = lambda x: x.rearrange("p (b k) -> p b k", k=S)
                dve.tensor_tensor(v(dst), v(slot(name)), over(const(("cos2", "sin2")[n]), 16), ALU.mult)\
                    .then_inc(read(name), 1)

            flat = big[:, 0:2, :].rearrange("p a (g e) -> p (a g) e", e=E0)
            eq = big[:, 2:4, :].rearrange("p a (g e) -> p (a g) e", e=E0)
            first = big[:, 4:6, :].rearrange("p a (g e) -> p (a g) e", e=E0)
            left = PB[:, 0:2, :].rearrange("p a (g e) -> p (a g) e", e=E0)
            best = small[:, 0:256]
            wait_read(dve, "gs.0")
            wait_read(dve, "gs.1")
            for n in range(2):
                src = flat if n == 0 else left
                out = first if n == 0 else eq
                settle(dve.tensor_reduce(best, src, AX.X, ALU.max))
                settle(dve.tensor_tensor(eq, src, over(best, E0, 2), ALU.is_equal))
                settle(dve.tensor_tensor(eq, eq, over(const("prefer"), 256), ALU.mult))
                settle(dve.tensor_reduce(best, eq, AX.X, ALU.max))
                settle(dve.tensor_tensor(out, eq, over(best, E0, 2), ALU.is_equal))
                if n == 0:
                    settle(dve.scalar_tensor_tensor(out=left, in0=first, scalar=-4.0, in1=flat,
                                                    op0=ALU.mult, op1=ALU.add))
            settle(dve.tensor_tensor(eq, eq, first, ALU.add))
            settle(dve.tensor_tensor(flat, flat, eq, ALU.mult))
            for h in range(2):
                q = slice(4 * h, 4 * h + 4)
                gates = GVO[:, q, 1, :].rearrange("p t (h g) -> p t h g", h=HP)
                rest2 = big[:, 2, 0:512].rearrange("p (t h g) -> p t h g", t=4, h=HP)
                three_parts(gates, lambda i: G3h[:, q, :, 16 * i:16 * i + 16], 16, rest2)
                dve.wait_ge(gates_ready, 2 + h)
            for k in range(4):
                rope2_product(0, k)
            for hp in range(HP):
                name = f"s.{hp}"
                wait_full(dve, name)
                if hp >= 2:
                    wait_full(dve, f"pt.{hp - 2}")
                if hp >= 2:
                    dve.wait_ge(s_norm, hp - 1)
                sc = slot(name).rearrange("p (g k) -> p g k", g=16)
                pb = PB[:, hp % 2, :].rearrange("p (g k) -> p g k", g=16)
                settle(dve.tensor_reduce(mx2[:, hp % 2, :], sc, AX.X, ALU.max))
                dve.tensor_tensor(pb, sc, over(mx2[:, hp % 2, :], S, 2), ALU.subtract).then_inc(read(name), 1)
                for t in range(T):
                    name = f"y.{hp}.{t}"
                    wait_full(dve, name)
                    if hp * T + t >= 2:
                        dve.wait_ge(v_ready, hp * T + t - 1)
                    dve.tensor_tensor(YG[t % 2].rearrange("p (g v) -> p g v", v=64),
                                      slot(name).rearrange("p (g v) -> p g v", v=64),
                                      over(GVO[:, t, 0, 16 * hp:16 * hp + 16], 64, 2), ALU.mult)\
                        .then_inc(read(name), 1)
                    if t == 1:
                        dve.wait_ge(s_exp, hp + 1)
                        settle(dve.tensor_reduce(rsum2[:, hp % 2, :], pb, AX.X, ALU.add))
                        dve.reciprocal(rsum2[:, hp % 2, :], rsum2[:, hp % 2, :]).then_inc(s_recip, 1)
                wait_read(dve, f"o.{hp}", 2)
                if hp == 0:
                    wait_full(dve, "gt2.3", 1)
                for e in range(E0):
                    n = 8 * hp + e
                    name = f"E2.{hp}.{e}"
                    wait_full(dve, name)
                    if n >= 2:
                        dve.wait_ge(acc_full, ACC_COUNT["l2"] + n - 1)
                    dve.tensor_tensor(AT[e % 2], OC[:, :], slot(name), ALU.mult).then_inc(read(name), 1)
                    if hp < HP - 1 and e % 2 == 1:
                        rope2_product(hp + 1, e // 2)
            dve.wait_ge(acc_full, ACC_COUNT["l2"] + 64)
            settle(dve.tensor_tensor(XN[0][:, :, :], XN[0][:, :, :], ACC.rearrange("p (t n) -> p t n", t=T), ALU.add))
            norm(7, XN[0])
            values(3, row("bv3"), 0)
            dve.wait_ge(y1_ready, 1)
            for p in range(2):
                q = slice(4 * p, 4 * p + 4)
                dve.wait_ge(acc_full, ACC_COUNT["ff"] + p + 1)
                ins = dve.tensor_tensor(XN[0][:, q, :], XN[0][:, q, :],
                                        half(ACC, p).rearrange("p (t n) -> p t n", t=4), ALU.add)
            settle(ins)
            norm(8, XN[0])
            settle(dve.tensor_tensor(XN[1][:, :, :], XN[1][:, :, :], over(row("ln2_g"), T), ALU.mult))
            dve.wait_ge(x_added, 12)
            settle(dve.tensor_tensor(X[:, :, :], X[:, :, :], XN[1][:, :, :], ALU.add))
            norm(9, X)
            attention(3)
            dve.wait_ge(x_added, 13)
            add_out("out3")
            norm(10, X)
            logits = small[:, 0:128]
            by_batch = logits.rearrange("p (b k) -> p b k", b=2)
            work = small[:, 128:256]
            rowgate = small[:, 256:384].rearrange("p (t e) -> p t e", t=T)
            best8 = small[:, 384:400]
            outbias = small[:, 400:408]
            rest = small[:, 512:640].rearrange("p (t e) -> p t e", t=T)
            wait_full(dve, "lg", 1)
            dve.tensor_scalar(logits, slot("lg")[:, 0:128], col("bg"), None, ALU.add).then_inc(read("lg"), 1)
            wait_read(dve, "lg")
            settle(dve.tensor_reduce(mx[:, 0:2], by_batch, AX.X, ALU.max))
            dve.tensor_tensor(by_batch, by_batch, over(mx[:, 0:2], S, 2), ALU.subtract).then_inc(l3_shift, 1)
            dve.wait_ge(l3_exp, 1)
            settle(dve.tensor_reduce(rsum[:, 0:2], by_batch, AX.X, ALU.add))
            settle(dve.reciprocal(rsum[:, 0:2], rsum[:, 0:2]))
            settle(dve.tensor_tensor(by_batch, by_batch, over(rsum[:, 0:2], S, 2), ALU.mult))
            settle(dve.tensor_copy(work, logits))
            for k in range(4):
                for b in range(2):
                    ins = dve.max(best8[:, 8 * b:8 * b + 8], work[:, 64 * b:64 * b + 64])
                settle(ins)
                for b in range(2):
                    w = work[:, 64 * b:64 * b + 64]
                    ins = dve.match_replace(w, best8[:, 8 * b:8 * b + 8], w, -1.0)
                settle(ins)
            dve.scalar_tensor_tensor(out=logits, in0=work, scalar=0.0, in1=logits, op0=ALU.is_lt, op1=ALU.mult)\
                .then_inc(l3_val, 1)
            wait_full(dve, "vt", 1)
            dve.tensor_copy(small[:, 256:384], slot("vt")[:, 0:128]).then_inc(read("vt"), 1)
            wait_read(dve, "vt")
            three_parts(rowgate, lambda i: G3[:, :, 16 * i:16 * i + 16], 16, rest)
            dve.wait_ge(gates_ready, 4)
            settle(dve.tensor_tensor(rest, rowgate, over(row("b3_3"), T), ALU.mult))
            settle(dve.tensor_reduce(outbias, rest, AX.X, ALU.add))
            for e in range(16):
                wait_read(dve, f"h2.{e}")
                wait_full(dve, f"E3.{e}")
                if e >= 2:
                    dve.wait_ge(acc_full, ACC_COUNT["l3"] + e - 1)
                dve.tensor_tensor(big[:, 4 + e % 2, :], big[:, 2 + e % 2, :], slot(f"E3.{e}"), ALU.mult)\
                    .then_inc(read(f"E3.{e}"), 1)
            dve.wait_ge(acc_full, ACC_COUNT["l3"] + 16)
            for t in range(T):
                ins = dve.scalar_tensor_tensor(out=X[:, t, :], in0=ACC[:, 128 * t:128 * t + 128],
                                               scalar=outbias[:, t:t + 1], in1=X[:, t, :], op0=ALU.add, op1=ALU.add)
            ins.then_inc(x_final, 1)

        @block.tensor
        def _(pe):
            def done(ins, name):
                ins.then_inc(full(name), 1)

            def rows_to_columns(n, src=None):
                l = COLUMNS_OF[n]
                name = f"x.{n}"
                s = take(pe, name)
                for t in range(T):
                    if t % 4 == 0:
                        pe.wait_ge(xn_ready, 2 * l + t // 4 + 1)
                    ins = pe.transpose(s[:, 128 * t:128 * t + 128], XN[LN_ROWS[l]][:, t, :], ident)
                    if t % 4 == 3:
                        done(ins, name)

            def project(name, w, x, wait=None):
                s = take(pe, name)
                for p in range(2):
                    if wait is not None:
                        wait(p)
                    done(pe.matmul(half(s, p), w, half(x, p), start=True, stop=True), name)

            def columns_there(n):
                return lambda p: wait_read(pe, f"x.{n}", p + 1)

            def project_rows(name, x, w, wait=None):
                s = take(pe, name)
                for t in range(T):
                    if wait is not None and t % 4 == 0:
                        wait(t // 4)
                    ins = pe.matmul(s[:, 128 * t:128 * t + 128], x[:, 128 * t:128 * t + 128], w,
                                    start=True, stop=True)
                    if t % 4 == 3:
                        done(ins, name)

            def project_values(i, w):
                for n in range(2):
                    name = f"v{i}.{n}"
                    s = take(pe, name)
                    for b in range(8):
                        tb = 8 * n + b
                        for j in range(2):
                            ins = pe.matmul(s[64 * j:64 * j + 64, 128 * b:128 * b + 128],
                                            ctxT[:, 64 * tb:64 * tb + 64], w, start=True, stop=True)
                        if b % 4 == 3:
                            done(ins, name)

            def attention(i, q, wait_q, mask, v):
                for t in range(T + 2):
                    if t < T:
                        name = f"s{i}.{t}"
                        wait_q(t // 4)
                        pe.wait_ge(kx_ready, 8 * ATT[i] + t + 1)
                        s = take(pe, name)
                        for n in range(2):
                            out = half(s, n)
                            if mask is not None:
                                pe.matmul(out, identb, over(mask(t), 8), start=True, stop=True)
                            for bb in range(2):
                                tok = 128 * t + 64 * bb
                                ins = pe.matmul(out[64 * bb:64 * bb + 64, :], q[:, tok:tok + 64],
                                                KX[t % 2][:, bb, 8 * n:8 * n + 8, :],
                                                start=mask is None, stop=True, skip_group_check=True)
                            done(ins, name)
                    if 1 <= t <= T:
                        u = t - 1
                        name = f"p{i}.{u}"
                        pe.wait_ge(at_exp, 8 * ATT[i] + u + 1 + (i == 3))
                        s = take(pe, name)
                        for hp in range(HP):
                            c = slice(128 * hp, 128 * hp + 128)
                            ins = pe.transpose(s[:, c], PB[:, u % 3, c], ident)
                            if hp % 4 == 3:
                                done(ins, name)
                    if t >= 2:
                        u = t - 2
                        if u == 0:
                            v[1]()
                        wait_read(pe, f"p{i}.{u}", 2)
                        if u >= 2:
                            pe.wait_ge(at_out, 8 * ATT[i] + u - 1)
                        for hp in range(HP):
                            for bb in range(2):
                                at = 512 * (u % 2) + 18 * hp
                                ins = pe.matmul(ACC[64 * bb:64 * bb + 64, at:at + 18],
                                                PT[u % 2][:, 128 * hp + 64 * bb:128 * hp + 64 * bb + 64],
                                                VX[v[0]][:, 2 * u + bb, hp, :, :], start=True, stop=True)
                        ins.then_inc(acc_full, 1)

            def attention_out(i, w):
                name = f"ot{i}"
                s = take(pe, name)
                pe.wait_ge(at_out, 8 * ATT[i] + 8)
                for t in range(T):
                    ins = pe.transpose(s[:, 128 * t:128 * t + 128], ON[:, t, :], ident)
                    if t % 4 == 3:
                        done(ins, name)
                project_rows(f"out{i}", OC, w, lambda p: wait_read(pe, name, p + 1))

            def gate_columns(name, src):
                s = take(pe, name)[0:96, 0:512].bitcast(BF16)
                for t in range(T):
                    ins = pe.transpose(s[:, 128 * t:128 * t + 128], src(t), identb)
                done(ins, name)

            def expand(name, k, gates):
                s = take(pe, name)
                for p in range(2):
                    done(pe.matmul(half(s, p), sel[:, k, :], half(gates, p), start=True, stop=True), name)

            def accumulate(x, w, first, last):
                for t in range(T):
                    ins = pe.matmul(ACC[:, 128 * t:128 * t + 128], x[:, 128 * t:128 * t + 128], w,
                                    start=first and t % 4 == 0, stop=True, skip_group_check=True)
                ins.then_inc(acc_full, 1)

            pe.wait_ge(ld_small, 48)
            rows_to_columns(0)
            attention(0, XT[0], lambda p: wait_read(pe, "x.0", p + 1), lambda t: causal,
                      (0, lambda: pe.wait_ge(vx_ready, 1)))
            pe.wait_ge(ld_wb, 16)
            pe.wait_ge(ld_ctxT, 16)
            project("k1a", weight("wk1"), ctxT)
            project("k1b", weight("wk1p"), ctxT)
            project_values(1, weight("wv1"))
            rows_to_columns(1)
            pe.wait_ge(ld_l0, 16)
            s = take(pe, "xa")
            for p in range(2):
                wait_read(pe, "x.1", p + 1)
                pe.wait_ge(xn_ready, 4)
                pe.matmul(half(s, p), attn_w, half(XT[1], p), start=True, stop=True, skip_group_check=True)
                for t in range(4 * p, 4 * p + 4):
                    ins = pe.matmul(s[:, 128 * t:128 * t + 128], XN[1][:, t, :], ident,
                                    start=False, stop=True, skip_group_check=True)
                done(ins, "xa")
            for t in range(T + 1):
                if t < T:
                    name = f"h.{t}"
                    s = take(pe, name)
                    wait_read(pe, "xa", t // 4 + 1)
                    for c in range(4):
                        ins = pe.matmul(s[:, 128 * c:128 * c + 128], w1_0[:, t, 128 * c:128 * c + 128],
                                        XAT[:, 128 * t:128 * t + 128], start=True, stop=True)
                    done(ins, name)
                if t >= 1:
                    u = t - 1
                    wait_read(pe, f"h.{u}")
                    for c in range(4):
                        ins = pe.matmul(ACC[:, 128 * u:128 * u + 128], w2_0[:, u, c, :],
                                        big[:, 2 + u % 2, 128 * c:128 * c + 128], start=c == 0, stop=c == 3)
                    ins.then_inc(acc_full, 1)
            project_rows("nx", OC, next_w, lambda p: pe.wait_ge(acc_read, p + 1))
            rows_to_columns(2)
            project("qa", weight("wq1"), XT[0], columns_there(2))
            project("qb", weight("wq1p"), XT[0])
            attention(1, QT, lambda p: pe.wait_ge(q_ready, p + 1), None, (1, lambda: wait_read(pe, "v1.1", 4)))
            attention_out(1, weight("wo1"))
            rows_to_columns(3)
            s = take(pe, "rt")
            wait_read(pe, "x.3", 2)
            for t in range(T):
                ins = pe.matmul(s[:, 16 * t:16 * t + 16], XT[1][:, 128 * t:128 * t + 128], weight("w_gate"),
                                start=True, stop=True)
            done(ins, "rt")
            pe.wait_ge(ld_l1, 16)
            pe.wait_ge(ld_sel, 16)
            for c in range(10):
                if c < 9:
                    project(f"G.{c}", w_l1[:, 0, c, :], XT[1])
                    project(f"U.{c}", w_l1[:, 1, c, :], XT[1])
                    if c == 0:
                        pe.wait_ge(gates_ready, 1)
                        gate_columns("gt1", lambda t: G3[:, t, :])
                        wait_read(pe, "gt1")
                    if c < 8:
                        expand(f"E1.{c}", SEL_DUO + c, GT)
                if c >= 1:
                    wait_read(pe, f"E1.{c - 1}" if c < 9 else "U.8")
                    accumulate(big[:, 2 + (c - 1) % 2, :], w_l1[:, 2, c - 1, :], c == 1, c == 9)
            rows_to_columns(4)
            s = take(pe, "s2")
            for p in range(2):
                wait_read(pe, "x.4", p + 1)
                pe.matmul(half(s, p), identb, over(blocks, 4), start=True, stop=True, skip_group_check=True)
                for t in range(4 * p, 4 * p + 4):
                    c = slice(128 * t, 128 * t + 128)
                    ins = pe.matmul(s[:, c], XT[0][:, c], ctxT[:, c], start=False, stop=True,
                                    skip_group_check=True)
                done(ins, "s2")
            s = take(pe, "p2")
            pe.wait_ge(at_exp, 17)
            for t in range(T):
                c = slice(128 * t, 128 * t + 128)
                ins = pe.transpose(s[:, c], PB[:, 0, c], ident)
                if t % 4 == 3:
                    done(ins, "p2")
            s = take(pe, "o2")
            pe.wait_ge(ld_ctxR, 32)
            for t in range(T):
                if t % 4 == 0:
                    wait_read(pe, "p2", t // 4 + 1)
                c = slice(128 * t, 128 * t + 128)
                ins = pe.matmul(s[:, c], PT[0][:, c], ctxR[:, t, :], start=True, stop=True)
                if t % 4 == 3:
                    done(ins, "o2")
            rows_to_columns(5)
            for g in range(2):
                s = take(pe, f"gs.{g}")
                wait_read(pe, "x.5", 2)
                for t in range(4):
                    ins = pe.matmul(s[:, 256 * t:256 * t + 256],
                                    XT[1][:, 128 * (4 * g + t):128 * (4 * g + t) + 128], weight("wsel"),
                                    start=True, stop=True)
                    if t % 2 == 1:
                        done(ins, f"gs.{g}")

            def rope2_job(hp, k):
                project(f"{'qk'[k // 2]}{'ab'[k % 2]}.{hp}", w_l2[hp % 2][:, 128 * k:128 * k + 128], XT[1])

            pe.wait_ge(ld_l2[0], 16)
            for k in range(4):
                rope2_job(0, k)
            for hp in range(HP):
                w = w_l2[hp % 2]
                name = f"s.{hp}"
                s = take(pe, name)
                pe.wait_ge(roped, 2 * hp + 2)
                for t in range(T):
                    for b in range(2):
                        for j in range(2):
                            r, c = slice(64 * j, 64 * j + 64), slice(128 * t + 64 * b, 128 * t + 64 * b + 64)
                            ins = pe.matmul(s[r, c], QT[r, c], KT[r, c], start=True, stop=True)
                    if t % 4 == 3:
                        done(ins, name)
                for t in range(T):
                    name = f"y.{hp}.{t}"
                    s = take(pe, name)
                    for j in range(2):
                        done(pe.matmul(half(s, j), XT[1][:, 128 * t:128 * t + 128],
                                       w[:, 512 + 512 * j:1024 + 512 * j], start=True, stop=True), name)
                if hp == 0:
                    pe.wait_ge(gates_ready, 3)
                    for g in range(4):
                        gate_columns(f"gt2.{g}", lambda t: G3h[:, t, 2 * g:2 * g + 2, :])
                name = f"pt.{hp}"
                s = take(pe, name)
                pe.wait_ge(s_norm, hp + 1)
                for t in range(T):
                    c = slice(128 * t, 128 * t + 128)
                    ins = pe.transpose(s[:, c], PB[:, hp % 2, c], ident)
                    if t % 4 == 3:
                        done(ins, name)
                name = f"o.{hp}"
                s = take(pe, name)
                pe.wait_ge(v_ready, 8 * hp + 8)
                wait_read(pe, f"pt.{hp}", 2)
                for t in range(T):
                    for j in range(2):
                        for b in range(2):
                            r = slice(64 * b, 64 * b + 64)
                            ins = pe.matmul(s[64 * j:64 * j + 64, 512 * b + 64 * t:512 * b + 64 * t + 64],
                                            V2[r, t, j, :], PT[0][r, 128 * t + 64 * j:128 * t + 64 * j + 64],
                                            start=True, stop=True)
                            if t == T - 1 and j == 1:
                                done(ins, name)
                if hp == 0:
                    wait_read(pe, "gt2.3")
                if hp < HP - 1:
                    pe.wait_ge(ld_l2[(hp + 1) % 2], 16 * ((hp + 1) // 2 + 1))
                for e in range(E0 + 1):
                    if e < E0:
                        expand(f"E2.{hp}.{e}", SEL_PAIR + 8 * (hp % 2) + e, GTh[:, hp // 2, :])
                        if hp < HP - 1 and e % 2 == 1:
                            rope2_job(hp + 1, e // 2)
                    if e >= 1:
                        wait_read(pe, f"E2.{hp}.{e - 1}")
                        accumulate(AT[(e - 1) % 2], w[:, 1536 + 128 * (e - 1):1536 + 128 * e],
                                   hp == 0 and e == 1, hp == HP - 1 and e == E0)
            project("k3", weight("wk3"), ctxT)
            project_values(3, weight("wv3"))
            rows_to_columns(6)
            for c in range(4):
                project(f"f.{c}", weight("W1")[:, 128 * c:128 * c + 128], XT[0], columns_there(6))
            for c in range(4):
                wait_read(pe, f"f.{c}")
            for t in range(T):
                for c in range(4):
                    ins = pe.matmul(ACC[:, 128 * t:128 * t + 128], big[:, c, 128 * t:128 * t + 128],
                                    weight("W2")[:, 128 * c:128 * c + 128], start=c == 0, stop=c == 3)
                if t % 4 == 3:
                    ins.then_inc(acc_full, 1)
            rows_to_columns(7)
            project("q3", weight("wq3"), XT[1], columns_there(7))
            pe.wait_ge(mask_ready, 1)
            attention(3, QT, lambda p: wait_read(pe, "q3", p + 1), lambda t: maskB[:, t, :],
                      (0, lambda: wait_read(pe, "v3.1", 4)))
            attention_out(3, weight("wo3"))
            rows_to_columns(8)
            s = take(pe, "lg")
            wait_read(pe, "x.8", 2)
            for t in range(T):
                ins = pe.matmul(s[:, 0:128], weight("wg_pad")[:, 112 - 16 * t:240 - 16 * t],
                                XT[0][:, 128 * t:128 * t + 128], start=t == 0, stop=t == T - 1)
            done(ins, "lg")
            pe.wait_ge(ld_l3, 16)
            project("h1.0", w_l3[:, 0, 0, :], XT[0])
            s = take(pe, "vt")
            pe.wait_ge(l3_val, 1)
            done(pe.transpose(s[:, 0:128], small[:, 0:128], ident), "vt")
            pe.wait_ge(gates_ready, 4)
            gate_columns("gt3", lambda t: G3[:, t, :])
            wait_read(pe, "gt3")
            for e in range(17):
                if e < 16:
                    if e > 0:
                        project(f"h1.{e}", w_l3[:, 0, e, :], XT[0])
                    wait_read(pe, f"h1.{e}")
                    project(f"h2.{e}", w_l3[:, 1, e, :], big[:, e % 2, :])
                    expand(f"E3.{e}", SEL_ONE + e, GT)
                if e >= 1:
                    wait_read(pe, f"E3.{e - 1}")
                    accumulate(big[:, 4 + (e - 1) % 2, :], w_l3[:, 2, e - 1, :], e == 1, e == 16)


def kernel(**inputs):
    import ml_dtypes
    import numpy as np
    import concourse.bacc as bacc
    from concourse.bass_utils import run_bass_kernel_spmd as run

    a = {k: np.asarray(v) for k, v in inputs.items()}
    f32 = np.float32
    arrays = {"x": a["x"], "ctx": a["ctx_1024"], "mask": a["mask_BxSxS2_ik0"]}
    order = [b + 8 * bb for b in range(8) for bb in range(2)]
    ctx = a["ctx_1024"][order]
    arrays["ctxT"] = ctx.transpose(2, 0, 1).reshape(P, TOK)
    heads = ctx.reshape(16, S, HP, 2, 8)
    arrays["ctxV"] = heads.transpose(3, 1, 0, 2, 4).reshape(P, 2 * T, HP, 8)
    partner1 = np.array([8 * (i // 8) + (i + 4) % 8 for i in range(P)])

    def pack(sizes, parts):
        for n, size in sizes.items():
            assert parts[n].shape[1] == size, (n, parts[n].shape)
        return np.concatenate([parts[n] for n in sizes], 1)

    def column(name):
        return a[name].reshape(P, 1)

    b_kv = a["L3_xattn_b_kv"].reshape(H, 2, 8)
    W_kv = a["L3_xattn_W_kv"].reshape(P, H, 2, 8)
    arrays["cols"] = pack(COLS, dict(
        ln_scale=column("L0_ffn_ln_scale"), ln_bias=column("L0_ffn_ln_bias"), attn_b=column("L0_ffn_attn_b"),
        b1_0=a["L0_ffn_b1"].reshape(8, 4, P).transpose(2, 0, 1).reshape(P, 32),
        b2_0=a["L0_ffn_b2"].T,
        bq1=column("L1_xattn_bq"), bq1p=column("L1_xattn_bq")[partner1],
        bk1=column("L1_xattn_bk"), bk1p=column("L1_xattn_bk")[partner1],
        bk3=b_kv[:, 0].reshape(P, 1), bq3=column("L3_xattn_b_q"),
        ln1_g=column("L2_ffn_ln1_g"), ln1_b=column("L2_ffn_ln1_b"),
        b1_2=a["L2_ffn_b1"].reshape(4, P).T, bg=np.tile(a["L3_ffn_bg"], 8).reshape(P, 1)))
    arrays["rows"] = pack(ROWS, {n: v.reshape(1, -1) for n, v in dict(
        next_b=a["L0_ffn_next_b"], bv1=a["L1_xattn_bv"], bo1=a["L1_xattn_bo"], ln1_gr=a["L2_ffn_ln1_g"],
        ln1_br=a["L2_ffn_ln1_b"], b2_2=a["L2_ffn_b2"], ln2_g=a["L2_ffn_ln2_g"], ln2_b=a["L2_ffn_ln2_b"],
        bv3=b_kv[:, 1], bo3=a["L3_xattn_b_o"], b1_3=a["L3_ffn_b1"], b2_3=a["L3_ffn_b2"],
        b3_3=a["L3_ffn_b3"]).items()})[0]
    wg_pad = np.zeros((P, 240), f32)
    wg_pad[:, 112:128] = a["L3_ffn_Wg"]
    wsel = np.stack([a["L2_ffn_Wsel_v"], a["L2_ffn_Wsel_o"]]).transpose(3, 0, 1, 2).reshape(P, 256)
    arrays["wb"] = pack(WB, dict(
        wq1=a["L1_xattn_Wq"].T, wq1p=a["L1_xattn_Wq"][partner1].T,
        wk1=a["L1_xattn_Wk"].T, wk1p=a["L1_xattn_Wk"][partner1].T,
        wv1=a["L1_xattn_Wv"].T, wo1=a["L1_xattn_Wo"].T,
        wk3=W_kv[:, :, 0].reshape(P, P), wv3=W_kv[:, :, 1].reshape(P, P),
        wq3=a["L3_xattn_W_q"], wo3=a["L3_xattn_W_o"], w_gate=a["L1_ffn_w_gate"].T, wsel=wsel,
        W1=a["L2_ffn_W1"], W2=a["L2_ffn_W2"].reshape(4, P, P).transpose(1, 0, 2).reshape(P, 512),
        wg_pad=wg_pad))
    arrays["w_l0"] = np.concatenate([
        a["L0_ffn_w1"].transpose(1, 0, 2).reshape(P, 4096),
        a["L0_ffn_w2"].reshape(8, 4, P, P).transpose(2, 0, 1, 3).reshape(P, 4096),
        a["L0_ffn_attn_w"].T, a["L0_ffn_next_w"].T], 1)
    arrays["w_l1"] = np.concatenate([
        a["L1_ffn_w1_e"].reshape(1024, P).T, a["L1_ffn_w1_s"].T,
        a["L1_ffn_w3_e"].reshape(1024, P).T, a["L1_ffn_w3_s"].T,
        a["L1_ffn_w2_e"].transpose(0, 2, 1).reshape(8, P, P).transpose(1, 0, 2).reshape(P, 1024),
        a["L1_ffn_w2_s"].T], 1)
    partner2 = np.array([(i + 16) % 32 if i < 32 else i for i in range(64)])
    q, k = a["L2_ffn_Wq"], a["L2_ffn_Wk"]
    four = np.stack([q, q[:, :, partner2], k, k[:, :, partner2]], 1)
    four = four.reshape(HP, 2, 4, P, 64).transpose(0, 3, 2, 1, 4).reshape(HP, P, 512)
    wv = a["L2_ffn_Wv"].reshape(HP, 2, E0, P, 64).transpose(0, 3, 1, 2, 4).reshape(HP, P, 1024)
    wo = a["L2_ffn_Wo"].reshape(HP, 2, E0, 64, P).transpose(0, 1, 3, 2, 4).reshape(HP, P, 1024)
    arrays["w_l2"] = np.concatenate([four, wv, wo], 2)
    arrays["w_l3"] = np.stack([a["L3_ffn_w1"], a["L3_ffn_w2"], a["L3_ffn_w3"]]).transpose(2, 0, 1, 3).reshape(P, L3W)

    d, s = np.arange(P), np.arange(S, dtype=f32)
    inv1 = (f32(1.0) / f32(10000.0) ** (np.arange(0, 8, 2, dtype=f32) / f32(8)))[d % 4]
    ang1 = (inv1[:, None] * s[None]).astype(f32)
    sign1 = np.where(d % 8 < 4, -1, 1)[:, None]
    inv2 = (f32(10000.0) ** (-np.arange(16, dtype=f32) / f32(16)))[d % 16]
    ang2 = (inv2[:, None] * s[None]).astype(f32)
    turned = (d % 64 < 32)[:, None]
    sign2 = np.where(d % 32 < 16, -1, 1)[:, None]
    lower = lambda n: np.tile(np.tri(n, n, -1).reshape(1, n * n), (P, 1))
    arrays["consts"] = pack(CONSTS, dict(
        ident=np.eye(P), cos1=np.cos(ang1), sin1=np.sin(ang1) * sign1,
        cos2=np.where(turned, np.cos(ang2), 1), sin2=np.where(turned, np.sin(ang2) * sign2, 0),
        lt4=lower(4), lt16=lower(16), prefer=np.tile(8 - np.arange(8), (P, 1)),
        headof=(d[:, None] // 8 == np.arange(H)[None]))).astype(f32)
    bmask = np.zeros((P, 320), f32)
    bmask[:, 0:64] = np.where(s[None] <= (d % 64)[:, None], 0, MASKED)
    bmask[:, 64:192] = np.where(d[None] // 64 == d[:, None] // 64, 0, MASKED)
    bmask[:, 192:320] = np.eye(P)
    arrays["bmask"] = bmask.astype(ml_dtypes.bfloat16)
    sel = np.zeros((96, NSEL, P), f32)
    for part in range(3):
        for half in range(2):
            to = slice(64 * half, 64 * half + 64)
            for e in range(8):
                for odd in range(2):
                    sel[48 * odd + 16 * part + 8 * half + e, SEL_PAIR + 8 * odd + e, to] = 1
                sel[16 * part + 2 * e + half, SEL_DUO + e, to] = 1
        for e in range(16):
            sel[16 * part + e, SEL_ONE + e, :] = 1
    arrays["sel"] = sel.astype(ml_dtypes.bfloat16)

    nc = bacc.Bacc("TRN2", target_bir_lowering=False, num_devices=1)
    io = {}
    for name in arrays:
        arrays[name] = np.ascontiguousarray(arrays[name])
        io[name] = nc.dram_tensor(f"in_{name}", arrays[name].shape, mybir.dt.from_np(arrays[name].dtype),
                                  kind="ExternalInput").ap()
    io["y"] = nc.dram_tensor("out_y", (16, S, P), F32, kind="ExternalOutput").ap()
    build(nc, io)
    r = run(nc, [{f"in_{name}": v for name, v in arrays.items()}], core_ids=[0])
    return r.results[0]["out_y"]
```

```python
from contextlib import ExitStack

import concourse.bass as bass
from concourse import mybir

F32 = mybir.dt.float32
BF16 = mybir.dt.bfloat16
F32R = mybir.dt.float32r
I32 = mybir.dt.int32
ALU = mybir.AluOpType
ACT = mybir.ActivationFunctionType
AX = mybir.AxisListType

P = 128
T = 8
S = 64
TOK = 1024
H = 16
HP = H // 2
E0 = 8
EPS = 1e-5
MASKED = -1.0e30
HIDDEN = -1.0e20 * 8.0 ** 0.5

COLS = dict(ln_scale=1, ln_bias=1, attn_b=1, b1_0=32, b2_0=8, bq1=1, bq1p=1, bk1=1, bk1p=1,
            bk3=1, bq3=1, ln1_g=1, ln1_b=1, b1_2=4, bg=1)
ROWS = dict(next_b=128, bv1=128, bo1=128, ln1_gr=128, ln1_br=128, b2_2=128, ln2_g=128, ln2_b=128,
            bv3=128, bo3=128, b1_3=16, b2_3=16, b3_3=16)
CONSTS = dict(ident=128, cos1=64, sin1=64, cos2=64, sin2=64, lt4=16, prefer=8, headof=16)
WB = dict(wq1=128, wq1p=128, wk1=128, wk1p=128, wv1=128, wo1=128, wk3=128, wv3=128, wq3=128, wo3=128,
          w_gate=16, wsel=256, W1=512, W2=512, wg_pad=240)
SEL_PAIR, SEL_DUO, SEL_ONE, NSEL = 0, 16, 24, 40


def offsets(sizes):
    at, out = 0, {}
    for name, n in sizes.items():
        out[name] = (at, n)
        at += n
    return out, at


COL_AT, NCOL = offsets(COLS)
ROW_AT, NROW = offsets(ROWS)
CONST_AT, NCONST = offsets(CONSTS)
WB_AT, NWB = offsets(WB)

L0W = 2 * 4096 + 2 * 128
L1W = 3 * 9 * 128
L2W = 512 + 1024 + 1024
L3W = 3 * 16 * 128
L1_AT = 2 * L2W
L1_LAG = 2
TOP2_AT = [[0], [1], [2], [3], [4, 5], [], [], [6]]
L3_LAG = 3
STAGE = max(L0W, L1_AT + L1W, L3W)

ATT = {0: 0, 1: 1, 3: 2}
LN_ROWS = [0, 1, 0, 1, 0, 1, 0, 1, 1, 0, 1]
COLUMNS_OF = [0, 2, 3, 4, 5, 6, 7, 9, 10]

ACC_COUNT = {}
_n = 0
for _name, _k in (("att0", T), ("eo", T), ("att1", T), ("l1", 9), ("l2", 64), ("ff", 2), ("att3", T), ("l3", 16)):
    ACC_COUNT[_name] = _n
    _n += _k


def psum_plan():
    jobs = []

    def job(name, banks=2, reads=2):
        jobs.append((name, banks, reads))

    def attention(i):
        for t in range(T + 1):
            if t < T:
                job(f"s{i}.{t}", 2, 1)
            if t >= 1:
                job(f"p{i}.{t - 1}")

    job("x.0")
    attention(0)
    job("k1a")
    job("k1b")
    job("x.1")
    job("xa")
    for t in range(T):
        job(f"h.{t}", 1, 1)
    job("nx")
    job("v1.0", 2, 4)
    job("v1.1", 2, 4)
    job("x.2")
    job("qa")
    job("qb")
    attention(1)
    job("ot1")
    job("out1")
    job("x.3")
    job("rt", 1, 1)
    for c in range(9 + L1_LAG):
        if c < 9:
            job(f"G.{c}")
            job(f"U.{c}", 2, 1)
        if c == L1_LAG:
            job("gt1", 1, 1)
        if L1_LAG <= c < 8 + L1_LAG:
            job(f"E1.{c - L1_LAG}", 2, 1)
    job("x.4")
    job("s2", 2, 1)
    job("p2")
    job("o2")
    job("x.5")
    job("gs.0", 2, 1)
    job("gs.1", 2, 1)
    for m in "qk":
        for n in "ab":
            job(f"{m}{n}.0", 2, 1)
    job("s.0", 2, 1)
    for t in range(T):
        job(f"y.0.{t}", 2, 1)
    job("pt.0")
    job("gt2.0", 1, 1)
    job("o.0")
    for hp in range(HP):
        for k in range(E0):
            job(f"E2.{hp}.{k}", 2, 1)
            if hp < HP - 1:
                if k < 2:
                    job(f"{'qk'[k]}a.{hp + 1}", 2, 1)
                    job(f"{'qk'[k]}b.{hp + 1}", 2, 1)
                job(f"y.{hp + 1}.{k}", 2, 1)
                if k == 4:
                    job(f"s.{hp + 1}", 2, 1)
        if hp < HP - 1:
            job(f"pt.{hp + 1}")
            if hp % 2 == 1:
                job(f"gt2.{(hp + 1) // 2}", 1, 1)
            job(f"o.{hp + 1}")
    job("k3")
    job("v3.0", 2, 4)
    job("v3.1", 2, 4)
    job("x.6")
    for c in range(4):
        job(f"f.{c}", 2, 1)
    job("x.7")
    job("q3")
    attention(3)
    job("ot3")
    job("out3")
    job("x.8")
    job("lg", 1, 1)
    job("h1.0", 2, 1)
    for e in range(16 + L3_LAG):
        if e < 15:
            job(f"h1.{e + 1}", 2, 1)
        if e < 16:
            job(f"h2.{e}", 2, 1)
        if e == L3_LAG:
            job("vt", 1, 1)
            job("gt3", 1, 1)
        if e >= L3_LAG:
            job(f"E3.{e - L3_LAG}", 2, 1)
    return jobs


def build(nc, io):
    with ExitStack() as ctx:
        def sb(name, shape, dt=F32):
            return ctx.enter_context(nc.sbuf_tensor(name, shape, dt))

        def sb_twice(name, shape, count=1):
            with ExitStack() as scope:
                plain = [scope.enter_context(nc.sbuf_tensor(f"{name}{i}", shape, F32)) for i in range(count)]
            rounded = [sb(f"{name}{i}_r", shape, F32R) for i in range(count)]
            return plain, rounded

        def sem(name):
            return ctx.enter_context(nc.semaphore(name))

        X = sb("X", [P, T, P])
        XN, XN_r = sb_twice("XN", [P, T, P], 2)
        XT, XT_r = sb_twice("XT", [P, TOK], 2)
        ctxT = sb("ctxT_sb", [P, TOK])
        (ctxR,), (ctxR_r,) = sb_twice("ctxR_sb", [P, T, P])
        KX, KX_r = sb_twice("KX", [P, 2, H, S], 2)
        VX = [sb(f"VX{i}", [P, 2 * T, HP, 2, 9]) for i in range(2)]
        KT = sb("KT", [P, TOK])
        QT = sb("QT", [P, TOK])
        PB = sb("PB", [P, 3, TOK])
        PT, PT_r = sb_twice("PT", [P, TOK], 2)
        (ON,), (ON_r,) = sb_twice("ON", [P, T, P])
        (OC,), (OC_r,) = sb_twice("OC", [P, TOK])
        (stage,), (stage_r,) = sb_twice("stage", [P, STAGE])
        wb = sb("wb_sb", [P, NWB])
        cols = sb("cols_sb", [P, NCOL])
        rows = sb("rows_sb", [P, NROW])
        consts = sb("consts_sb", [P, NCONST])
        sel = sb("sel_sb", [96, NSEL, P], BF16)
        bmask = sb("bmask_sb", [P, 64 + 128 + 128], BF16)
        stats = sb("stats", [P, T, 6])
        meanvar = sb("meanvar", [P, T, 2])
        vareps = sb("vareps", [P, T])
        rstd = sb("rstd", [P, T])
        minus_half = sb("minus_half", [P, T])
        mx2 = sb("mx", [P, 2, 16])
        rsum2 = sb("rsum", [P, 2, 16])
        SC = sb("SC", [P, T, 16])
        small = sb("small", [P, 1024])
        G3 = sb("G3", [P, T, 96], BF16)
        GT = sb("GT", [96, TOK], BF16)
        GTh = sb("GTh", [96, 4, TOK], BF16)
        maskB = sb("maskB", [P, T, S], BF16)
        (big,), (big_r,) = sb_twice("big", [P, 6, TOK])
        psum = ctx.enter_context(nc.psum_tensor("psum", [P, 4, 1024], F32))
        ACC = psum[:, 3, :]
        mx, rsum = mx2[:, 0, :], rsum2[:, 0, :]

        def col(name, i=0, n=1):
            at = COL_AT[name][0]
            return cols[:, at + i:at + i + n]

        def row(name):
            at, n = ROW_AT[name]
            return rows[:, at:at + n]

        def const(name):
            at, n = CONST_AT[name]
            return consts[:, at:at + n]

        def weight(name):
            at, n = WB_AT[name]
            return wb[:, at:at + n]

        def half(x, p):
            return x[:, 512 * p:512 * p + 512]

        def over(x, n, at=1):
            shape = list(x.shape)
            shape.insert(at, n)
            return x.unsqueeze(at).broadcast_to(shape)

        ident = const("ident")
        causal = bmask[:, 0:64]
        blocks = bmask[:, 64:192]
        identb = bmask[:, 192:320]
        w1_0 = stage[:, 0:4096].rearrange("p (t n) -> p t n", t=T)
        w2_0 = stage[:, 4096:8192].rearrange("p (t c n) -> p t c n", t=T, c=4)
        attn_w = stage[:, 8192:8320]
        next_w = stage[:, 8320:8448]
        XAT = big[:, 5, :]
        SG = [QT[:, :], KT[:, :]]
        HID = [KX[i // 2][:, i % 2, :, :].rearrange("p h k -> p (h k)") for i in range(4)]
        X_hi, X_lo = PT_r[0][:, :], PT_r[1][:, :]
        w_l1_lo = stage_r[:, L1_AT:L1_AT + L1W].rearrange("p (m c n) -> p m c n", m=3, c=9)
        w_l1_hi = [big_r[:, 2 * m:2 * m + 2, :].rearrange("p a n -> p (a n)")[:, 0:9 * 128]
                   .rearrange("p (c n) -> p c n", c=9) for m in range(2)]
        w_l1 = stage[:, L1_AT:L1_AT + L1W].rearrange("p (m c n) -> p m c n", m=3, c=9)
        w_qkv = [stage[:, 1536 * i:1536 * (i + 1)] for i in range(2)]
        w_o = [stage[:, 3072 + 1024 * i:3072 + 1024 * (i + 1)] for i in range(2)]
        GVO = big[:, 0:2, :].rearrange("p a (t v g) -> p (a t) v g", t=4, v=2)
        YG = [big[:, 2, :], big[:, 3, :]]
        AT = [big[:, 4, :], big[:, 5, :]]
        ROTQ = XT[0][:, :]
        ROTK = ON[:, :, :].rearrange("p t n -> p (t n)")
        w_qkv_hi = [k[:, :, :, :].rearrange("p b h k -> p (b h k)")[:, 0:1536] for k in KX_r]
        w_qkv_lo = [stage_r[:, 1536 * i:1536 * (i + 1)] for i in range(2)]
        X2_hi = PT_r[1][:, :]
        X2_lo = ctxR_r[:, :, :].rearrange("p t n -> p (t n)")
        V2 = XN[1][:, :, :].rearrange("p t (j v) -> p t j v", j=2)
        w_l3 = stage[:, 0:L3W].rearrange("p (m e n) -> p m e n", m=3, e=16)
        w_l3_lo = stage_r[:, 0:L3W].rearrange("p (m e n) -> p m e n", m=3, e=16)
        w_l3_hi = [big_r[:, 2 * m:2 * m + 2, :].rearrange("p a (e n) -> p (a e) n", n=P) for m in range(2)]
        A1 = [PB[:, i, :] for i in range(2)]
        A1_hi = [XN_r[1][:, :, :].rearrange("p t n -> p (t n)"), OC_r[:, :]]
        A1_lo = [ON_r[:, :, :].rearrange("p t n -> p (t n)"), XT_r[1][:, :]]
        A2 = HID
        A3 = [big[:, 4 + i, :] for i in range(2)]
        ctxV = big[:, 0, :].rearrange("p (b h d) -> p b h d", b=2 * T, h=HP)
        maskI = big[:, 1, 0:512].bitcast(I32).rearrange("p (t k) -> p t k", t=T)

        ld_x = sem("ld_x")
        ld_small = sem("ld_small")
        ld_ctxT = sem("ld_ctxT")
        ld_ctxR = sem("ld_ctxR")
        ld_ctxV = sem("ld_ctxV")
        ld_rows = sem("ld_rows")
        ld_wb = sem("ld_wb")
        ld_sel = sem("ld_sel")
        ld_mask = sem("ld_mask")
        ld_l0 = sem("ld_l0")
        ld_l1 = sem("ld_l1")
        ld_qkv = [sem(f"ld_qkv{i}") for i in range(2)]
        ld_o = [sem(f"ld_o{i}") for i in range(2)]
        ld_l3 = sem("ld_l3")
        stored = sem("stored")
        cleared = sem("cleared")
        slot_full = [sem(f"slot_full{i}") for i in range(3)]
        slot_read = [sem(f"slot_read{i}") for i in range(3)]
        acc_full = sem("acc_full")
        acc_read = sem("acc_read")
        dve_step = sem("dve_step")
        pool_step = sem("pool_step")
        ln_var = sem("ln_var")
        ln_rstd = sem("ln_rstd")
        xn_ready = sem("xn_ready")
        kx_ready = sem("kx_ready")
        vx_ready = sem("vx_ready")
        k_ready = sem("k_ready")
        q_ready = sem("q_ready")
        at_exp = sem("at_exp")
        at_out = sem("at_out")
        x_added = sem("x_added")
        mask_ready = sem("mask_ready")
        nx_gelu = sem("nx_gelu")
        gates_ready = sem("gates_ready")
        ff_hi = sem("ff_hi")
        ff_lo = sem("ff_lo")
        a1_parts = sem("a1_parts")
        x2_hi = sem("x2_hi")
        x2_lo = sem("x2_lo")
        qkv_hi = sem("qkv_hi")
        qkv_lo = sem("qkv_lo")
        roped = sem("roped")
        v_ready = sem("v_ready")
        s_exp = sem("s_exp")
        s_recip = sem("s_recip")
        s_norm = sem("s_norm")
        y1_ready = sem("y1_ready")
        l3_shift = sem("l3_shift")
        l3_exp = sem("l3_exp")
        l3_val = sem("l3_val")
        x_final = sem("x_final")

        slot_of, full_before, read_before = {}, {}, {}
        filled, emptied = [0, 0, 0], [0, 0, 0]
        for n, (name, banks, reads) in enumerate(psum_plan()):
            s = n % 3
            slot_of[name], full_before[name], read_before[name] = s, filled[s], emptied[s]
            filled[s] += banks
            emptied[s] += reads

        def slot(name):
            return psum[:, slot_of[name], :]

        def take(pe, name):
            if read_before[name]:
                pe.wait_ge(slot_read[slot_of[name]], read_before[name])
            return slot(name)

        def full(name):
            return slot_full[slot_of[name]]

        def read(name):
            return slot_read[slot_of[name]]

        def wait_full(eng, name, banks=2):
            eng.wait_ge(slot_full[slot_of[name]], full_before[name] + banks)

        def wait_read(eng, name, reads=1):
            eng.wait_ge(slot_read[slot_of[name]], read_before[name] + reads)

        block = ctx.enter_context(nc.Block())

        @block.sync
        def _(sp):
            for bb in range(2):
                sp.dma_start(X[64 * bb:64 * bb + 64, :, :], io["x"][8 * bb:8 * bb + 8].rearrange("t s d -> s t d"))\
                    .then_inc(ld_x, 16)
            sp.dma_start(consts[:, :], io["consts"]).then_inc(ld_small, 16)
            sp.dma_start(bmask[:, :], io["bmask"]).then_inc(ld_small, 16)
            sp.dma_start(cols[:, :], io["cols"]).then_inc(ld_small, 16)
            sp.dma_start(wb[:, :], io["wb"]).then_inc(ld_wb, 16)
            sp.dma_start(sel[:, :, :], io["sel"]).then_inc(ld_sel, 16)
            wait_read(sp, "nx", 2)
            sp.dma_start(stage[:, L1_AT:L1_AT + L1W], io["w_l1"]).then_inc(ld_l1, 16)
            for hp in range(HP):
                if hp >= 2:
                    wait_full(sp, f"y.{hp - 2}.7")
                sp.dma_start(w_qkv[hp % 2], io["w_l2"][hp, :, 0:1536]).then_inc(ld_qkv[hp % 2], 16)
                if hp >= 2:
                    sp.wait_ge(acc_full, ACC_COUNT["l2"] + 8 * (hp - 1))
                sp.dma_start(w_o[hp % 2], io["w_l2"][hp, :, 1536:L2W]).then_inc(ld_o[hp % 2], 16)
            sp.wait_ge(acc_full, ACC_COUNT["l2"] + 64)
            sp.dma_start(stage[:, 0:L3W], io["w_l3"]).then_inc(ld_l3, 16)
            sp.wait_ge(x_final, 1)
            for bb in range(2):
                sp.dma_start(io["y"][8 * bb:8 * bb + 8].rearrange("t s d -> s t d"), X[64 * bb:64 * bb + 64, :, :])\
                    .then_inc(stored, 16)
            sp.wait_ge(stored, 32)

        @block.gpsimd
        def _(pool):
            steps = [0]

            def settle(ins):
                steps[0] += 1
                ins.then_inc(pool_step, 1)
                pool.wait_ge(pool_step, steps[0])

            def rsqrt(l):
                for p in range(2):
                    q = slice(4 * p, 4 * p + 4)
                    pool.wait_ge(ln_var, 2 * l + p + 1)
                    pool.tensor_tensor(rstd[:, q], vareps[:, q], minus_half[:, q], ALU.pow).then_inc(ln_rstd, 1)

            def add_row(l, name):
                pool.wait_ge(xn_ready, 2 * l + 2)
                pool.tensor_tensor(X[:, :, :], X[:, :, :], over(row(name), T), ALU.add).then_inc(x_added, 1)

            def keys(i, t):
                n = 8 * ATT[i] + t
                if t >= 2:
                    wait_full(pool, f"s{i}.{t - 2}")
                src = (ctxT if i == 0 else KT)[:, 128 * t:128 * t + 128].rearrange("p (b k) -> p b k", b=2)
                pool.tensor_tensor(KX[t % 2][:, :, :, :], over(src, H, 2),
                                   over(over(const("headof"), S, 2), 2, 1), ALU.mult).then_inc(kx_ready, 1)

            def attention_keys(i):
                for t in range(2, T):
                    keys(i, t)

            pool.memset(minus_half[:, :], -0.5).then_inc(cleared, 1)
            for v in VX:
                pool.memset(v[:, :, :, :, :], 0.0).then_inc(cleared, 1)
            pool.memset(G3[:, :, :], 0.0).then_inc(cleared, 1)
            pool.wait_ge(cleared, 4)
            for v in VX:
                for j in range(2):
                    pool.memset(v[64 * j:64 * j + 64, :, :, j, 8:9], 1.0).then_inc(cleared, 1)
            pool.wait_ge(cleared, 8)
            rsqrt(0)
            pool.wait_ge(ld_small, 48)
            pool.wait_ge(ld_ctxT, 16)
            keys(0, 0)
            keys(0, 1)
            attention_keys(0)
            rsqrt(1)
            rsqrt(2)
            for p in range(2):
                q = slice(4 * p, 4 * p + 4)
                pool.wait_ge(nx_gelu, p + 1)
                pool.tensor_tensor(X[:, q, :], X[:, q, :], ON[:, q, :], ALU.add).then_inc(x_added, 1)
            rsqrt(3)
            pool.wait_ge(k_ready, 2)
            keys(1, 0)
            keys(1, 1)
            pool.wait_ge(ld_rows, 16)
            add_row(3, "bo1")
            attention_keys(1)
            def split_qkv(hp):
                pool.wait_ge(qkv_hi, hp + 1)
                pool.tensor_tensor(w_qkv_lo[hp % 2], w_qkv[hp % 2], w_qkv_hi[hp % 2].bitcast(F32), ALU.subtract)\
                    .then_inc(qkv_lo, 1)

            rsqrt(4)
            rsqrt(5)
            split_qkv(0)
            split_qkv(1)
            rsqrt(6)
            add_row(6, "ln2_b")
            def rope2_sum(hp, m):
                wait_read(pool, f"{'qk'[m]}a.{hp}")
                wait_read(pool, f"{'qk'[m]}b.{hp}")
                dst, rot = (QT[:, :], ROTQ) if m == 0 else (KT[:, :], ROTK)
                pool.tensor_tensor(dst, dst, rot, ALU.add).then_inc(roped, 1)

            def mix_values(hp, t):
                wait_read(pool, f"y.{hp}.{t}")
                yb = YG[t % 2].rearrange("p (j e v) -> p j e v", j=2, e=E0)
                settle(pool.tensor_tensor(yb[:, :, 0:4, :], yb[:, :, 0:4, :], yb[:, :, 4:8, :], ALU.add))
                settle(pool.tensor_tensor(yb[:, :, 0:2, :], yb[:, :, 0:2, :], yb[:, :, 2:4, :], ALU.add))
                if t == 0 and hp >= 1:
                    wait_full(pool, f"o.{hp - 1}")
                pool.tensor_tensor(V2[:, t, :, :], yb[:, :, 0, :], yb[:, :, 1, :], ALU.add).then_inc(v_ready, 1)

            def divide(hp):
                pool.wait_ge(s_recip, hp + 1)
                pb = PB[:, hp % 2, :].rearrange("p (g k) -> p g k", g=16)
                pool.tensor_tensor(pb, pb, over(rsum2[:, hp % 2, :], 64, 2), ALU.mult).then_inc(s_norm, 1)

            rope2_sum(0, 0)
            rope2_sum(0, 1)
            for hp in range(HP):
                for k in range(T):
                    if hp >= 1 and k < 2:
                        rope2_sum(hp, k)
                    mix_values(hp, k)
                    if k == 3 and 1 <= hp < HP - 1:
                        split_qkv(hp + 1)
                    if k == 5:
                        divide(hp)
            rsqrt(7)
            pool.wait_ge(xn_ready, 16)
            settle(pool.tensor_tensor(XN[0][:, :, :], XN[1][:, :, :], over(row("ln1_gr"), T), ALU.mult))
            settle(pool.tensor_tensor(XN[0][:, :, :], XN[0][:, :, :], over(row("ln1_br"), T), ALU.add))
            pool.tensor_tensor(XN[0][:, :, :], XN[0][:, :, :], over(row("b2_2"), T), ALU.add).then_inc(y1_ready, 1)
            wait_read(pool, "k3", 2)
            keys(3, 0)
            keys(3, 1)
            rsqrt(8)
            rsqrt(9)
            add_row(9, "bo3")
            attention_keys(3)
            rsqrt(10)

        @block.scalar
        def _(act):
            act.dma_start(ctxT[:, :], io["ctxT"]).then_inc(ld_ctxT, 16)
            act.dma_start(ctxV, io["ctxV"]).then_inc(ld_ctxV, 16)
            act.dma_start(rows[:, :], io["rows"].partition_broadcast(P)).then_inc(ld_rows, 16)
            for bb in range(2):
                act.dma_start(maskI[64 * bb:64 * bb + 64, :, :],
                              io["mask"][8 * bb:8 * bb + 8].rearrange("t q k -> q t k")).then_inc(ld_mask, 16)
            act.dma_start(stage[:, 0:L0W], io["w_l0"]).then_inc(ld_l0, 16)
            for bb in range(2):
                act.dma_start(ctxR[64 * bb:64 * bb + 64, :, :],
                              io["ctx"][8 * bb:8 * bb + 8].rearrange("t s d -> s t d")).then_inc(ld_ctxR, 16)

            def columns(n, scale=None, bias=None):
                for p in range(2):
                    wait_full(act, f"x.{n}", p + 1)
                    out, src = half(XT[n % 2], p), half(slot(f"x.{n}"), p)
                    if scale is None:
                        act.activation(out, src, ACT.Copy).then_inc(read(f"x.{n}"), 1)
                    else:
                        act.activation(out, src, ACT.Identity, scale=scale, bias=bias).then_inc(read(f"x.{n}"), 1)

            def upper(dst, src):
                act.activation(dst, src, ACT.Copy).then_inc(ff_hi, 1)

            def attention(i, upper_parts=()):
                for t in range(T + 1):
                    if t == 3 and upper_parts:
                        act.wait_ge(ld_l1 if i == 1 else ld_l3, 16)
                    if upper_parts and 3 <= t < 3 + len(upper_parts):
                        upper(*upper_parts[t - 3])
                    if t < T:
                        wait_read(act, f"s{i}.{t}")
                        act.activation(PB[:, t % 3, :], PB[:, t % 3, :], ACT.Exp, scale=8.0 ** -0.5)\
                            .then_inc(at_exp, 1)
                    if t >= 1:
                        u = t - 1
                        if u >= 2:
                            act.wait_ge(acc_full, ACC_COUNT[f"att{i}"] + u - 1)
                        for p in range(2):
                            wait_full(act, f"p{i}.{u}", p + 1)
                            act.activation(half(PT[u % 2], p), half(slot(f"p{i}.{u}"), p), ACT.Copy)\
                                .then_inc(read(f"p{i}.{u}"), 1)

            def out_columns(i):
                for p in range(2):
                    wait_full(act, f"ot{i}", p + 1)
                    act.activation(half(OC, p), half(slot(f"ot{i}"), p), ACT.Copy).then_inc(read(f"ot{i}"), 1)

            def gate_columns(name, out):
                wait_full(act, name, 1)
                act.activation(out, slot(name)[0:96, 0:512].bitcast(BF16), ACT.Copy).then_inc(read(name), 1)

            columns(0)
            attention(0)
            act.wait_ge(ld_small, 48)
            columns(1, col("ln_scale"), col("ln_bias"))
            for p in range(2):
                wait_full(act, "xa", p + 1)
                act.activation(half(XAT, p), half(slot("xa"), p), ACT.Identity, bias=col("attn_b"))\
                    .then_inc(read("xa"), 1)
            act.wait_ge(vx_ready, 1)
            for t in range(T):
                wait_full(act, f"h.{t}", 1)
                if t >= 2:
                    act.wait_ge(acc_full, ACC_COUNT["eo"] + t - 1)
                for c in range(4):
                    f = slice(128 * c, 128 * c + 128)
                    ins = act.activation(big[:, 2 + t % 2, f], slot(f"h.{t}")[:, f], ACT.Gelu,
                                         bias=col("b1_0", 4 * t + c))
                ins.then_inc(read(f"h.{t}"), 1)
            for p in range(2):
                q = slice(4 * p, 4 * p + 4)
                wait_read(act, "nx", p + 1)
                act.activation(ON[:, q, :], ON[:, q, :], ACT.Gelu).then_inc(nx_gelu, 1)
            columns(2)
            attention(1, [(w_l1_hi[m], w_l1[:, m]) for m in range(2)])
            out_columns(1)
            def split_qkv(hp):
                act.wait_ge(ld_qkv[hp % 2], 16 * (hp // 2 + 1))
                act.activation(w_qkv_hi[hp % 2], w_qkv[hp % 2], ACT.Copy).then_inc(qkv_hi, 1)

            columns(3)
            wait_read(act, "x.3", 2)
            upper(X_hi, XT[1][:, :])
            wait_full(act, "rt", 1)
            act.activation(SC[:, :, :], slot("rt")[:, 0:128].rearrange("p (t e) -> p t e", t=T),
                           ACT.Sigmoid).then_inc(read("rt"), 1)
            for c in range(9):
                if c >= 2:
                    wait_read(act, f"U.{c - 2}")
                for p in range(2):
                    wait_full(act, f"G.{c}", p + 1)
                    act.activation(half(SG[c % 2], p), half(slot(f"G.{c}"), p), ACT.Silu)\
                        .then_inc(read(f"G.{c}"), 1)
                if c == L1_LAG:
                    gate_columns("gt1", GT[:, :])
            columns(4)
            split_qkv(0)
            wait_read(act, "s2")
            act.activation(PB[:, 0, :], PB[:, 0, :], ACT.Exp, scale=128.0 ** -0.5).then_inc(at_exp, 1)
            split_qkv(1)
            for p in range(2):
                wait_full(act, "p2", p + 1)
                act.activation(half(PT[0], p), half(slot("p2"), p), ACT.Copy).then_inc(read("p2"), 1)
            columns(5)
            wait_read(act, "x.5", 2)
            act.activation(X2_hi, XT[1][:, :], ACT.Copy).then_inc(x2_hi, 1)
            for g in range(2):
                wait_full(act, f"gs.{g}")
                act.activation(big[:, g, :], slot(f"gs.{g}"), ACT.Sigmoid).then_inc(read(f"gs.{g}"), 1)
            def numerators(hp):
                wait_read(act, f"s.{hp}")
                act.activation(PB[:, hp % 2, :], PB[:, hp % 2, :], ACT.Exp, scale=64.0 ** -0.5).then_inc(s_exp, 1)

            numerators(0)
            for hp in range(HP):
                for p in range(2):
                    wait_full(act, f"pt.{hp}", p + 1)
                    act.activation(half(PT[0], p), half(slot(f"pt.{hp}"), p), ACT.Copy).then_inc(read(f"pt.{hp}"), 1)
                if hp % 2 == 0:
                    gate_columns(f"gt2.{hp // 2}", GTh[:, hp // 2, :])
                if hp >= 1:
                    wait_read(act, f"E2.{hp - 1}.7")
                for b in range(2):
                    wait_full(act, f"o.{hp}", b + 1)
                    act.activation(OC[:, :].rearrange("p (t b q) -> p t b q", t=T, b=2)[:, :, b, :],
                                   half(slot(f"o.{hp}"), b).rearrange("p (t q) -> p t q", t=T), ACT.Copy)\
                        .then_inc(read(f"o.{hp}"), 1)
                if hp < HP - 2:
                    split_qkv(hp + 2)
                if hp < HP - 1:
                    numerators(hp + 1)
            for p in range(2):
                wait_full(act, "k3", p + 1)
                act.activation(half(KT, p), half(slot("k3"), p), ACT.Identity, bias=col("bk3"))\
                    .then_inc(read("k3"), 1)
            columns(6, col("ln1_g"), col("ln1_b"))
            for c in range(4):
                wait_full(act, f"f.{c}")
                act.activation(big[:, c, :], slot(f"f.{c}"), ACT.Relu, bias=col("b1_2", c)).then_inc(read(f"f.{c}"), 1)
            columns(7)
            for p in range(2):
                wait_full(act, "q3", p + 1)
                act.activation(half(QT, p), half(slot("q3"), p), ACT.Identity, bias=col("bq3"))\
                    .then_inc(read("q3"), 1)
            attention(3, [(w_l3_hi[m][:, 8 * n:8 * n + 8, :], w_l3[:, m, 8 * n:8 * n + 8, :])
                          for m in range(2) for n in range(2)])
            out_columns(3)
            columns(8)
            wait_read(act, "x.8", 2)
            upper(X_hi, XT[0][:, :])

            def relu(m, e):
                name = f"h{m}.{e}"
                wait_full(act, name)
                if m == 1 and e >= 2:
                    act.wait_ge(a1_parts, e - 1)
                if m == 2 and e >= 4:
                    wait_read(act, f"E3.{e - 4}")
                act.activation(A1[e % 2] if m == 1 else A2[e % 4], slot(name), ACT.Relu,
                               bias=row(f"b{m}_3")[:, e:e + 1]).then_inc(read(name), 1)

            act.wait_ge(l3_shift, 1)
            act.activation(small[:, 0:128], small[:, 0:128], ACT.Exp).then_inc(l3_exp, 1)
            relu(1, 0)
            for e in range(16):
                if e < 15:
                    relu(1, e + 1)
                relu(2, e)
                if e == L3_LAG:
                    gate_columns("gt3", GT[:, :])

        @block.vector
        def _(dve):
            steps = [0]

            def settle(ins):
                steps[0] += 1
                ins.then_inc(dve_step, 1)
                dve.wait_ge(dve_step, steps[0])

            def norm(l, src, wait=None):
                dst = XN[LN_ROWS[l]]
                for p in range(2):
                    q = slice(4 * p, 4 * p + 4)
                    for t in range(4 * p, 4 * p + 4):
                        if wait is not None:
                            wait(t)
                        ins = dve.bn_stats(stats[:, t, :], src[:, t, :])
                    settle(ins)
                    for t in range(4 * p, 4 * p + 4):
                        ins = dve.bn_aggr(meanvar[:, t, :], stats[:, t, :])
                    settle(ins)
                    dve.tensor_scalar(vareps[:, q], meanvar[:, q, 1], EPS, None, ALU.add).then_inc(ln_var, 1)
                for p in range(2):
                    dve.wait_ge(ln_rstd, 2 * l + p + 1)
                    for t in range(4 * p, 4 * p + 4):
                        ins = dve.tensor_scalar(dst[:, t, :], src[:, t, :], meanvar[:, t, 0:1], rstd[:, t:t + 1],
                                                ALU.subtract, ALU.mult)
                    ins.then_inc(xn_ready, 1)
                dve.wait_ge(xn_ready, 2 * l + 2)

            def lower(dst, src, hi, n):
                dve.wait_ge(ff_hi, n)
                dve.tensor_tensor(dst, src, hi.bitcast(F32), ALU.subtract).then_inc(ff_lo, 1)

            def attention(i, lower_parts=()):
                for t in range(T + 2):
                    if lower_parts and 4 <= t < 4 + len(lower_parts):
                        lower(*lower_parts[t - 4])
                    if t < T:
                        name = f"s{i}.{t}"
                        wait_full(dve, name)
                        if t >= 3:
                            wait_full(dve, f"p{i}.{t - 3}")
                        sc = slot(name).rearrange("p (h k) -> p h k", h=H)
                        m = mx2[:, t % 2, :]
                        settle(dve.tensor_reduce(m, sc, AX.X, ALU.max))
                        dve.tensor_tensor(PB[:, t % 3, :].rearrange("p (h k) -> p h k", h=H), sc,
                                          over(m, S, 2), ALU.subtract).then_inc(read(name), 1)
                    if t >= 2:
                        u = t - 2
                        dve.wait_ge(acc_full, ACC_COUNT[f"att{i}"] + u + 1)
                        o = ACC[:, 512 * (u % 2):512 * (u % 2) + 144].rearrange("p (h d) -> p h d", h=H)
                        r = rsum2[:, u % 2, :]
                        settle(dve.reciprocal(r, o[:, :, 8]))
                        dve.tensor_tensor(ON[:, u, :].rearrange("p (h d) -> p h d", h=H), o[:, :, 0:8],
                                          over(r, 8, 2), ALU.mult).then_inc(at_out, 1)
                        if i == 0:
                            dve.wait_ge(at_out, u + 1)
                            ins = dve.tensor_tensor(X[:, u, :], X[:, u, :], ON[:, u, :], ALU.add)
                if i == 0:
                    settle(ins)

            def values(i, bias, v):
                for n in range(2):
                    name = f"v{i}.{n}"
                    for m in range(2):
                        wait_full(dve, name, m + 1)
                        for j in range(2):
                            rows_j = slice(64 * j, 64 * j + 64)
                            dve.tensor_tensor(
                                VX[v][rows_j, 8 * n + 4 * m:8 * n + 4 * m + 4, :, j, 0:8],
                                half(slot(name), m)[rows_j].rearrange("p (b h j d) -> p b h j d", b=4, h=HP, j=2)[:, :, :, j, :],
                                over(bias[rows_j].rearrange("p (h j d) -> p h j d", h=HP, j=2)[:, :, j, :], 4),
                                ALU.add).then_inc(read(name), 1)

            def rope1(a, b, bias_a, bias_b, out, done):
                for p in range(2):
                    wait_full(dve, a, p + 1)
                    v = lambda x: half(x, p).rearrange("p (b k) -> p b k", k=S)
                    dve.scalar_tensor_tensor(out=v(out), in0=v(slot(a)), scalar=bias_a, in1=over(const("cos1"), 8),
                                             op0=ALU.add, op1=ALU.mult).then_inc(read(a), 1)
                    wait_full(dve, b, p + 1)
                    dve.scalar_tensor_tensor(out=v(PB[:, 0, :]), in0=v(slot(b)), scalar=bias_b,
                                             in1=over(const("sin1"), 8), op0=ALU.add, op1=ALU.mult)\
                        .then_inc(read(b), 1)
                    wait_read(dve, b, p + 1)
                    dve.tensor_tensor(half(out, p), half(out, p), half(PB[:, 0, :], p), ALU.add).then_inc(done, 1)

            def add_out(name):
                for p in range(2):
                    q = slice(4 * p, 4 * p + 4)
                    wait_full(dve, name, p + 1)
                    dve.tensor_tensor(X[:, q, :], X[:, q, :], half(slot(name), p).rearrange("p (t n) -> p t n", t=4),
                                      ALU.add).then_inc(read(name), 1)
                wait_read(dve, name, 2)

            def three_parts(gates, dst, n, rest):
                settle(dve.tensor_copy(dst(0), gates))
                settle(dve.tensor_tensor(rest, gates, dst(0), ALU.subtract))
                settle(dve.tensor_copy(dst(1), rest))
                settle(dve.tensor_tensor(rest, rest, dst(1), ALU.subtract))
                dve.tensor_copy(dst(2), rest).then_inc(gates_ready, 1)

            def ranks(v, n, lt, work, work2, out):
                a, b = over(v, n, 2), over(v, n, 3)
                settle(dve.tensor_tensor(work, a, b, ALU.is_equal))
                settle(dve.tensor_tensor(work, work, over(lt, T), ALU.mult))
                settle(dve.tensor_tensor(work2, a, b, ALU.is_gt))
                settle(dve.tensor_tensor(work, work, work2, ALU.add))
                settle(dve.tensor_reduce(out, work, AX.X, ALU.add))

            dve.wait_ge(ld_x, 32)
            norm(0, X)
            dve.wait_ge(ld_ctxV, 16)
            dve.wait_ge(cleared, 8)
            for j in range(2):
                r = slice(64 * j, 64 * j + 64)
                ins = dve.tensor_copy(VX[0][r, :, :, j, 0:8], ctxV[r])
            ins.then_inc(vx_ready, 1)
            attention(0)
            norm(1, X, None)
            norm(2, XN[1])
            dve.wait_ge(ld_small, 48)
            rope1("k1a", "k1b", col("bk1"), col("bk1p"), KT, k_ready)
            dve.wait_ge(ld_rows, 16)
            dve.wait_ge(ld_mask, 32)
            dve.tensor_scalar(maskB[:, :, :], maskI, 0.0, HIDDEN, ALU.is_equal, ALU.mult).then_inc(mask_ready, 1)
            for p in range(2):
                dve.wait_ge(acc_full, ACC_COUNT["eo"] + 4 * p + 4)
                dve.tensor_tensor(half(OC, p).rearrange("p (t n) -> p t n", t=4),
                                  half(ACC, p).rearrange("p (t n) -> p t n", t=4),
                                  over(col("b2_0", 4 * p, 4), P, 2), ALU.add).then_inc(acc_read, 1)
            for p in range(2):
                q = slice(4 * p, 4 * p + 4)
                wait_full(dve, "nx", p + 1)
                dve.tensor_tensor(ON[:, q, :], half(slot("nx"), p).rearrange("p (t n) -> p t n", t=4),
                                  over(row("next_b"), 4), ALU.add).then_inc(read("nx"), 1)
            norm(3, X, lambda t: dve.wait_ge(x_added, t // 4 + 1))
            values(1, row("bv1"), 1)
            rope1("qa", "qb", col("bq1"), col("bq1p"), QT, q_ready)
            attention(1, [(w_l1_lo[:, m], w_l1[:, m], w_l1_hi[m], m + 1) for m in range(2)])
            dve.wait_ge(x_added, 3)
            add_out("out1")
            norm(4, X)
            lower(X_lo, XT[1][:, :], X_hi, 3)
            wait_read(dve, "rt")
            s4 = SC[:, :, :].rearrange("p t (g e) -> p (t g) e", g=4)
            pairs = small[:, 0:192].rearrange("p (g n) -> p g n", n=6)
            gsum = small[:, 192:224].rearrange("p (t g) -> p t g", t=T)
            grank = small[:, 224:256].rearrange("p (t g) -> p t g", t=T)
            masked = small[:, 256:384].rearrange("p (t e) -> p t e", t=T)
            gates = small[:, 384:512].rearrange("p (t e) -> p t e", t=T)
            best4 = small[:, 520:584].rearrange("p (t n) -> p t n", t=T)
            wsum = small[:, 512:520]
            rest = small[:, 640:768].rearrange("p (t e) -> p t e", t=T)
            w4 = [small[:, 768 + 128 * i:896 + 128 * i].rearrange("p (t a b) -> p t a b", t=T, a=4) for i in range(2)]
            def hidden(c):
                wait_read(dve, f"G.{c}", 2)
                wait_full(dve, f"U.{c}")
                if c >= 4:
                    dve.wait_ge(acc_full, ACC_COUNT["l1"] + c - 3)
                dve.tensor_tensor(HID[c % 4], SG[c % 2], slot(f"U.{c}"), ALU.mult).then_inc(read(f"U.{c}"), 1)

            def gated(c):
                wait_full(dve, f"E1.{c}")
                wait_read(dve, f"U.{c}")
                dve.tensor_tensor(HID[c % 4], HID[c % 4], slot(f"E1.{c}"), ALU.mult)\
                    .then_inc(read(f"E1.{c}"), 1)

            dve.tensor_tensor(pairs[:, :, 0:3], s4[:, :, 0:3], s4[:, :, 1:4], ALU.add)
            dve.tensor_tensor(pairs[:, :, 3:5], s4[:, :, 0:2], s4[:, :, 2:4], ALU.add)
            settle(dve.tensor_tensor(pairs[:, :, 5:6], s4[:, :, 0:1], s4[:, :, 3:4], ALU.add))
            settle(dve.tensor_reduce(small[:, 192:224], pairs, AX.X, ALU.max))
            ranks(gsum, 4, const("lt4").rearrange("p (a b) -> p a b", a=4), w4[0], w4[1], grank)
            settle(dve.tensor_scalar(grank, grank, 2.0, 2.0, ALU.is_lt, ALU.mult))
            settle(dve.tensor_scalar(grank, grank, -2.0, None, ALU.add))
            settle(dve.tensor_tensor(masked.rearrange("p t (g e) -> p (t g) e", g=4), s4,
                                     over(small[:, 224:256], 4, 2), ALU.add))
            hidden(0)
            for t in range(T):
                ins = dve.max(best4[:, t, :], masked[:, t, :])
            settle(ins)
            settle(dve.memset(best4[:, :, 4:8], 9.0))
            for t in range(T):
                ins = dve.match_replace(gates[:, t, :], best4[:, t, :], masked[:, t, :], -9.0)
            settle(ins)
            settle(dve.scalar_tensor_tensor(out=gates, in0=gates, scalar=-5.0, in1=SC[:, :, :],
                                            op0=ALU.is_lt, op1=ALU.mult))
            settle(dve.tensor_reduce(wsum, gates, AX.X, ALU.add))
            settle(dve.tensor_scalar(wsum, wsum, 1e-6, None, ALU.add))
            settle(dve.reciprocal(wsum, wsum))
            settle(dve.tensor_tensor(gates, gates, over(wsum, 16, 2), ALU.mult))
            three_parts(gates, lambda i: G3[:, :, 16 * i:16 * i + 16], 16, rest)
            for c in range(1, 9 + L1_LAG):
                if c < 9:
                    hidden(c)
                if L1_LAG <= c < 8 + L1_LAG:
                    gated(c - L1_LAG)
            dve.wait_ge(acc_full, ACC_COUNT["l1"] + 9)
            settle(dve.tensor_tensor(X[:, :, :], X[:, :, :], ACC.rearrange("p (t n) -> p t n", t=T), ALU.add))
            norm(5, X)
            wait_full(dve, "s2")
            s2 = slot("s2").rearrange("p (t k) -> p t k", t=T)
            p2 = PB[:, 0, :].rearrange("p (t k) -> p t k", t=T)
            settle(dve.tensor_reduce(mx[:, 0:8], s2, AX.X, ALU.max))
            dve.tensor_tensor(p2, s2, over(mx[:, 0:8], P, 2), ALU.subtract).then_inc(read("s2"), 1)
            dve.wait_ge(at_exp, 17)
            settle(dve.tensor_reduce(rsum[:, 0:8], p2, AX.X, ALU.add))
            settle(dve.reciprocal(rsum[:, 0:8], rsum[:, 0:8]))
            for t in range(T):
                wait_full(dve, "o2", t // 4 + 1)
                ins = dve.scalar_tensor_tensor(out=X[:, t, :], in0=slot("o2")[:, 128 * t:128 * t + 128],
                                               scalar=rsum[:, t:t + 1], in1=X[:, t, :], op0=ALU.mult, op1=ALU.add)
                if t % 4 == 3:
                    ins.then_inc(read("o2"), 1)
            wait_read(dve, "o2", 2)
            norm(6, X)

            def rope2_product(hp, k):
                m, n = k // 2, k % 2
                name = f"{'qk'[m]}{'ab'[n]}.{hp}"
                wait_full(dve, name)
                if hp >= 1:
                    dve.wait_ge(roped, 2 * hp)
                dst = ((QT[:, :], ROTQ), (KT[:, :], ROTK))[m][n]
                v = lambda x: x.rearrange("p (b k) -> p b k", k=S)
                dve.tensor_tensor(v(dst), v(slot(name)), over(const(("cos2", "sin2")[n]), 16), ALU.mult)\
                    .then_inc(read(name), 1)

            tv = lambda x: x.rearrange("p (g j e) -> p g j e", g=2 * T, j=2)
            eq, first, left = (tv(small[:, 256 * i:256 * i + 256]) for i in range(3))
            best = small[:, 768:800].rearrange("p (g j) -> p g j", j=2)
            rest2 = small[:, 800:928].rearrange("p (t g) -> p t g", t=T)

            def top2(hp, part):
                s2 = GVO[:, :, :, 16 * hp:16 * hp + 16].rearrange("p t v (j e) -> p (t v) j e", j=2)
                src, out = (s2, first) if part < 3 else (left, eq)
                prefer = over(over(const("prefer"), 2), 2 * T)
                if part in (0, 3):
                    settle(dve.tensor_reduce(best, src, AX.X, ALU.max))
                    settle(dve.tensor_tensor(eq, src, over(best, E0, 3), ALU.is_equal))
                if part in (1, 4):
                    settle(dve.tensor_tensor(eq, eq, prefer, ALU.mult))
                    settle(dve.tensor_reduce(best, eq, AX.X, ALU.max))
                    settle(dve.tensor_tensor(out, eq, over(best, E0, 3), ALU.is_equal))
                if part == 2:
                    settle(dve.tensor_scalar(left, first, -4.0, None, ALU.mult))
                    settle(dve.tensor_tensor(left, left, s2, ALU.add))
                if part == 5:
                    settle(dve.tensor_tensor(eq, eq, first, ALU.add))
                    settle(dve.tensor_tensor(s2, s2, eq, ALU.mult))
                if part == 6:
                    if hp >= 2:
                        wait_full(dve, f"gt2.{hp // 2 - 1}", 1)
                    at = 48 * (hp % 2)
                    three_parts(GVO[:, :, 1, 16 * hp:16 * hp + 16],
                                lambda i: G3[:, :, at + 16 * i:at + 16 * i + 16], 16, rest2)

            def shifted(hp):
                name = f"s.{hp}"
                wait_full(dve, name)
                if hp >= 2:
                    wait_full(dve, f"pt.{hp - 2}")
                sc = slot(name).rearrange("p (g k) -> p g k", g=16)
                settle(dve.tensor_reduce(mx2[:, hp % 2, :], sc, AX.X, ALU.max))
                dve.tensor_tensor(PB[:, hp % 2, :].rearrange("p (g k) -> p g k", g=16), sc,
                                  over(mx2[:, hp % 2, :], S, 2), ALU.subtract).then_inc(read(name), 1)

            def reciprocals(hp):
                if hp >= 2:
                    dve.wait_ge(s_norm, hp - 1)
                dve.wait_ge(s_exp, hp + 1)
                r = rsum2[:, hp % 2, :]
                settle(dve.tensor_reduce(r, PB[:, hp % 2, :].rearrange("p (g k) -> p g k", g=16), AX.X, ALU.add))
                dve.reciprocal(r, r).then_inc(s_recip, 1)

            def gate_values(hp, t):
                name = f"y.{hp}.{t}"
                wait_full(dve, name)
                if hp * T + t >= 2:
                    dve.wait_ge(v_ready, hp * T + t - 1)
                dve.tensor_tensor(YG[t % 2].rearrange("p (g v) -> p g v", v=64),
                                  slot(name).rearrange("p (g v) -> p g v", v=64),
                                  over(GVO[:, t, 0, 16 * hp:16 * hp + 16], 64, 2), ALU.mult)\
                    .then_inc(read(name), 1)

            def gate_outputs(hp, e):
                n = 8 * hp + e
                name = f"E2.{hp}.{e}"
                wait_full(dve, name)
                if e == 0:
                    wait_read(dve, f"o.{hp}", 2)
                if n >= 2:
                    dve.wait_ge(acc_full, ACC_COUNT["l2"] + n - 1)
                dve.tensor_tensor(AT[e % 2], OC[:, :], slot(name), ALU.mult).then_inc(read(name), 1)

            dve.wait_ge(x2_hi, 1)
            dve.tensor_tensor(X2_lo, XT[1][:, :], X2_hi.bitcast(F32), ALU.subtract).then_inc(x2_lo, 1)
            for k in range(4):
                rope2_product(0, k)
            wait_read(dve, "gs.0")
            wait_read(dve, "gs.1")
            for part in range(6):
                top2(0, part)
            shifted(0)
            for t in range(T):
                gate_values(0, t)
                if t == 1:
                    reciprocals(0)
                top2(0 if t == 0 else 1, 6 if t == 0 else t - 1)
            for hp in range(HP):
                for k in range(E0):
                    gate_outputs(hp, k)
                    if hp < HP - 1:
                        if k < 2:
                            rope2_product(hp + 1, 2 * k)
                            rope2_product(hp + 1, 2 * k + 1)
                        gate_values(hp + 1, k)
                    if hp < HP - 2:
                        for part in TOP2_AT[k]:
                            top2(hp + 2, part)
                    if hp < HP - 1:
                        if k == 4:
                            shifted(hp + 1)
                        if k == 5:
                            reciprocals(hp + 1)
            dve.wait_ge(acc_full, ACC_COUNT["l2"] + 64)
            settle(dve.tensor_tensor(XN[0][:, :, :], XN[0][:, :, :], ACC.rearrange("p (t n) -> p t n", t=T), ALU.add))
            norm(7, XN[0])
            values(3, row("bv3"), 0)
            dve.wait_ge(y1_ready, 1)
            for p in range(2):
                q = slice(4 * p, 4 * p + 4)
                dve.wait_ge(acc_full, ACC_COUNT["ff"] + p + 1)
                ins = dve.tensor_tensor(XN[0][:, q, :], XN[0][:, q, :],
                                        half(ACC, p).rearrange("p (t n) -> p t n", t=4), ALU.add)
            settle(ins)
            norm(8, XN[0])
            settle(dve.tensor_tensor(XN[1][:, :, :], XN[1][:, :, :], over(row("ln2_g"), T), ALU.mult))
            dve.wait_ge(x_added, 4)
            settle(dve.tensor_tensor(X[:, :, :], X[:, :, :], XN[1][:, :, :], ALU.add))
            norm(9, X)
            attention(3, [(w_l3_lo[:, m, 8 * n:8 * n + 8, :], w_l3[:, m, 8 * n:8 * n + 8, :],
                           w_l3_hi[m][:, 8 * n:8 * n + 8, :], 4 + 2 * m + n) for m in range(2) for n in range(2)])
            dve.wait_ge(x_added, 5)
            add_out("out3")
            norm(10, X)
            logits = small[:, 0:128]
            by_batch = logits.rearrange("p (b k) -> p b k", b=2)
            work = small[:, 128:256]
            rowgate = small[:, 256:384].rearrange("p (t e) -> p t e", t=T)
            best8 = small[:, 384:400]
            outbias = small[:, 400:408]
            rest = small[:, 512:640].rearrange("p (t e) -> p t e", t=T)
            lower(X_lo, XT[0][:, :], X_hi, 8)
            wait_full(dve, "lg", 1)
            def first_parts(e):
                wait_read(dve, f"h1.{e}")
                if e >= 2:
                    wait_full(dve, f"h2.{e - 2}")
                settle(dve.tensor_copy(A1_hi[e % 2], A1[e % 2]))
                dve.tensor_tensor(A1_lo[e % 2], A1[e % 2], A1_hi[e % 2].bitcast(F32), ALU.subtract)\
                    .then_inc(a1_parts, 1)

            dve.tensor_scalar(logits, slot("lg")[:, 0:128], col("bg"), None, ALU.add).then_inc(read("lg"), 1)
            wait_read(dve, "lg")
            settle(dve.tensor_reduce(mx[:, 0:2], by_batch, AX.X, ALU.max))
            dve.tensor_tensor(by_batch, by_batch, over(mx[:, 0:2], S, 2), ALU.subtract).then_inc(l3_shift, 1)
            dve.wait_ge(l3_exp, 1)
            settle(dve.tensor_reduce(rsum[:, 0:2], by_batch, AX.X, ALU.add))
            settle(dve.reciprocal(rsum[:, 0:2], rsum[:, 0:2]))
            settle(dve.tensor_tensor(by_batch, by_batch, over(rsum[:, 0:2], S, 2), ALU.mult))
            settle(dve.tensor_copy(work, logits))
            first_parts(0)
            for k in range(4):
                for b in range(2):
                    ins = dve.max(best8[:, 8 * b:8 * b + 8], work[:, 64 * b:64 * b + 64])
                settle(ins)
                for b in range(2):
                    w = work[:, 64 * b:64 * b + 64]
                    ins = dve.match_replace(w, best8[:, 8 * b:8 * b + 8], w, -1.0)
                settle(ins)
                if k == 1:
                    first_parts(1)
            dve.scalar_tensor_tensor(out=logits, in0=work, scalar=0.0, in1=logits, op0=ALU.is_lt, op1=ALU.mult)\
                .then_inc(l3_val, 1)
            first_parts(2)
            first_parts(3)
            wait_full(dve, "vt", 1)
            dve.tensor_copy(small[:, 256:384], slot("vt")[:, 0:128]).then_inc(read("vt"), 1)
            wait_read(dve, "vt")
            three_parts(rowgate, lambda i: G3[:, :, 16 * i:16 * i + 16], 16, rest)
            dve.wait_ge(gates_ready, 10)
            settle(dve.tensor_tensor(rest, rowgate, over(row("b3_3"), T), ALU.mult))
            settle(dve.tensor_reduce(outbias, rest, AX.X, ALU.add))
            for e in range(16):
                if e + L3_LAG + 1 < 16:
                    first_parts(e + L3_LAG + 1)
                wait_read(dve, f"h2.{e}")
                wait_full(dve, f"E3.{e}")
                if e >= 2:
                    dve.wait_ge(acc_full, ACC_COUNT["l3"] + e - 1)
                dve.tensor_tensor(A3[e % 2], A2[e % 4], slot(f"E3.{e}"), ALU.mult)\
                    .then_inc(read(f"E3.{e}"), 1)
            dve.wait_ge(acc_full, ACC_COUNT["l3"] + 16)
            for t in range(T):
                ins = dve.scalar_tensor_tensor(out=X[:, t, :], in0=ACC[:, 128 * t:128 * t + 128],
                                               scalar=outbias[:, t:t + 1], in1=X[:, t, :], op0=ALU.add, op1=ALU.add)
            ins.then_inc(x_final, 1)

        @block.tensor
        def _(pe):
            def done(ins, name):
                ins.then_inc(full(name), 1)

            def rows_to_columns(n, src=None):
                l = COLUMNS_OF[n]
                name = f"x.{n}"
                s = take(pe, name)
                for t in range(T):
                    if t % 4 == 0:
                        pe.wait_ge(xn_ready, 2 * l + t // 4 + 1)
                    ins = pe.transpose(s[:, 128 * t:128 * t + 128], XN[LN_ROWS[l]][:, t, :], ident)
                    if t % 4 == 3:
                        done(ins, name)

            def project(name, w, x, wait=None):
                s = take(pe, name)
                for p in range(2):
                    if wait is not None:
                        wait(p)
                    done(pe.matmul(half(s, p), w, half(x, p), start=True, stop=True), name)

            def in_parts(out, w, x):
                pe.matmul(out, w[1], x[0], start=True, stop=True, skip_group_check=True)
                pe.matmul(out, w[0], x[1], start=False, stop=True, skip_group_check=True)
                return pe.matmul(out, w[0], x[0], start=False, stop=True, skip_group_check=True)

            def columns_of(parts, at, n):
                return [x[:, at:at + n] for x in parts]

            def project_parts(name, w, x):
                s = take(pe, name)
                for p in range(2):
                    done(in_parts(half(s, p), w, columns_of(x, 512 * p, 512)), name)

            def columns_there(n):
                return lambda p: wait_read(pe, f"x.{n}", p + 1)

            def project_rows(name, x, w, wait=None):
                s = take(pe, name)
                for t in range(T):
                    if wait is not None and t % 4 == 0:
                        wait(t // 4)
                    ins = pe.matmul(s[:, 128 * t:128 * t + 128], x[:, 128 * t:128 * t + 128], w,
                                    start=True, stop=True)
                    if t % 4 == 3:
                        done(ins, name)

            def project_values(i, w):
                for n in range(2):
                    name = f"v{i}.{n}"
                    s = take(pe, name)
                    for b in range(8):
                        tb = 8 * n + b
                        for j in range(2):
                            ins = pe.matmul(s[64 * j:64 * j + 64, 128 * b:128 * b + 128],
                                            ctxT[:, 64 * tb:64 * tb + 64], w, start=True, stop=True)
                        if b % 4 == 3:
                            done(ins, name)

            def attention(i, q, wait_q, mask, v):
                for t in range(T + 2):
                    if t < T:
                        name = f"s{i}.{t}"
                        wait_q(t // 4)
                        pe.wait_ge(kx_ready, 8 * ATT[i] + t + 1)
                        s = take(pe, name)
                        for n in range(2):
                            out = half(s, n)
                            if mask is not None:
                                pe.matmul(out, identb, over(mask(t), 8), start=True, stop=True)
                            for bb in range(2):
                                tok = 128 * t + 64 * bb
                                ins = pe.matmul(out[64 * bb:64 * bb + 64, :], q[:, tok:tok + 64],
                                                KX[t % 2][:, bb, 8 * n:8 * n + 8, :],
                                                start=mask is None, stop=True, skip_group_check=True)
                            done(ins, name)
                    if 1 <= t <= T:
                        u = t - 1
                        name = f"p{i}.{u}"
                        pe.wait_ge(at_exp, 8 * ATT[i] + u + 1 + (i == 3))
                        s = take(pe, name)
                        for hp in range(HP):
                            c = slice(128 * hp, 128 * hp + 128)
                            ins = pe.transpose(s[:, c], PB[:, u % 3, c], ident)
                            if hp % 4 == 3:
                                done(ins, name)
                    if t >= 2:
                        u = t - 2
                        if u == 0:
                            v[1]()
                        wait_read(pe, f"p{i}.{u}", 2)
                        if u >= 2:
                            pe.wait_ge(at_out, 8 * ATT[i] + u - 1)
                        for hp in range(HP):
                            for bb in range(2):
                                at = 512 * (u % 2) + 18 * hp
                                ins = pe.matmul(ACC[64 * bb:64 * bb + 64, at:at + 18],
                                                PT[u % 2][:, 128 * hp + 64 * bb:128 * hp + 64 * bb + 64],
                                                VX[v[0]][:, 2 * u + bb, hp, :, :], start=True, stop=True)
                        ins.then_inc(acc_full, 1)

            def attention_out(i, w):
                name = f"ot{i}"
                s = take(pe, name)
                pe.wait_ge(at_out, 8 * ATT[i] + 8)
                for t in range(T):
                    ins = pe.transpose(s[:, 128 * t:128 * t + 128], ON[:, t, :], ident)
                    if t % 4 == 3:
                        done(ins, name)
                project_rows(f"out{i}", OC, w, lambda p: wait_read(pe, name, p + 1))

            def gate_columns(name, src):
                s = take(pe, name)[0:96, 0:512].bitcast(BF16)
                for t in range(T):
                    ins = pe.transpose(s[:, 128 * t:128 * t + 128], src(t), identb)
                done(ins, name)

            def expand(name, k, gates):
                s = take(pe, name)
                for p in range(2):
                    done(pe.matmul(half(s, p), sel[:, k, :], half(gates, p), start=True, stop=True), name)

            def accumulate(x, w, first, last):
                for t in range(T):
                    ins = pe.matmul(ACC[:, 128 * t:128 * t + 128], x[:, 128 * t:128 * t + 128], w,
                                    start=first and t % 4 == 0, stop=True, skip_group_check=True)
                ins.then_inc(acc_full, 1)

            pe.wait_ge(ld_small, 48)
            rows_to_columns(0)
            attention(0, XT[0], lambda p: wait_read(pe, "x.0", p + 1), lambda t: causal,
                      (0, lambda: pe.wait_ge(vx_ready, 1)))
            pe.wait_ge(ld_wb, 16)
            pe.wait_ge(ld_ctxT, 16)
            project("k1a", weight("wk1"), ctxT)
            project("k1b", weight("wk1p"), ctxT)
            rows_to_columns(1)
            pe.wait_ge(ld_l0, 16)
            s = take(pe, "xa")
            for p in range(2):
                wait_read(pe, "x.1", p + 1)
                pe.wait_ge(xn_ready, 4)
                pe.matmul(half(s, p), attn_w, half(XT[1], p), start=True, stop=True, skip_group_check=True)
                for t in range(4 * p, 4 * p + 4):
                    ins = pe.matmul(s[:, 128 * t:128 * t + 128], XN[1][:, t, :], ident,
                                    start=False, stop=True, skip_group_check=True)
                done(ins, "xa")
            for t in range(T + 1):
                if t < T:
                    name = f"h.{t}"
                    s = take(pe, name)
                    wait_read(pe, "xa", t // 4 + 1)
                    for c in range(4):
                        ins = pe.matmul(s[:, 128 * c:128 * c + 128], w1_0[:, t, 128 * c:128 * c + 128],
                                        XAT[:, 128 * t:128 * t + 128], start=True, stop=True)
                    done(ins, name)
                if t >= 1:
                    u = t - 1
                    wait_read(pe, f"h.{u}")
                    for c in range(4):
                        ins = pe.matmul(ACC[:, 128 * u:128 * u + 128], w2_0[:, u, c, :],
                                        big[:, 2 + u % 2, 128 * c:128 * c + 128], start=c == 0, stop=c == 3)
                    ins.then_inc(acc_full, 1)
            project_rows("nx", OC, next_w, lambda p: pe.wait_ge(acc_read, p + 1))
            project_values(1, weight("wv1"))
            rows_to_columns(2)
            project("qa", weight("wq1"), XT[0], columns_there(2))
            project("qb", weight("wq1p"), XT[0])
            attention(1, QT, lambda p: pe.wait_ge(q_ready, p + 1), None, (1, lambda: wait_read(pe, "v1.1", 4)))
            attention_out(1, weight("wo1"))
            rows_to_columns(3)
            s = take(pe, "rt")
            wait_read(pe, "x.3", 2)
            for t in range(T):
                ins = pe.matmul(s[:, 16 * t:16 * t + 16], XT[1][:, 128 * t:128 * t + 128], weight("w_gate"),
                                start=True, stop=True)
            done(ins, "rt")
            pe.wait_ge(ff_lo, 3)
            pe.wait_ge(ld_sel, 16)
            for c in range(9 + L1_LAG + 1):
                if c < 9:
                    for m in range(2):
                        project_parts(f"{'GU'[m]}.{c}", (w_l1_hi[m][:, c, :], w_l1_lo[:, m, c, :]), (X_hi, X_lo))
                if c == L1_LAG:
                    pe.wait_ge(gates_ready, 1)
                    gate_columns("gt1", lambda t: G3[:, t, :])
                    wait_read(pe, "gt1")
                if L1_LAG <= c < 8 + L1_LAG:
                    expand(f"E1.{c - L1_LAG}", SEL_DUO + c - L1_LAG, GT)
                u = c - L1_LAG - 1
                if u >= 0:
                    wait_read(pe, f"E1.{u}" if u < 8 else "U.8")
                    accumulate(HID[u % 4], w_l1[:, 2, u, :], u == 0, u == 8)
            rows_to_columns(4)
            s = take(pe, "s2")
            for p in range(2):
                wait_read(pe, "x.4", p + 1)
                pe.matmul(half(s, p), identb, over(blocks, 4), start=True, stop=True, skip_group_check=True)
                for t in range(4 * p, 4 * p + 4):
                    c = slice(128 * t, 128 * t + 128)
                    ins = pe.matmul(s[:, c], XT[0][:, c], ctxT[:, c], start=False, stop=True,
                                    skip_group_check=True)
                done(ins, "s2")
            s = take(pe, "p2")
            pe.wait_ge(at_exp, 17)
            for t in range(T):
                c = slice(128 * t, 128 * t + 128)
                ins = pe.transpose(s[:, c], PB[:, 0, c], ident)
                if t % 4 == 3:
                    done(ins, "p2")
            s = take(pe, "o2")
            pe.wait_ge(ld_ctxR, 32)
            for t in range(T):
                if t % 4 == 0:
                    wait_read(pe, "p2", t // 4 + 1)
                c = slice(128 * t, 128 * t + 128)
                ins = pe.matmul(s[:, c], PT[0][:, c], ctxR[:, t, :], start=True, stop=True)
                if t % 4 == 3:
                    done(ins, "o2")
            rows_to_columns(5)
            for g in range(2):
                s = take(pe, f"gs.{g}")
                wait_read(pe, "x.5", 2)
                for t in range(4):
                    ins = pe.matmul(s[:, 256 * t:256 * t + 256],
                                    XT[1][:, 128 * (4 * g + t):128 * (4 * g + t) + 128], weight("wsel"),
                                    start=True, stop=True)
                    if t % 2 == 1:
                        done(ins, f"gs.{g}")

            def rope2_job(hp, k):
                project_parts(f"{'qk'[k // 2]}{'ab'[k % 2]}.{hp}",
                              columns_of((w_qkv_hi[hp % 2], w_qkv_lo[hp % 2]), 128 * k, 128), (X2_hi, X2_lo))

            def scores2(hp):
                name = f"s.{hp}"
                s = take(pe, name)
                pe.wait_ge(roped, 2 * hp + 2)
                for t in range(T):
                    for b in range(2):
                        for j in range(2):
                            r, c = slice(64 * j, 64 * j + 64), slice(128 * t + 64 * b, 128 * t + 64 * b + 64)
                            ins = pe.matmul(s[r, c], QT[r, c], KT[r, c], start=True, stop=True)
                    if t % 4 == 3:
                        done(ins, name)

            def expert_values(hp, t):
                name = f"y.{hp}.{t}"
                s = take(pe, name)
                w = (w_qkv_hi[hp % 2], w_qkv_lo[hp % 2])
                for j in range(2):
                    done(in_parts(half(s, j), columns_of((X2_hi, X2_lo), 128 * t, 128),
                                  columns_of(w, 512 + 512 * j, 512)), name)

            def turned_probabilities(hp):
                name = f"pt.{hp}"
                s = take(pe, name)
                pe.wait_ge(s_norm, hp + 1)
                for t in range(T):
                    c = slice(128 * t, 128 * t + 128)
                    ins = pe.transpose(s[:, c], PB[:, hp % 2, c], ident)
                    if t % 4 == 3:
                        done(ins, name)

            def outputs2(hp):
                name = f"o.{hp}"
                s = take(pe, name)
                wait_read(pe, f"pt.{hp}", 2)
                for t in range(T):
                    pe.wait_ge(v_ready, 8 * hp + t + 1)
                    for j in range(2):
                        for b in range(2):
                            r = slice(64 * b, 64 * b + 64)
                            ins = pe.matmul(s[64 * j:64 * j + 64, 512 * b + 64 * t:512 * b + 64 * t + 64],
                                            V2[r, t, j, :], PT[0][r, 128 * t + 64 * j:128 * t + 64 * j + 64],
                                            start=True, stop=True)
                            if t == T - 1 and j == 1:
                                done(ins, name)

            def output_gates(g):
                pe.wait_ge(gates_ready, 2 * g + 3)
                gate_columns(f"gt2.{g}", lambda t: G3[:, t, :])

            def project_out(hp, e):
                wait_read(pe, f"E2.{hp}.{e}")
                accumulate(AT[e % 2], w_o[hp % 2][:, 128 * e:128 * e + 128],
                           hp == 0 and e == 0, hp == HP - 1 and e == E0 - 1)

            pe.wait_ge(x2_lo, 1)
            pe.wait_ge(qkv_lo, 1)
            for k in range(4):
                rope2_job(0, k)
            scores2(0)
            for t in range(T):
                expert_values(0, t)
            turned_probabilities(0)
            output_gates(0)
            outputs2(0)
            for hp in range(HP):
                if hp < HP - 1:
                    pe.wait_ge(qkv_lo, hp + 2)
                pe.wait_ge(ld_o[hp % 2], 16 * (hp // 2 + 1))
                if hp % 2 == 0:
                    wait_read(pe, f"gt2.{hp // 2}")
                for k in range(E0):
                    expand(f"E2.{hp}.{k}", SEL_PAIR + 8 * (hp % 2) + k, GTh[:, hp // 2, :])
                    if hp < HP - 1:
                        if k < 2:
                            rope2_job(hp + 1, 2 * k)
                            rope2_job(hp + 1, 2 * k + 1)
                        expert_values(hp + 1, k)
                        if k == 7:
                            turned_probabilities(hp + 1)
                    if k >= 1:
                        project_out(hp, k - 1)
                    if hp < HP - 1 and k == 4:
                        scores2(hp + 1)
                project_out(hp, E0 - 1)
                if hp < HP - 1:
                    if hp % 2 == 1:
                        output_gates((hp + 1) // 2)
                    outputs2(hp + 1)
            project("k3", weight("wk3"), ctxT)
            project_values(3, weight("wv3"))
            rows_to_columns(6)
            for c in range(4):
                project(f"f.{c}", weight("W1")[:, 128 * c:128 * c + 128], XT[0], columns_there(6))
            for c in range(4):
                wait_read(pe, f"f.{c}")
            for t in range(T):
                for c in range(4):
                    ins = pe.matmul(ACC[:, 128 * t:128 * t + 128], big[:, c, 128 * t:128 * t + 128],
                                    weight("W2")[:, 128 * c:128 * c + 128], start=c == 0, stop=c == 3)
                if t % 4 == 3:
                    ins.then_inc(acc_full, 1)
            rows_to_columns(7)
            project("q3", weight("wq3"), XT[1], columns_there(7))
            pe.wait_ge(mask_ready, 1)
            attention(3, QT, lambda p: wait_read(pe, "q3", p + 1), lambda t: maskB[:, t, :],
                      (0, lambda: wait_read(pe, "v3.1", 4)))
            attention_out(3, weight("wo3"))
            rows_to_columns(8)
            s = take(pe, "lg")
            wait_read(pe, "x.8", 2)
            for t in range(T):
                ins = pe.matmul(s[:, 0:128], weight("wg_pad")[:, 112 - 16 * t:240 - 16 * t],
                                XT[0][:, 128 * t:128 * t + 128], start=t == 0, stop=t == T - 1)
            done(ins, "lg")
            pe.wait_ge(ff_lo, 8)
            w3 = lambda m, e: (w_l3_hi[m][:, e, :], w_l3_lo[:, m, e, :])
            project_parts("h1.0", w3(0, 0), (X_hi, X_lo))
            for e in range(16 + L3_LAG + 1):
                if e < 15:
                    project_parts(f"h1.{e + 1}", w3(0, e + 1), (X_hi, X_lo))
                if e < 16:
                    pe.wait_ge(a1_parts, e + 1)
                    project_parts(f"h2.{e}", w3(1, e), (A1_hi[e % 2], A1_lo[e % 2]))
                if e == L3_LAG:
                    s = take(pe, "vt")
                    pe.wait_ge(l3_val, 1)
                    done(pe.transpose(s[:, 0:128], small[:, 0:128], ident), "vt")
                    pe.wait_ge(gates_ready, 10)
                    gate_columns("gt3", lambda t: G3[:, t, :])
                    wait_read(pe, "gt3")
                if L3_LAG <= e < 16 + L3_LAG:
                    expand(f"E3.{e - L3_LAG}", SEL_ONE + e - L3_LAG, GT)
                u = e - L3_LAG - 1
                if u >= 0:
                    wait_read(pe, f"E3.{u}")
                    accumulate(A3[u % 2], w_l3[:, 2, u, :], u == 0, u == 15)


def kernel(**inputs):
    import ml_dtypes
    import numpy as np
    import concourse.bacc as bacc
    from concourse.bass_utils import run_bass_kernel_spmd as run

    a = {k: np.asarray(v) for k, v in inputs.items()}
    f32 = np.float32
    arrays = {"x": a["x"], "ctx": a["ctx_1024"], "mask": a["mask_BxSxS2_ik0"]}
    order = [b + 8 * bb for b in range(8) for bb in range(2)]
    ctx = a["ctx_1024"][order]
    arrays["ctxT"] = ctx.transpose(2, 0, 1).reshape(P, TOK)
    heads = ctx.reshape(16, S, HP, 2, 8)
    arrays["ctxV"] = heads.transpose(3, 1, 0, 2, 4).reshape(P, 2 * T, HP, 8)
    partner1 = np.array([8 * (i // 8) + (i + 4) % 8 for i in range(P)])

    def pack(sizes, parts):
        for n, size in sizes.items():
            assert parts[n].shape[1] == size, (n, parts[n].shape)
        return np.concatenate([parts[n] for n in sizes], 1)

    def column(name):
        return a[name].reshape(P, 1)

    b_kv = a["L3_xattn_b_kv"].reshape(H, 2, 8)
    W_kv = a["L3_xattn_W_kv"].reshape(P, H, 2, 8)
    arrays["cols"] = pack(COLS, dict(
        ln_scale=column("L0_ffn_ln_scale"), ln_bias=column("L0_ffn_ln_bias"), attn_b=column("L0_ffn_attn_b"),
        b1_0=a["L0_ffn_b1"].reshape(8, 4, P).transpose(2, 0, 1).reshape(P, 32),
        b2_0=a["L0_ffn_b2"].T,
        bq1=column("L1_xattn_bq"), bq1p=column("L1_xattn_bq")[partner1],
        bk1=column("L1_xattn_bk"), bk1p=column("L1_xattn_bk")[partner1],
        bk3=b_kv[:, 0].reshape(P, 1), bq3=column("L3_xattn_b_q"),
        ln1_g=column("L2_ffn_ln1_g"), ln1_b=column("L2_ffn_ln1_b"),
        b1_2=a["L2_ffn_b1"].reshape(4, P).T, bg=np.tile(a["L3_ffn_bg"], 8).reshape(P, 1)))
    arrays["rows"] = pack(ROWS, {n: v.reshape(1, -1) for n, v in dict(
        next_b=a["L0_ffn_next_b"], bv1=a["L1_xattn_bv"], bo1=a["L1_xattn_bo"], ln1_gr=a["L2_ffn_ln1_g"],
        ln1_br=a["L2_ffn_ln1_b"], b2_2=a["L2_ffn_b2"], ln2_g=a["L2_ffn_ln2_g"], ln2_b=a["L2_ffn_ln2_b"],
        bv3=b_kv[:, 1], bo3=a["L3_xattn_b_o"], b1_3=a["L3_ffn_b1"], b2_3=a["L3_ffn_b2"],
        b3_3=a["L3_ffn_b3"]).items()})[0]
    wg_pad = np.zeros((P, 240), f32)
    wg_pad[:, 112:128] = a["L3_ffn_Wg"]
    wsel = np.stack([a["L2_ffn_Wsel_v"], a["L2_ffn_Wsel_o"]]).transpose(3, 0, 1, 2).reshape(P, 256)
    arrays["wb"] = pack(WB, dict(
        wq1=a["L1_xattn_Wq"].T, wq1p=a["L1_xattn_Wq"][partner1].T,
        wk1=a["L1_xattn_Wk"].T, wk1p=a["L1_xattn_Wk"][partner1].T,
        wv1=a["L1_xattn_Wv"].T, wo1=a["L1_xattn_Wo"].T,
        wk3=W_kv[:, :, 0].reshape(P, P), wv3=W_kv[:, :, 1].reshape(P, P),
        wq3=a["L3_xattn_W_q"], wo3=a["L3_xattn_W_o"], w_gate=a["L1_ffn_w_gate"].T, wsel=wsel,
        W1=a["L2_ffn_W1"], W2=a["L2_ffn_W2"].reshape(4, P, P).transpose(1, 0, 2).reshape(P, 512),
        wg_pad=wg_pad))
    arrays["w_l0"] = np.concatenate([
        a["L0_ffn_w1"].transpose(1, 0, 2).reshape(P, 4096),
        a["L0_ffn_w2"].reshape(8, 4, P, P).transpose(2, 0, 1, 3).reshape(P, 4096),
        a["L0_ffn_attn_w"].T, a["L0_ffn_next_w"].T], 1)
    arrays["w_l1"] = np.concatenate([
        a["L1_ffn_w1_e"].reshape(1024, P).T, a["L1_ffn_w1_s"].T,
        a["L1_ffn_w3_e"].reshape(1024, P).T, a["L1_ffn_w3_s"].T,
        a["L1_ffn_w2_e"].transpose(0, 2, 1).reshape(8, P, P).transpose(1, 0, 2).reshape(P, 1024),
        a["L1_ffn_w2_s"].T], 1)
    partner2 = np.array([(i + 16) % 32 if i < 32 else i for i in range(64)])
    q, k = a["L2_ffn_Wq"], a["L2_ffn_Wk"]
    four = np.stack([q, q[:, :, partner2], k, k[:, :, partner2]], 1)
    four = four.reshape(HP, 2, 4, P, 64).transpose(0, 3, 2, 1, 4).reshape(HP, P, 512)
    wv = a["L2_ffn_Wv"].reshape(HP, 2, E0, P, 64).transpose(0, 3, 1, 2, 4).reshape(HP, P, 1024)
    wo = a["L2_ffn_Wo"].reshape(HP, 2, E0, 64, P).transpose(0, 1, 3, 2, 4).reshape(HP, P, 1024)
    arrays["w_l2"] = np.concatenate([four, wv, wo], 2)
    arrays["w_l3"] = np.stack([a["L3_ffn_w1"], a["L3_ffn_w2"], a["L3_ffn_w3"]]).transpose(2, 0, 1, 3).reshape(P, L3W)

    d, s = np.arange(P), np.arange(S, dtype=f32)
    inv1 = (f32(1.0) / f32(10000.0) ** (np.arange(0, 8, 2, dtype=f32) / f32(8)))[d % 4]
    ang1 = (inv1[:, None] * s[None]).astype(f32)
    sign1 = np.where(d % 8 < 4, -1, 1)[:, None]
    inv2 = (f32(10000.0) ** (-np.arange(16, dtype=f32) / f32(16)))[d % 16]
    ang2 = (inv2[:, None] * s[None]).astype(f32)
    turned = (d % 64 < 32)[:, None]
    sign2 = np.where(d % 32 < 16, -1, 1)[:, None]
    lower = lambda n: np.tile(np.tri(n, n, -1).reshape(1, n * n), (P, 1))
    arrays["consts"] = pack(CONSTS, dict(
        ident=np.eye(P), cos1=np.cos(ang1), sin1=np.sin(ang1) * sign1,
        cos2=np.where(turned, np.cos(ang2), 1), sin2=np.where(turned, np.sin(ang2) * sign2, 0),
        lt4=lower(4), prefer=np.tile(8 - np.arange(8), (P, 1)),
        headof=(d[:, None] // 8 == np.arange(H)[None]))).astype(f32)
    bmask = np.zeros((P, 320), f32)
    bmask[:, 0:64] = np.where(s[None] <= (d % 64)[:, None], 0, MASKED)
    bmask[:, 64:192] = np.where(d[None] // 64 == d[:, None] // 64, 0, MASKED)
    bmask[:, 192:320] = np.eye(P)
    arrays["bmask"] = bmask.astype(ml_dtypes.bfloat16)
    sel = np.zeros((96, NSEL, P), f32)
    for part in range(3):
        for half in range(2):
            to = slice(64 * half, 64 * half + 64)
            for e in range(8):
                for odd in range(2):
                    sel[48 * odd + 16 * part + 8 * half + e, SEL_PAIR + 8 * odd + e, to] = 1
                sel[16 * part + 2 * e + half, SEL_DUO + e, to] = 1
        for e in range(16):
            sel[16 * part + e, SEL_ONE + e, :] = 1
    arrays["sel"] = sel.astype(ml_dtypes.bfloat16)

    nc = bacc.Bacc("TRN2", target_bir_lowering=False, num_devices=1)
    io = {}
    for name in arrays:
        arrays[name] = np.ascontiguousarray(arrays[name])
        io[name] = nc.dram_tensor(f"in_{name}", arrays[name].shape, mybir.dt.from_np(arrays[name].dtype),
                                  kind="ExternalInput").ap()
    io["y"] = nc.dram_tensor("out_y", (16, S, P), F32, kind="ExternalOutput").ap()
    build(nc, io)
    r = run(nc, [{f"in_{name}": v for name, v in arrays.items()}], core_ids=[0])
    return r.results[0]["out_y"]
```

```python
from contextlib import ExitStack

import concourse.bass as bass
from concourse import mybir

F32 = mybir.dt.float32
BF16 = mybir.dt.bfloat16
F32R = mybir.dt.float32r
I32 = mybir.dt.int32
ALU = mybir.AluOpType
ACT = mybir.ActivationFunctionType
AX = mybir.AxisListType

P = 128
T = 8
S = 64
TOK = 1024
H = 16
HP = H // 2
E0 = 8
EPS = 1e-5
MASKED = -1.0e30
HIDDEN = -1.0e20 * 8.0 ** 0.5

COLS = dict(ln_scale=1, ln_bias=1, attn_b=1, b1_0=32, b2_0=8, bq1=1, bq1p=1, bk1=1, bk1p=1,
            bk3=1, bq3=1, ln1_g=1, ln1_b=1, b1_2=4, bg=1)
ROWS = dict(next_b=128, bv1=128, bo1=128, ln1_gr=128, ln1_br=128, b2_2=128, ln2_g=128, ln2_b=128,
            bv3=128, bo3=128, b1_3=16, b2_3=16, b3_3=16)
CONSTS = dict(ident=128, cos1=64, sin1=64, cos2=64, sin2=64, lt4=16, prefer=8, headof=16)
WB = dict(wq1=128, wq1p=128, wv1=128, wo1=128, wk3=128, wv3=128, wq3=128, wo3=128,
          w_gate=16, wsel=256, W1=512, W2=512, wg_pad=240)
SEL_PAIR, SEL_DUO, SEL_ONE, NSEL = 0, 16, 24, 40


def offsets(sizes):
    at, out = 0, {}
    for name, n in sizes.items():
        out[name] = (at, n)
        at += n
    return out, at


COL_AT, NCOL = offsets(COLS)
ROW_AT, NROW = offsets(ROWS)
CONST_AT, NCONST = offsets(CONSTS)
WB_AT, NWB = offsets(WB)

L0W = 2 * 4096 + 2 * 128
L1W = 3 * 9 * 128
L2W = 512 + 1024 + 1024
L3W = 3 * 16 * 128
L1_AT = 2 * L2W
L1_LAG = 2
TOP2_AT = [[0], [1], [2], [3], [4, 5], [], [], [6]]
L3_LAG = 3
STAGE = max(L0W, L1_AT + L1W, L3W)

ATT = {0: 0, 1: 1, 3: 2}
LN_ROWS = [0, 1, 0, 1, 0, 1, 0, 1, 1, 0, 1]
COLUMNS_OF = [0, 2, 3, 4, 5, 6, 7, 9, 10]

ACC_COUNT = {}
_n = 0
for _name, _k in (("att0", T), ("eo", T), ("att1", T), ("l1", 10), ("l2", 65), ("ff", 2), ("att3", T), ("l3", 17)):
    ACC_COUNT[_name] = _n
    _n += _k


FF_PARTS, _n = {}, 0
for _name, _k in (("w1", 2), ("x1", 2), ("x2", 2), ("w3", 4), ("x3", 2), ("end", 0)):
    FF_PARTS[_name] = _n
    _n += _k


def psum_plan():
    jobs = []

    def job(name, banks=2, reads=2):
        jobs.append((name, banks, reads))

    def attention(i):
        for t in range(T + 1):
            if t < T:
                job(f"s{i}.{t}", 2, 1)
            if t >= 1:
                job(f"p{i}.{t - 1}")
            if i != 0 and t == 7:
                job(f"ot{i}.0", 1, 1)
            if i != 0 and t == 8:
                job(f"out{i}.0", 1, 1)

    def columns(n, p):
        job(f"x.{n}.{p}", 1, 1)

    job("k1a")
    job("k1b")
    columns(0, 0)
    columns(0, 1)
    attention(0)
    for t in range(T):
        if t % 4 == 0:
            columns(1, t // 4)
            job(f"xa.{t // 4}", 1, 1)
        job(f"h.{t}", 1, 1)
        if t == 6:
            job("nx.0", 1, 1)
    job("nx.1", 1, 1)
    columns(2, 0)
    job("v1.0", 2, 4)
    job("v1.1", 2, 4)
    columns(2, 1)
    job("qa")
    job("qb")
    attention(1)
    job("ot1.1", 1, 1)
    job("out1.1", 1, 1)
    columns(3, 0)
    job("rt", 1, 1)
    columns(3, 1)
    for c in range(9 + L1_LAG):
        if c < 9:
            job(f"G.{c}")
            job(f"U.{c}", 2, 1)
        if c == L1_LAG:
            job("gt1", 1, 1)
        if L1_LAG <= c < 8 + L1_LAG:
            job(f"E1.{c - L1_LAG}", 2, 1)
    columns(4, 0)
    columns(4, 1)
    job("s2")
    job("p2")
    job("o2")
    columns(5, 0)
    columns(5, 1)
    job("gs.0", 2, 1)
    job("gs.1", 2, 1)
    for m in "qk":
        for n in "ab":
            job(f"{m}{n}.0", 2, 1)
    job("s.0", 2, 1)
    for t in range(T):
        job(f"y.0.{t}", 2, 1)
    job("pt.0")
    job("gt2.first", 1, 1)
    job("o.0")
    for hp in range(HP):
        for k in range(E0):
            job(f"E2.{hp}.{k}", 2, 1)
            if hp < HP - 1:
                if k < 2:
                    job(f"{'qk'[k]}a.{hp + 1}", 2, 1)
                    job(f"{'qk'[k]}b.{hp + 1}", 2, 1)
                job(f"y.{hp + 1}.{k}", 2, 1)
                if k == 4:
                    job(f"s.{hp + 1}", 2, 1)
        if hp < HP - 1:
            job(f"pt.{hp + 1}")
            if hp == 0 or hp % 2 == 1:
                job(f"gt2.{(hp + 1) // 2}", 1, 1)
            job(f"o.{hp + 1}")
    job("k3")
    job("v3.0", 2, 4)
    job("v3.1", 2, 4)
    columns(6, 0)
    columns(6, 1)
    for c in range(4):
        job(f"f.{c}", 2, 1)
    columns(7, 0)
    columns(7, 1)
    job("q3")
    attention(3)
    job("ot3.1", 1, 1)
    job("out3.1", 1, 1)
    columns(8, 0)
    job("lg", 1, 1)
    columns(8, 1)
    job("h1.0", 2, 1)
    for e in range(16 + L3_LAG):
        if e < 15:
            job(f"h1.{e + 1}", 2, 1)
        if e < 16:
            job(f"h2.{e}", 2, 1)
        if e == L3_LAG:
            job("vt", 1, 1)
            job("gt3", 1, 1)
        if e >= L3_LAG:
            job(f"E3.{e - L3_LAG}", 2, 1)
    return jobs


def build(nc, io):
    with ExitStack() as ctx:
        def sb(name, shape, dt=F32):
            return ctx.enter_context(nc.sbuf_tensor(name, shape, dt))

        def sb_twice(name, shape, count=1):
            with ExitStack() as scope:
                plain = [scope.enter_context(nc.sbuf_tensor(f"{name}{i}", shape, F32)) for i in range(count)]
            rounded = [sb(f"{name}{i}_r", shape, F32R) for i in range(count)]
            return plain, rounded

        def sem(name):
            return ctx.enter_context(nc.semaphore(name))

        X = sb("X", [P, T, P])
        XN, XN_r = sb_twice("XN", [P, T, P], 2)
        XT, XT_r = sb_twice("XT", [P, TOK], 2)
        ctxT = sb("ctxT_sb", [P, TOK])
        (ctxR,), (ctxR_r,) = sb_twice("ctxR_sb", [P, T, P])
        KX, KX_r = sb_twice("KX", [P, 2, H, S], 2)
        VX = [sb(f"VX{i}", [P, 2 * T, HP, 2, 9]) for i in range(2)]
        KT = sb("KT", [P, TOK])
        QT = sb("QT", [P, TOK])
        PB = sb("PB", [P, 3, TOK])
        PT, PT_r = sb_twice("PT", [P, TOK], 2)
        (ON,), (ON_r,) = sb_twice("ON", [P, T, P])
        (OC,), (OC_r,) = sb_twice("OC", [P, TOK])
        (stage,), (stage_r,) = sb_twice("stage", [P, STAGE])
        wb = sb("wb_sb", [P, NWB])
        wk1 = sb("wk1_sb", [P, 2 * P])
        cols = sb("cols_sb", [P, NCOL])
        rows = sb("rows_sb", [P, NROW])
        consts = sb("consts_sb", [P, NCONST])
        sel = sb("sel_sb", [96, NSEL, P], BF16)
        bmask = sb("bmask_sb", [P, 64 + 128 + 128], BF16)
        stats = sb("stats", [P, T, 6])
        meanvar = sb("meanvar", [P, T, 2])
        vareps = sb("vareps", [P, T])
        rstd = sb("rstd", [P, T])
        minus_half = sb("minus_half", [P, T])
        mx2 = sb("mx", [P, 2, 16])
        rsum2 = sb("rsum", [P, 2, 16])
        SC = sb("SC", [P, T, 16])
        small = sb("small", [P, 1024])
        G3 = sb("G3", [P, T, 96], BF16)
        GT = sb("GT", [96, TOK], BF16)
        GTh = sb("GTh", [96, 4, TOK], BF16)
        maskB = sb("maskB", [P, T, S], BF16)
        (big,), (big_r,) = sb_twice("big", [P, 6, TOK])
        psum = ctx.enter_context(nc.psum_tensor("psum", [P, 4, 1024], F32))
        ACC = psum[:, 3, :]
        mx, rsum = mx2[:, 0, :], rsum2[:, 0, :]

        def col(name, i=0, n=1):
            at = COL_AT[name][0]
            return cols[:, at + i:at + i + n]

        def row(name):
            at, n = ROW_AT[name]
            return rows[:, at:at + n]

        def const(name):
            at, n = CONST_AT[name]
            return consts[:, at:at + n]

        def weight(name):
            at, n = WB_AT[name]
            return wb[:, at:at + n]

        def half(x, p):
            return x[:, 512 * p:512 * p + 512]

        def over(x, n, at=1):
            shape = list(x.shape)
            shape.insert(at, n)
            return x.unsqueeze(at).broadcast_to(shape)

        ident = const("ident")
        causal = bmask[:, 0:64]
        blocks = bmask[:, 64:192]
        identb = bmask[:, 192:320]
        w1_0 = stage[:, 0:4096].rearrange("p (t n) -> p t n", t=T)
        w2_0 = stage[:, 4096:8192].rearrange("p (t c n) -> p t c n", t=T, c=4)
        attn_w = stage[:, 8192:8320]
        next_w = stage[:, 8320:8448]
        XAT = big[:, 5, :]
        SG = [QT[:, :], KT[:, :]]
        HID = [KX[i // 2][:, i % 2, :, :].rearrange("p h k -> p (h k)") for i in range(4)]
        X_hi, X_lo = PT_r[0][:, :], PT_r[1][:, :]
        w_l1_lo = stage_r[:, L1_AT:L1_AT + L1W].rearrange("p (m c n) -> p m c n", m=3, c=9)
        w_l1_hi = [big_r[:, 2 * m:2 * m + 2, :].rearrange("p a n -> p (a n)")[:, 0:9 * 128]
                   .rearrange("p (c n) -> p c n", c=9) for m in range(2)]
        w_l1 = stage[:, L1_AT:L1_AT + L1W].rearrange("p (m c n) -> p m c n", m=3, c=9)
        w_qkv = [stage[:, 1536 * i:1536 * (i + 1)] for i in range(2)]
        w_o = [stage[:, 3072 + 1024 * i:3072 + 1024 * (i + 1)] for i in range(2)]
        GVO = big[:, 0:2, :].rearrange("p a (t v g) -> p (a t) v g", t=4, v=2)
        YG = [big[:, 2, :], big[:, 3, :]]
        AT = [big[:, 4, :], big[:, 5, :]]
        ROTQ = XT[0][:, :]
        ROTK = ON[:, :, :].rearrange("p t n -> p (t n)")
        w_qkv_hi = [k[:, :, :, :].rearrange("p b h k -> p (b h k)")[:, 0:1536] for k in KX_r]
        w_qkv_lo = [stage_r[:, 1536 * i:1536 * (i + 1)] for i in range(2)]
        X2_hi = PT_r[1][:, :]
        X2_lo = ctxR_r[:, :, :].rearrange("p t n -> p (t n)")
        V2 = XN[1][:, :, :].rearrange("p t (j v) -> p t j v", j=2)
        w_l3 = stage[:, 0:L3W].rearrange("p (m e n) -> p m e n", m=3, e=16)
        w_l3_lo = stage_r[:, 0:L3W].rearrange("p (m e n) -> p m e n", m=3, e=16)
        w_l3_hi = [big_r[:, 2 * m:2 * m + 2, :].rearrange("p a (e n) -> p (a e) n", n=P) for m in range(2)]
        A1 = [PB[:, i, :] for i in range(2)]
        A1_hi = [XN_r[1][:, :, :].rearrange("p t n -> p (t n)"), OC_r[:, :]]
        A1_lo = [ON_r[:, :, :].rearrange("p t n -> p (t n)"), XT_r[1][:, :]]
        A2 = HID
        A3 = [big[:, 4 + i, :] for i in range(2)]
        zeros = G3[:, :, :].rearrange("p t g -> p (t g)")
        OT = [small[:, 256 * i:256 * i + 256] for i in range(2)]
        OT_acc = [ACC[:, 512 * i:512 * i + 256] for i in range(2)]
        OR_acc = [ACC[:, 512 * i + 256:512 * i + 512] for i in range(2)]
        ctxV = big[:, 0, :].rearrange("p (b h d) -> p b h d", b=2 * T, h=HP)
        maskI = big[:, 1, 0:512].bitcast(I32).rearrange("p (t k) -> p t k", t=T)

        ld_x = sem("ld_x")
        ld_small = sem("ld_small")
        ld_ctxT = sem("ld_ctxT")
        ld_ctxR = sem("ld_ctxR")
        ld_ctxV = sem("ld_ctxV")
        ld_rows = sem("ld_rows")
        ld_wk1 = sem("ld_wk1")
        ld_wb = sem("ld_wb")
        ld_sel = sem("ld_sel")
        ld_mask = sem("ld_mask")
        ld_l0 = sem("ld_l0")
        ld_l1 = sem("ld_l1")
        ld_qkv = [sem(f"ld_qkv{i}") for i in range(2)]
        ld_o = [sem(f"ld_o{i}") for i in range(2)]
        ld_l3 = sem("ld_l3")
        stored = sem("stored")
        cleared = sem("cleared")
        slot_full = [sem(f"slot_full{i}") for i in range(3)]
        slot_read = [sem(f"slot_read{i}") for i in range(3)]
        acc_full = sem("acc_full")
        acc_read = sem("acc_read")
        dve_step = sem("dve_step")
        pool_step = sem("pool_step")
        ln_var = [sem(f"ln_var{p}") for p in range(2)]
        ln_rstd = [sem(f"ln_rstd{p}") for p in range(2)]
        xn_ready = [sem(f"xn_ready{p}") for p in range(2)]
        kx_ready = sem("kx_ready")
        vx_ready = sem("vx_ready")
        k_ready = sem("k_ready")
        q_ready = sem("q_ready")
        at_exp = sem("at_exp")
        ot_full = sem("ot_full")
        ot_read = sem("ot_read")
        at_out = sem("at_out")
        x_added = sem("x_added")
        mask_ready = sem("mask_ready")
        nx_gelu = sem("nx_gelu")
        gates_ready = sem("gates_ready")
        ff_hi = sem("ff_hi")
        ff_lo = sem("ff_lo")
        a1_parts = sem("a1_parts")
        qkv_hi = sem("qkv_hi")
        qkv_lo = sem("qkv_lo")
        roped = sem("roped")
        v_ready = sem("v_ready")
        s_exp = sem("s_exp")
        s_recip = sem("s_recip")
        s_norm = sem("s_norm")
        y1_ready = sem("y1_ready")
        l3_shift = sem("l3_shift")
        l3_exp = sem("l3_exp")
        l3_val = sem("l3_val")
        x_final = sem("x_final")

        slot_of, full_before, read_before = {}, {}, {}
        filled, emptied = [0, 0, 0], [0, 0, 0]
        for n, (name, banks, reads) in enumerate(psum_plan()):
            s = n % 3
            slot_of[name], full_before[name], read_before[name] = s, filled[s], emptied[s]
            filled[s] += banks
            emptied[s] += reads

        def slot(name):
            return psum[:, slot_of[name], :]

        def take(pe, name):
            if read_before[name]:
                pe.wait_ge(slot_read[slot_of[name]], read_before[name])
            return slot(name)

        def full(name):
            return slot_full[slot_of[name]]

        def read(name):
            return slot_read[slot_of[name]]

        def wait_full(eng, name, banks=2):
            eng.wait_ge(slot_full[slot_of[name]], full_before[name] + banks)

        def wait_read(eng, name, reads=1):
            eng.wait_ge(slot_read[slot_of[name]], read_before[name] + reads)

        block = ctx.enter_context(nc.Block())

        @block.sync
        def _(sp):
            for bb in range(2):
                sp.dma_start(X[64 * bb:64 * bb + 64, :, :], io["x"][8 * bb:8 * bb + 8].rearrange("t s d -> s t d"))\
                    .then_inc(ld_x, 16)
            sp.dma_start(wk1[:, :], io["wk1"]).then_inc(ld_wk1, 16)
            sp.dma_start(consts[:, :], io["consts"]).then_inc(ld_small, 16)
            sp.dma_start(bmask[:, :], io["bmask"]).then_inc(ld_small, 16)
            sp.dma_start(cols[:, :], io["cols"]).then_inc(ld_small, 16)
            sp.dma_start(wb[:, :], io["wb"]).then_inc(ld_wb, 16)
            sp.dma_start(sel[:, :, :], io["sel"]).then_inc(ld_sel, 16)
            wait_read(sp, "nx.1")
            sp.dma_start(stage[:, L1_AT:L1_AT + L1W], io["w_l1"]).then_inc(ld_l1, 16)
            for hp in range(HP):
                if hp >= 2:
                    wait_full(sp, f"y.{hp - 2}.7")
                sp.dma_start(w_qkv[hp % 2], io["w_l2"][hp, :, 0:1536]).then_inc(ld_qkv[hp % 2], 16)
                if hp >= 2:
                    sp.wait_ge(acc_full, ACC_COUNT["l2"] + 8 * (hp - 1))
                sp.dma_start(w_o[hp % 2], io["w_l2"][hp, :, 1536:L2W]).then_inc(ld_o[hp % 2], 16)
            sp.wait_ge(acc_full, ACC_COUNT["l2"] + 65)
            sp.dma_start(stage[:, 0:L3W], io["w_l3"]).then_inc(ld_l3, 16)
            sp.wait_ge(x_final, 1)
            for bb in range(2):
                sp.dma_start(io["y"][8 * bb:8 * bb + 8].rearrange("t s d -> s t d"), X[64 * bb:64 * bb + 64, :, :])\
                    .then_inc(stored, 16)
            sp.wait_ge(stored, 32)

        @block.gpsimd
        def _(pool):
            steps = [0]

            def settle(ins):
                steps[0] += 1
                ins.then_inc(pool_step, 1)
                pool.wait_ge(pool_step, steps[0])

            def rsqrt(l, halves=(0, 1)):
                for p in halves:
                    q = slice(4 * p, 4 * p + 4)
                    pool.wait_ge(ln_var[p], l + 1)
                    pool.tensor_tensor(rstd[:, q], vareps[:, q], minus_half[:, q], ALU.pow).then_inc(ln_rstd[p], 1)

            def add_row(l, name):
                for p in range(2):
                    pool.wait_ge(xn_ready[p], l + 1)
                pool.tensor_tensor(X[:, :, :], X[:, :, :], over(row(name), T), ALU.add).then_inc(x_added, 1)

            def keys(i, t):
                n = 8 * ATT[i] + t
                if t >= 2:
                    wait_full(pool, f"s{i}.{t - 2}")
                src = (ctxT if i == 0 else KT)[:, 128 * t:128 * t + 128].rearrange("p (b k) -> p b k", b=2)
                pool.tensor_tensor(KX[t % 2][:, :, :, :], over(src, H, 2),
                                   over(over(const("headof"), S, 2), 2, 1), ALU.mult).then_inc(kx_ready, 1)

            def attention_keys(i):
                for t in range(2, T):
                    keys(i, t)

            pool.memset(minus_half[:, :], -0.5).then_inc(cleared, 1)
            for v in VX:
                pool.memset(v[:, :, :, :, :], 0.0).then_inc(cleared, 1)
            pool.memset(G3[:, :, :], 0.0).then_inc(cleared, 1)
            pool.wait_ge(cleared, 4)
            for v in VX:
                for j in range(2):
                    pool.memset(v[64 * j:64 * j + 64, :, :, j, 8:9], 1.0).then_inc(cleared, 1)
            pool.wait_ge(cleared, 8)
            rsqrt(0)
            pool.wait_ge(ld_small, 48)
            pool.wait_ge(ld_ctxT, 16)
            keys(0, 0)
            keys(0, 1)
            attention_keys(0)
            for p in range(2):
                rsqrt(1, [p])
                rsqrt(2, [p])
            rsqrt(3)
            pool.wait_ge(k_ready, 2)
            keys(1, 0)
            keys(1, 1)
            pool.wait_ge(ld_rows, 16)
            add_row(3, "bo1")
            attention_keys(1)
            def split_qkv(hp):
                pool.wait_ge(qkv_hi, hp + 1)
                pool.tensor_tensor(w_qkv_lo[hp % 2], w_qkv[hp % 2], w_qkv_hi[hp % 2].bitcast(F32), ALU.subtract)\
                    .then_inc(qkv_lo, 1)

            rsqrt(4)
            rsqrt(5)
            split_qkv(0)
            split_qkv(1)
            rsqrt(6)
            add_row(6, "ln2_b")
            def rope2_sum(hp, m):
                wait_read(pool, f"{'qk'[m]}a.{hp}")
                wait_read(pool, f"{'qk'[m]}b.{hp}")
                dst, rot = (QT[:, :], ROTQ) if m == 0 else (KT[:, :], ROTK)
                pool.tensor_tensor(dst, dst, rot, ALU.add).then_inc(roped, 1)

            def mix_values(hp, t):
                wait_read(pool, f"y.{hp}.{t}")
                yb = YG[t % 2].rearrange("p (j e v) -> p j e v", j=2, e=E0)
                settle(pool.tensor_tensor(yb[:, :, 0:4, :], yb[:, :, 0:4, :], yb[:, :, 4:8, :], ALU.add))
                settle(pool.tensor_tensor(yb[:, :, 0:2, :], yb[:, :, 0:2, :], yb[:, :, 2:4, :], ALU.add))
                if t == 0 and hp >= 1:
                    wait_full(pool, f"o.{hp - 1}")
                pool.tensor_tensor(V2[:, t, :, :], yb[:, :, 0, :], yb[:, :, 1, :], ALU.add).then_inc(v_ready, 1)

            def divide(hp):
                pool.wait_ge(s_recip, hp + 1)
                pb = PB[:, hp % 2, :].rearrange("p (g k) -> p g k", g=16)
                pool.tensor_tensor(pb, pb, over(rsum2[:, hp % 2, :], 64, 2), ALU.mult).then_inc(s_norm, 1)

            rope2_sum(0, 0)
            rope2_sum(0, 1)
            for hp in range(HP):
                for k in range(T):
                    if hp >= 1 and k < 2:
                        rope2_sum(hp, k)
                    mix_values(hp, k)
                    if k == 3 and 1 <= hp < HP - 1:
                        split_qkv(hp + 1)
                    if k == (5 if hp else 2):
                        divide(hp)
            rsqrt(7)
            for p in range(2):
                pool.wait_ge(xn_ready[p], 8)
            settle(pool.tensor_tensor(XN[0][:, :, :], XN[1][:, :, :], over(row("ln1_gr"), T), ALU.mult))
            settle(pool.tensor_tensor(XN[0][:, :, :], XN[0][:, :, :], over(row("ln1_br"), T), ALU.add))
            pool.tensor_tensor(XN[0][:, :, :], XN[0][:, :, :], over(row("b2_2"), T), ALU.add).then_inc(y1_ready, 1)
            wait_read(pool, "k3", 2)
            keys(3, 0)
            keys(3, 1)
            rsqrt(8)
            rsqrt(9)
            add_row(9, "bo3")
            attention_keys(3)
            rsqrt(10)

        @block.scalar
        def _(act):
            act.dma_start(ctxT[:, :], io["ctxT"]).then_inc(ld_ctxT, 16)
            act.dma_start(ctxV, io["ctxV"]).then_inc(ld_ctxV, 16)
            act.dma_start(rows[:, :], io["rows"].partition_broadcast(P)).then_inc(ld_rows, 16)
            for bb in range(2):
                act.dma_start(maskI[64 * bb:64 * bb + 64, :, :],
                              io["mask"][8 * bb:8 * bb + 8].rearrange("t q k -> q t k")).then_inc(ld_mask, 16)
            act.dma_start(stage[:, 0:L0W], io["w_l0"]).then_inc(ld_l0, 16)
            for bb in range(2):
                act.dma_start(ctxR[64 * bb:64 * bb + 64, :, :],
                              io["ctx"][8 * bb:8 * bb + 8].rearrange("t s d -> s t d")).then_inc(ld_ctxR, 16)

            def columns(n, scale=None, bias=None, hi=None):
                for p in range(2):
                    name = f"x.{n}.{p}"
                    wait_full(act, name, 1)
                    out, src = half(XT[n % 2], p), slot(name)[:, 0:512]
                    if scale is None:
                        act.activation(out, src, ACT.Copy).then_inc(read(name), 1)
                    else:
                        act.activation(out, src, ACT.Identity, scale=scale, bias=bias).then_inc(read(name), 1)
                    if hi is not None:
                        wait_read(act, name)
                        upper(half(hi, p), out)

            def upper(dst, src):
                act.activation(dst, src, ACT.Copy).then_inc(ff_hi, 1)

            def attention(i, upper_parts=()):
                for t in range(T + 2):
                    if t == 3 and upper_parts:
                        act.wait_ge(ld_l1 if i == 1 else ld_l3, 16)
                    if upper_parts and 3 <= t < 3 + len(upper_parts):
                        upper(*upper_parts[t - 3])
                    if t < T:
                        wait_read(act, f"s{i}.{t}")
                        act.activation(PB[:, t % 3, :], PB[:, t % 3, :], ACT.Exp, scale=8.0 ** -0.5)\
                            .then_inc(at_exp, 1)
                    if 1 <= t <= T:
                        u = t - 1
                        if u >= 2:
                            act.wait_ge(ot_full, 8 * ATT[i] + u - 1)
                        for p in range(2):
                            wait_full(act, f"p{i}.{u}", p + 1)
                            act.activation(half(PT[u % 2], p), half(slot(f"p{i}.{u}"), p), ACT.Copy)\
                                .then_inc(read(f"p{i}.{u}"), 1)
                    if t >= 2:
                        u = t - 2
                        act.wait_ge(ot_full, 8 * ATT[i] + u + 1)
                        if u >= 2:
                            act.wait_ge(acc_full, ACC_COUNT[f"att{i}"] + u - 1)
                        act.activation(OT[u % 2], OT_acc[u % 2], ACT.Copy).then_inc(ot_read, 1)
                    if i != 0 and t == 7:
                        out_columns(i, 0)

            def out_columns(i, p):
                wait_full(act, f"ot{i}.{p}", 1)
                act.activation(half(OC, p), slot(f"ot{i}.{p}")[:, 0:512], ACT.Copy).then_inc(read(f"ot{i}.{p}"), 1)

            def gate_columns(name, out):
                wait_full(act, name, 1)
                act.activation(out, slot(name)[0:96, 0:512].bitcast(BF16), ACT.Copy).then_inc(read(name), 1)

            columns(0)
            attention(0)
            act.wait_ge(ld_small, 48)
            for t in range(T):
                if t % 4 == 0:
                    p = t // 4
                    wait_full(act, f"x.1.{p}", 1)
                    act.activation(half(XT[1], p), slot(f"x.1.{p}")[:, 0:512], ACT.Identity, scale=col("ln_scale"),
                                   bias=col("ln_bias")).then_inc(read(f"x.1.{p}"), 1)
                    wait_full(act, f"xa.{p}", 1)
                    act.activation(half(XAT, p), slot(f"xa.{p}")[:, 0:512], ACT.Identity, bias=col("attn_b"))\
                        .then_inc(read(f"xa.{p}"), 1)
                wait_full(act, f"h.{t}", 1)
                if t >= 2:
                    act.wait_ge(acc_full, ACC_COUNT["eo"] + t - 1)
                for c in range(4):
                    f = slice(128 * c, 128 * c + 128)
                    ins = act.activation(big[:, 2 + t % 2, f], slot(f"h.{t}")[:, f], ACT.Gelu,
                                         bias=col("b1_0", 4 * t + c))
                ins.then_inc(read(f"h.{t}"), 1)
                if t >= 6:
                    p = t - 6
                    q = slice(4 * p, 4 * p + 4)
                    wait_read(act, f"nx.{p}")
                    act.activation(ON[:, q, :], ON[:, q, :], ACT.Gelu).then_inc(nx_gelu, 1)
            columns(2)
            attention(1, [(w_l1_hi[m], w_l1[:, m]) for m in range(2)])
            out_columns(1, 1)
            def split_qkv(hp):
                act.wait_ge(ld_qkv[hp % 2], 16 * (hp // 2 + 1))
                act.activation(w_qkv_hi[hp % 2], w_qkv[hp % 2], ACT.Copy).then_inc(qkv_hi, 1)

            columns(3, hi=X_hi)
            wait_full(act, "rt", 1)
            act.activation(SC[:, :, :], slot("rt")[:, 0:128].rearrange("p (t e) -> p t e", t=T),
                           ACT.Sigmoid).then_inc(read("rt"), 1)
            for c in range(9):
                if c >= 2:
                    wait_read(act, f"U.{c - 2}")
                for p in range(2):
                    wait_full(act, f"G.{c}", p + 1)
                    act.activation(half(SG[c % 2], p), half(slot(f"G.{c}"), p), ACT.Silu)\
                        .then_inc(read(f"G.{c}"), 1)
                if c == L1_LAG:
                    gate_columns("gt1", GT[:, :])
            columns(4)
            split_qkv(0)
            for p in range(2):
                wait_read(act, "s2", p + 1)
                act.activation(half(PB[:, 0, :], p), half(PB[:, 0, :], p), ACT.Exp, scale=128.0 ** -0.5)\
                    .then_inc(at_exp, 1)
            split_qkv(1)
            for p in range(2):
                wait_full(act, "p2", p + 1)
                act.activation(half(PT[0], p), half(slot("p2"), p), ACT.Copy).then_inc(read("p2"), 1)
            columns(5, hi=X2_hi)
            for g in range(2):
                wait_full(act, f"gs.{g}")
                act.activation(big[:, g, :], slot(f"gs.{g}"), ACT.Sigmoid).then_inc(read(f"gs.{g}"), 1)

            def numerators(hp):
                wait_read(act, f"s.{hp}")
                act.activation(PB[:, hp % 2, :], PB[:, hp % 2, :], ACT.Exp, scale=64.0 ** -0.5).then_inc(s_exp, 1)

            numerators(0)
            for hp in range(HP):
                for p in range(2):
                    wait_full(act, f"pt.{hp}", p + 1)
                    act.activation(half(PT[0], p), half(slot(f"pt.{hp}"), p), ACT.Copy).then_inc(read(f"pt.{hp}"), 1)
                if hp <= 1 or hp % 2 == 0:
                    gate_columns(f"gt2.{hp // 2}" if hp else "gt2.first", GTh[:, hp // 2, :])
                if hp >= 1:
                    wait_read(act, f"E2.{hp - 1}.7")
                for b in range(2):
                    wait_full(act, f"o.{hp}", b + 1)
                    act.activation(OC[:, :].rearrange("p (t b q) -> p t b q", t=T, b=2)[:, :, b, :],
                                   half(slot(f"o.{hp}"), b).rearrange("p (t q) -> p t q", t=T), ACT.Copy)\
                        .then_inc(read(f"o.{hp}"), 1)
                if hp < HP - 2:
                    split_qkv(hp + 2)
                if hp < HP - 1:
                    numerators(hp + 1)
            for p in range(2):
                wait_full(act, "k3", p + 1)
                act.activation(half(KT, p), half(slot("k3"), p), ACT.Identity, bias=col("bk3"))\
                    .then_inc(read("k3"), 1)
            columns(6, col("ln1_g"), col("ln1_b"))
            for c in range(4):
                wait_full(act, f"f.{c}")
                act.activation(big[:, c, :], slot(f"f.{c}"), ACT.Relu, bias=col("b1_2", c)).then_inc(read(f"f.{c}"), 1)
            columns(7)
            for p in range(2):
                wait_full(act, "q3", p + 1)
                act.activation(half(QT, p), half(slot("q3"), p), ACT.Identity, bias=col("bq3"))\
                    .then_inc(read("q3"), 1)
            attention(3, [(w_l3_hi[m][:, 8 * n:8 * n + 8, :], w_l3[:, m, 8 * n:8 * n + 8, :])
                          for m in range(2) for n in range(2)])
            out_columns(3, 1)
            columns(8, hi=X_hi)

            def relu(m, e):
                name = f"h{m}.{e}"
                wait_full(act, name)
                if m == 1 and e >= 2:
                    act.wait_ge(a1_parts, e - 1)
                if m == 2 and e >= 4:
                    wait_read(act, f"E3.{e - 4}")
                act.activation(A1[e % 2] if m == 1 else A2[e % 4], slot(name), ACT.Relu,
                               bias=row(f"b{m}_3")[:, e:e + 1]).then_inc(read(name), 1)

            act.wait_ge(l3_shift, 1)
            act.activation(small[:, 0:128], small[:, 0:128], ACT.Exp).then_inc(l3_exp, 1)
            relu(1, 0)
            for e in range(16):
                if e < 15:
                    relu(1, e + 1)
                relu(2, e)
                if e == L3_LAG:
                    gate_columns("gt3", GT[:, :])

        @block.vector
        def _(dve):
            steps = [0]

            def settle(ins):
                steps[0] += 1
                ins.then_inc(dve_step, 1)
                dve.wait_ge(dve_step, steps[0])

            def stats_of(l, src, p):
                q = slice(4 * p, 4 * p + 4)
                for t in range(4 * p, 4 * p + 4):
                    ins = dve.bn_stats(stats[:, t, :], src[:, t, :])
                settle(ins)
                for t in range(4 * p, 4 * p + 4):
                    ins = dve.bn_aggr(meanvar[:, t, :], stats[:, t, :])
                settle(ins)
                dve.tensor_scalar(vareps[:, q], meanvar[:, q, 1], EPS, None, ALU.add).then_inc(ln_var[p], 1)

            def scale(l, src, p):
                dve.wait_ge(ln_rstd[p], l + 1)
                for t in range(4 * p, 4 * p + 4):
                    ins = dve.tensor_scalar(XN[LN_ROWS[l]][:, t, :], src[:, t, :], meanvar[:, t, 0:1],
                                            rstd[:, t:t + 1], ALU.subtract, ALU.mult)
                ins.then_inc(xn_ready[p], 1)

            def scaled(l, halves=(0, 1)):
                for p in halves:
                    dve.wait_ge(xn_ready[p], l + 1)

            def norm(l, src, add=None):
                for p in range(2):
                    if add is not None:
                        settle(add(p))
                    stats_of(l, src, p)
                for p in range(2):
                    scale(l, src, p)
                scaled(l)

            def rows_of(x, p):
                return x[:, 4 * p:4 * p + 4, :]

            def add_acc(dst, name, n):
                def add(p):
                    dve.wait_ge(acc_full, ACC_COUNT[name] + n + p)
                    return dve.tensor_tensor(rows_of(dst, p), rows_of(dst, p),
                                             half(ACC, p).rearrange("p (t n) -> p t n", t=4), ALU.add)
                return add

            def lower(dst, src, hi, n):
                dve.wait_ge(ff_hi, n)
                dve.tensor_tensor(dst, src, hi.bitcast(F32), ALU.subtract).then_inc(ff_lo, 1)

            def attention(i, after, lower_parts=()):
                for t in range(T + 3):
                    if t < T:
                        name = f"s{i}.{t}"
                        wait_full(dve, name)
                        if t >= 3:
                            wait_full(dve, f"p{i}.{t - 3}")
                        sc = slot(name).rearrange("p (h k) -> p h k", h=H)
                        m = mx2[:, t % 2, :]
                        settle(dve.tensor_reduce(m, sc, AX.X, ALU.max))
                        dve.tensor_tensor(PB[:, t % 3, :].rearrange("p (h k) -> p h k", h=H), sc,
                                          over(m, S, 2), ALU.subtract).then_inc(read(name), 1)
                    if t >= 3:
                        u = t - 3
                        dve.wait_ge(acc_full, ACC_COUNT[f"att{i}"] + u + 1)
                        o = OR_acc[u % 2].rearrange("p (h x) -> p h x", h=HP)[:, :, 0:18]
                        o = o.rearrange("p h (j d) -> p h j d", j=2)
                        r = rsum2[:, u % 2, :].rearrange("p (h j) -> p h j", j=2)
                        settle(dve.reciprocal(r, o[:, :, :, 8]))
                        dve.tensor_tensor(ON[:, u, :].rearrange("p (h j d) -> p h j d", h=HP, j=2), o[:, :, :, 0:8],
                                          over(r, 8, 3), ALU.mult).then_inc(at_out, 1)
                        if i == 0:
                            dve.wait_ge(at_out, u + 1)
                            ins = dve.tensor_tensor(X[:, u, :], X[:, u, :], ON[:, u, :], ALU.add)
                            if u in (3, 7):
                                settle(ins)
                    if lower_parts and 4 <= t < 4 + len(lower_parts):
                        lower(*lower_parts[t - 4])
                    if t in after:
                        after[t]()

            def values(i, bias, v, parts=(0, 1)):
                for n in parts:
                    name = f"v{i}.{n}"
                    for m in range(2):
                        wait_full(dve, name, m + 1)
                        for j in range(2):
                            rows_j = slice(64 * j, 64 * j + 64)
                            dve.tensor_tensor(
                                VX[v][rows_j, 8 * n + 4 * m:8 * n + 4 * m + 4, :, j, 0:8],
                                half(slot(name), m)[rows_j].rearrange("p (b h j d) -> p b h j d", b=4, h=HP, j=2)[:, :, :, j, :],
                                over(bias[rows_j].rearrange("p (h j d) -> p h j d", h=HP, j=2)[:, :, j, :], 4),
                                ALU.add).then_inc(read(name), 1)

            def rope1_cos(name, bias, out, p):
                v = lambda x: half(x, p).rearrange("p (b k) -> p b k", k=S)
                wait_full(dve, name, p + 1)
                dve.scalar_tensor_tensor(out=v(out), in0=v(slot(name)), scalar=bias, in1=over(const("cos1"), 8),
                                         op0=ALU.add, op1=ALU.mult).then_inc(read(name), 1)

            def rope1_sin(name, bias, out, turned, p, done):
                v = lambda x: half(x, p).rearrange("p (b k) -> p b k", k=S)
                wait_full(dve, name, p + 1)
                dve.scalar_tensor_tensor(out=v(turned), in0=v(slot(name)), scalar=bias, in1=over(const("sin1"), 8),
                                         op0=ALU.add, op1=ALU.mult).then_inc(read(name), 1)
                wait_read(dve, name, p + 1)
                dve.tensor_tensor(half(out, p), half(out, p), half(turned, p), ALU.add).then_inc(done, 1)

            def add_out(i, p):
                name = f"out{i}.{p}"
                wait_full(dve, name, 1)
                dve.tensor_tensor(rows_of(X, p), rows_of(X, p), slot(name)[:, 0:512].rearrange("p (t n) -> p t n", t=4),
                                  ALU.add).then_inc(read(name), 1)
                wait_read(dve, name)

            def lower_x(name, dst, src, hi, p):
                lower(half(dst, p), half(src, p), half(hi, p), FF_PARTS[name] + p + 1)

            def attention_and_norm(i, biased, l, lower_parts, lower_columns):
                def first():
                    dve.wait_ge(x_added, biased)
                    add_out(i, 0)
                    stats_of(l, X, 0)

                attention(i, {10: first}, lower_parts)
                scale(l, X, 0)
                add_out(i, 1)
                stats_of(l, X, 1)
                lower_columns(0)
                scale(l, X, 1)
                scaled(l)
                lower_columns(1)

            def three_parts(gates, dst, n, rest):
                settle(dve.tensor_copy(dst(0), gates))
                settle(dve.tensor_tensor(rest, gates, dst(0), ALU.subtract))
                settle(dve.tensor_copy(dst(1), rest))
                settle(dve.tensor_tensor(rest, rest, dst(1), ALU.subtract))
                dve.tensor_copy(dst(2), rest).then_inc(gates_ready, 1)

            def ranks(v, n, lt, work, work2, out):
                a, b = over(v, n, 2), over(v, n, 3)
                settle(dve.tensor_tensor(work, a, b, ALU.is_equal))
                settle(dve.tensor_tensor(work, work, over(lt, T), ALU.mult))
                settle(dve.tensor_tensor(work2, a, b, ALU.is_gt))
                settle(dve.tensor_tensor(work, work, work2, ALU.add))
                settle(dve.tensor_reduce(out, work, AX.X, ALU.add))

            dve.wait_ge(ld_x, 32)
            norm(0, X)
            dve.wait_ge(ld_small, 48)
            for p in range(2):
                rope1_cos("k1a", col("bk1"), KT, p)
            for p in range(2):
                wait_read(dve, "k1a", p + 1)
                rope1_sin("k1b", col("bk1p"), KT, big[:, 2, :], p, k_ready)
            dve.wait_ge(ld_ctxV, 16)
            dve.wait_ge(cleared, 8)
            for j in range(2):
                r = slice(64 * j, 64 * j + 64)
                ins = dve.tensor_copy(VX[0][r, :, :, j, 0:8], ctxV[r])
            ins.then_inc(vx_ready, 1)

            def second_norm(p):
                scale(1, X, p)
                scaled(1, [p])
                stats_of(2, XN[1], p)

            attention(0, {6: lambda: stats_of(1, X, 0), 7: lambda: second_norm(0),
                          8: lambda: scale(2, XN[1], 0)})
            stats_of(1, X, 1)
            second_norm(1)
            scale(2, XN[1], 1)
            scaled(2)
            dve.wait_ge(ld_rows, 16)
            dve.wait_ge(ld_mask, 32)
            dve.tensor_scalar(maskB[:, :, :], maskI, 0.0, HIDDEN, ALU.is_equal, ALU.mult).then_inc(mask_ready, 1)

            def experts_out(p):
                dve.wait_ge(acc_full, ACC_COUNT["eo"] + 4 * p + 4)
                dve.tensor_tensor(half(OC, p).rearrange("p (t n) -> p t n", t=4),
                                  half(ACC, p).rearrange("p (t n) -> p t n", t=4),
                                  over(col("b2_0", 4 * p, 4), P, 2), ALU.add).then_inc(acc_read, 1)

            def add_next(p):
                wait_full(dve, f"nx.{p}", 1)
                dve.tensor_tensor(rows_of(ON, p), slot(f"nx.{p}")[:, 0:512].rearrange("p (t n) -> p t n", t=4),
                                  over(row("next_b"), 4), ALU.add).then_inc(read(f"nx.{p}"), 1)
                dve.wait_ge(nx_gelu, p + 1)
                settle(dve.tensor_tensor(rows_of(X, p), rows_of(X, p), rows_of(ON, p), ALU.add))
                stats_of(3, X, p)

            experts_out(0)
            add_next(0)
            experts_out(1)
            scale(3, X, 0)
            add_next(1)
            values(1, row("bv1"), 1, [0])
            scale(3, X, 1)
            values(1, row("bv1"), 1, [1])
            scaled(3)
            for p in range(2):
                rope1_cos("qa", col("bq1"), QT, p)
                wait_read(dve, "qa", p + 1)
                rope1_sin("qb", col("bq1p"), QT, PB[:, 0, :], p, q_ready)
            attention_and_norm(1, 1, 4, [(w_l1_lo[:, m], w_l1[:, m], w_l1_hi[m], FF_PARTS["w1"] + m + 1)
                                         for m in range(2)], lambda p: lower_x("x1", X_lo, XT[1], X_hi, p))
            wait_read(dve, "rt")
            s4 = SC[:, :, :].rearrange("p t (g e) -> p (t g) e", g=4)
            pairs = small[:, 0:192].rearrange("p (g n) -> p g n", n=6)
            gsum = small[:, 192:224].rearrange("p (t g) -> p t g", t=T)
            grank = small[:, 224:256].rearrange("p (t g) -> p t g", t=T)
            masked = small[:, 256:384].rearrange("p (t e) -> p t e", t=T)
            gates = small[:, 384:512].rearrange("p (t e) -> p t e", t=T)
            best4 = small[:, 520:584].rearrange("p (t n) -> p t n", t=T)
            wsum = small[:, 512:520]
            rest = small[:, 640:768].rearrange("p (t e) -> p t e", t=T)
            w4 = [small[:, 768 + 128 * i:896 + 128 * i].rearrange("p (t a b) -> p t a b", t=T, a=4) for i in range(2)]
            def hidden(c):
                wait_read(dve, f"G.{c}", 2)
                wait_full(dve, f"U.{c}")
                if c >= 4:
                    dve.wait_ge(acc_full, ACC_COUNT["l1"] + c - 3)
                dve.tensor_tensor(HID[c % 4], SG[c % 2], slot(f"U.{c}"), ALU.mult).then_inc(read(f"U.{c}"), 1)

            def gated(c):
                wait_full(dve, f"E1.{c}")
                wait_read(dve, f"U.{c}")
                dve.tensor_tensor(HID[c % 4], HID[c % 4], slot(f"E1.{c}"), ALU.mult)\
                    .then_inc(read(f"E1.{c}"), 1)

            dve.tensor_tensor(pairs[:, :, 0:3], s4[:, :, 0:3], s4[:, :, 1:4], ALU.add)
            dve.tensor_tensor(pairs[:, :, 3:5], s4[:, :, 0:2], s4[:, :, 2:4], ALU.add)
            settle(dve.tensor_tensor(pairs[:, :, 5:6], s4[:, :, 0:1], s4[:, :, 3:4], ALU.add))
            settle(dve.tensor_reduce(small[:, 192:224], pairs, AX.X, ALU.max))
            ranks(gsum, 4, const("lt4").rearrange("p (a b) -> p a b", a=4), w4[0], w4[1], grank)
            settle(dve.tensor_scalar(grank, grank, 2.0, 2.0, ALU.is_lt, ALU.mult))
            settle(dve.tensor_scalar(grank, grank, -2.0, None, ALU.add))
            settle(dve.tensor_tensor(masked.rearrange("p t (g e) -> p (t g) e", g=4), s4,
                                     over(small[:, 224:256], 4, 2), ALU.add))
            hidden(0)
            for t in range(T):
                ins = dve.max(best4[:, t, :], masked[:, t, :])
            settle(ins)
            settle(dve.memset(best4[:, :, 4:8], 9.0))
            for t in range(T):
                ins = dve.match_replace(gates[:, t, :], best4[:, t, :], masked[:, t, :], -9.0)
            settle(ins)
            settle(dve.scalar_tensor_tensor(out=gates, in0=gates, scalar=-5.0, in1=SC[:, :, :],
                                            op0=ALU.is_lt, op1=ALU.mult))
            settle(dve.tensor_reduce(wsum, gates, AX.X, ALU.add))
            settle(dve.tensor_scalar(wsum, wsum, 1e-6, None, ALU.add))
            settle(dve.reciprocal(wsum, wsum))
            settle(dve.tensor_tensor(gates, gates, over(wsum, 16, 2), ALU.mult))
            three_parts(gates, lambda i: G3[:, :, 16 * i:16 * i + 16], 16, rest)
            for c in range(1, 9 + L1_LAG):
                if c < 9:
                    hidden(c)
                if L1_LAG <= c < 8 + L1_LAG:
                    gated(c - L1_LAG)
            norm(5, X, add_acc(X, "l1", 9))
            p2 = PB[:, 0, :].rearrange("p (t k) -> p t k", t=T)
            for p in range(2):
                q = slice(4 * p, 4 * p + 4)
                wait_full(dve, "s2", p + 1)
                s2 = half(slot("s2"), p).rearrange("p (t k) -> p t k", t=4)
                settle(dve.tensor_reduce(mx[:, q], s2, AX.X, ALU.max))
                dve.tensor_tensor(p2[:, q], s2, over(mx[:, q], P, 2), ALU.subtract).then_inc(read("s2"), 1)
            dve.wait_ge(at_exp, 18)
            settle(dve.tensor_reduce(rsum[:, 0:8], p2, AX.X, ALU.add))
            settle(dve.reciprocal(rsum[:, 0:8], rsum[:, 0:8]))
            for t in range(T):
                wait_full(dve, "o2", t // 4 + 1)
                ins = dve.scalar_tensor_tensor(out=X[:, t, :], in0=slot("o2")[:, 128 * t:128 * t + 128],
                                               scalar=rsum[:, t:t + 1], in1=X[:, t, :], op0=ALU.mult, op1=ALU.add)
                if t % 4 == 3:
                    ins.then_inc(read("o2"), 1)
                    wait_read(dve, "o2", t // 4 + 1)
                    stats_of(6, X, t // 4)
            for p in range(2):
                scale(6, X, p)
            scaled(6)
            for p in range(2):
                lower_x("x2", X2_lo, XT[1], X2_hi, p)

            def rope2_product(hp, k):
                m, n = k // 2, k % 2
                name = f"{'qk'[m]}{'ab'[n]}.{hp}"
                wait_full(dve, name)
                if hp >= 1:
                    dve.wait_ge(roped, 2 * hp)
                dst = ((QT[:, :], ROTQ), (KT[:, :], ROTK))[m][n]
                v = lambda x: x.rearrange("p (b k) -> p b k", k=S)
                dve.tensor_tensor(v(dst), v(slot(name)), over(const(("cos2", "sin2")[n]), 16), ALU.mult)\
                    .then_inc(read(name), 1)

            tv = lambda x: x.rearrange("p (g j e) -> p g j e", g=2 * T, j=2)
            eq, first, left = (tv(small[:, 256 * i:256 * i + 256]) for i in range(3))
            best = small[:, 768:800].rearrange("p (g j) -> p g j", j=2)
            rest2 = small[:, 800:928].rearrange("p (t g) -> p t g", t=T)

            def top2(hp, part):
                s2 = GVO[:, :, :, 16 * hp:16 * hp + 16].rearrange("p t v (j e) -> p (t v) j e", j=2)
                src, out = (s2, first) if part < 3 else (left, eq)
                prefer = over(over(const("prefer"), 2), 2 * T)
                if part in (0, 3):
                    settle(dve.tensor_reduce(best, src, AX.X, ALU.max))
                    settle(dve.tensor_tensor(eq, src, over(best, E0, 3), ALU.is_equal))
                if part in (1, 4):
                    settle(dve.tensor_tensor(eq, eq, prefer, ALU.mult))
                    settle(dve.tensor_reduce(best, eq, AX.X, ALU.max))
                    settle(dve.tensor_tensor(out, eq, over(best, E0, 3), ALU.is_equal))
                if part == 2:
                    settle(dve.tensor_scalar(left, first, -4.0, None, ALU.mult))
                    settle(dve.tensor_tensor(left, left, s2, ALU.add))
                if part == 5:
                    settle(dve.tensor_tensor(eq, eq, first, ALU.add))
                    settle(dve.tensor_tensor(s2, s2, eq, ALU.mult))
                if part == 6:
                    if hp >= 1:
                        wait_full(dve, f"gt2.{hp // 2 - 1}" if hp > 1 else "gt2.first", 1)
                    at = 48 * (hp % 2)
                    three_parts(GVO[:, :, 1, 16 * hp:16 * hp + 16],
                                lambda i: G3[:, :, at + 16 * i:at + 16 * i + 16], 16, rest2)

            def shifted(hp):
                name = f"s.{hp}"
                wait_full(dve, name)
                if hp >= 2:
                    wait_full(dve, f"pt.{hp - 2}")
                sc = slot(name).rearrange("p (g k) -> p g k", g=16)
                settle(dve.tensor_reduce(mx2[:, hp % 2, :], sc, AX.X, ALU.max))
                dve.tensor_tensor(PB[:, hp % 2, :].rearrange("p (g k) -> p g k", g=16), sc,
                                  over(mx2[:, hp % 2, :], S, 2), ALU.subtract).then_inc(read(name), 1)

            def reciprocals(hp):
                if hp >= 2:
                    dve.wait_ge(s_norm, hp - 1)
                dve.wait_ge(s_exp, hp + 1)
                r = rsum2[:, hp % 2, :]
                settle(dve.tensor_reduce(r, PB[:, hp % 2, :].rearrange("p (g k) -> p g k", g=16), AX.X, ALU.add))
                dve.reciprocal(r, r).then_inc(s_recip, 1)

            def gate_values(hp, t):
                name = f"y.{hp}.{t}"
                wait_full(dve, name)
                if hp * T + t >= 2:
                    dve.wait_ge(v_ready, hp * T + t - 1)
                dve.tensor_tensor(YG[t % 2].rearrange("p (g v) -> p g v", v=64),
                                  slot(name).rearrange("p (g v) -> p g v", v=64),
                                  over(GVO[:, t, 0, 16 * hp:16 * hp + 16], 64, 2), ALU.mult)\
                    .then_inc(read(name), 1)

            def gate_outputs(hp, e):
                n = 8 * hp + e
                name = f"E2.{hp}.{e}"
                wait_full(dve, name)
                if e == 0:
                    wait_read(dve, f"o.{hp}", 2)
                if n >= 2:
                    dve.wait_ge(acc_full, ACC_COUNT["l2"] + n - 1)
                dve.tensor_tensor(AT[e % 2], OC[:, :], slot(name), ALU.mult).then_inc(read(name), 1)

            for k in range(4):
                rope2_product(0, k)
            wait_read(dve, "gs.0")
            wait_read(dve, "gs.1")
            for part in range(6):
                top2(0, part)
            shifted(0)
            for t in range(T):
                gate_values(0, t)
                if t == 1:
                    reciprocals(0)
                top2(0 if t == 0 else 1, 6 if t == 0 else t - 1)
            for hp in range(HP):
                for k in range(E0):
                    gate_outputs(hp, k)
                    if hp < HP - 1:
                        if k < 2:
                            rope2_product(hp + 1, 2 * k)
                            rope2_product(hp + 1, 2 * k + 1)
                        gate_values(hp + 1, k)
                    if hp < HP - 2:
                        for part in TOP2_AT[k]:
                            top2(hp + 2, part)
                    if hp < HP - 1:
                        if k == 4:
                            shifted(hp + 1)
                        if k == 5:
                            reciprocals(hp + 1)
            norm(7, XN[0], add_acc(XN[0], "l2", 64))
            values(3, row("bv3"), 0)
            dve.wait_ge(y1_ready, 1)
            add_ff = add_acc(XN[0], "ff", 1)
            for p in range(2):
                settle(add_ff(p))
                stats_of(8, XN[0], p)
            for p in range(2):
                scale(8, XN[0], p)
                scaled(8, [p])
                settle(dve.tensor_tensor(rows_of(XN[1], p), rows_of(XN[1], p), over(row("ln2_g"), 4), ALU.mult))
                dve.wait_ge(x_added, 2)
                settle(dve.tensor_tensor(rows_of(X, p), rows_of(X, p), rows_of(XN[1], p), ALU.add))
                stats_of(9, X, p)
            for p in range(2):
                scale(9, X, p)
            scaled(9)
            attention_and_norm(3, 3, 10, [(w_l3_lo[:, m, 8 * n:8 * n + 8, :], w_l3[:, m, 8 * n:8 * n + 8, :],
                                           w_l3_hi[m][:, 8 * n:8 * n + 8, :], FF_PARTS["w3"] + 2 * m + n + 1)
                                          for m in range(2) for n in range(2)],
                               lambda p: lower_x("x3", X_lo, XT[0], X_hi, p))
            logits = small[:, 0:128]
            by_batch = logits.rearrange("p (b k) -> p b k", b=2)
            work = small[:, 128:256]
            rowgate = small[:, 256:384].rearrange("p (t e) -> p t e", t=T)
            best8 = small[:, 384:400]
            outbias = small[:, 400:408]
            rest = small[:, 512:640].rearrange("p (t e) -> p t e", t=T)
            wait_full(dve, "lg", 1)
            def first_parts(e):
                wait_read(dve, f"h1.{e}")
                if e >= 2:
                    wait_full(dve, f"h2.{e - 2}")
                settle(dve.tensor_copy(A1_hi[e % 2], A1[e % 2]))
                dve.tensor_tensor(A1_lo[e % 2], A1[e % 2], A1_hi[e % 2].bitcast(F32), ALU.subtract)\
                    .then_inc(a1_parts, 1)

            dve.tensor_scalar(logits, slot("lg")[:, 0:128], col("bg"), None, ALU.add).then_inc(read("lg"), 1)
            wait_read(dve, "lg")
            settle(dve.tensor_reduce(mx[:, 0:2], by_batch, AX.X, ALU.max))
            dve.tensor_tensor(by_batch, by_batch, over(mx[:, 0:2], S, 2), ALU.subtract).then_inc(l3_shift, 1)
            first_parts(0)
            dve.wait_ge(l3_exp, 1)
            settle(dve.tensor_reduce(rsum[:, 0:2], by_batch, AX.X, ALU.add))
            settle(dve.reciprocal(rsum[:, 0:2], rsum[:, 0:2]))
            settle(dve.tensor_tensor(by_batch, by_batch, over(rsum[:, 0:2], S, 2), ALU.mult))
            settle(dve.tensor_copy(work, logits))
            first_parts(1)
            for k in range(4):
                for b in range(2):
                    ins = dve.max(best8[:, 8 * b:8 * b + 8], work[:, 64 * b:64 * b + 64])
                settle(ins)
                for b in range(2):
                    w = work[:, 64 * b:64 * b + 64]
                    ins = dve.match_replace(w, best8[:, 8 * b:8 * b + 8], w, -1.0)
                settle(ins)
                if k == 1:
                    first_parts(2)
            dve.scalar_tensor_tensor(out=logits, in0=work, scalar=0.0, in1=logits, op0=ALU.is_lt, op1=ALU.mult)\
                .then_inc(l3_val, 1)
            first_parts(3)
            wait_full(dve, "vt", 1)
            dve.tensor_copy(small[:, 256:384], slot("vt")[:, 0:128]).then_inc(read("vt"), 1)
            wait_read(dve, "vt")
            three_parts(rowgate, lambda i: G3[:, :, 16 * i:16 * i + 16], 16, rest)
            dve.wait_ge(gates_ready, 10)
            settle(dve.tensor_tensor(rest, rowgate, over(row("b3_3"), T), ALU.mult))
            settle(dve.tensor_reduce(outbias, rest, AX.X, ALU.add))
            for e in range(16):
                if e + L3_LAG + 1 < 16:
                    first_parts(e + L3_LAG + 1)
                wait_read(dve, f"h2.{e}")
                wait_full(dve, f"E3.{e}")
                if e >= 2:
                    dve.wait_ge(acc_full, ACC_COUNT["l3"] + e - 1)
                dve.tensor_tensor(A3[e % 2], A2[e % 4], slot(f"E3.{e}"), ALU.mult)\
                    .then_inc(read(f"E3.{e}"), 1)
            for t in range(T):
                if t % 4 == 0:
                    dve.wait_ge(acc_full, ACC_COUNT["l3"] + 16 + t // 4)
                ins = dve.scalar_tensor_tensor(out=X[:, t, :], in0=ACC[:, 128 * t:128 * t + 128],
                                               scalar=outbias[:, t:t + 1], in1=X[:, t, :], op0=ALU.add, op1=ALU.add)
            ins.then_inc(x_final, 1)

        @block.tensor
        def _(pe):
            def done(ins, name):
                ins.then_inc(full(name), 1)

            def rows_to_columns(n, p):
                l = COLUMNS_OF[n]
                name = f"x.{n}.{p}"
                s = take(pe, name)
                pe.wait_ge(xn_ready[p], l + 1)
                for t in range(4):
                    ins = pe.transpose(s[:, 128 * t:128 * t + 128], XN[LN_ROWS[l]][:, 4 * p + t, :], ident)
                done(ins, name)

            def project(name, w, x, halves=(0, 1)):
                s = take(pe, name) if 0 in halves else slot(name)
                for p in halves:
                    done(pe.matmul(half(s, p), w, half(x, p), start=True, stop=True), name)

            def in_parts(out, w, x):
                pe.matmul(out, w[1], x[0], start=True, stop=True, skip_group_check=True)
                pe.matmul(out, w[0], x[1], start=False, stop=True, skip_group_check=True)
                return pe.matmul(out, w[0], x[0], start=False, stop=True, skip_group_check=True)

            def columns_of(parts, at, n):
                return [x[:, at:at + n] for x in parts]

            def project_parts(name, w, x):
                s = take(pe, name)
                for p in range(2):
                    done(in_parts(half(s, p), w, columns_of(x, 512 * p, 512)), name)

            def columns_there(n, p=1):
                wait_read(pe, f"x.{n}.{p}")

            def project_values(i, w):
                for n in range(2):
                    name = f"v{i}.{n}"
                    s = take(pe, name)
                    for b in range(8):
                        tb = 8 * n + b
                        for j in range(2):
                            ins = pe.matmul(s[64 * j:64 * j + 64, 128 * b:128 * b + 128],
                                            ctxT[:, 64 * tb:64 * tb + 64], w, start=True, stop=True)
                        if b % 4 == 3:
                            done(ins, name)

            def attention(i, q, wait_q, mask, v):
                for t in range(T + 3):
                    if t < T:
                        name = f"s{i}.{t}"
                        wait_q(t // 4)
                        pe.wait_ge(kx_ready, 8 * ATT[i] + t + 1)
                        s = take(pe, name)
                        for n in range(2):
                            out = half(s, n)
                            if mask is not None:
                                pe.matmul(out, identb, over(mask(t), 8), start=True, stop=True)
                            for bb in range(2):
                                tok = 128 * t + 64 * bb
                                ins = pe.matmul(out[64 * bb:64 * bb + 64, :], q[:, tok:tok + 64],
                                                KX[t % 2][:, bb, 8 * n:8 * n + 8, :],
                                                start=mask is None, stop=True, skip_group_check=True)
                            done(ins, name)
                    if 1 <= t <= T:
                        u = t - 1
                        name = f"p{i}.{u}"
                        pe.wait_ge(at_exp, 8 * ATT[i] + u + 1 + 2 * (i == 3))
                        s = take(pe, name)
                        for hp in range(HP):
                            c = slice(128 * hp, 128 * hp + 128)
                            ins = pe.transpose(s[:, c], PB[:, u % 3, c], ident)
                            if hp % 4 == 3:
                                done(ins, name)
                    if 2 <= t < T + 2:
                        u = t - 2
                        if u == 0:
                            v[1]()
                        wait_read(pe, f"p{i}.{u}", 2)
                        if u >= 2:
                            pe.wait_ge(at_out, 8 * ATT[i] + u - 1)
                        for bb in range(2):
                            for hp in range(HP):
                                r, at = 32 * (hp % 4), 128 * (hp // 4) + 64 * bb
                                ins = pe.matmul(OT_acc[u % 2][r:r + 18, at:at + 64],
                                                VX[v[0]][:, 2 * u + bb, hp, :, :].rearrange("p j d -> p (j d)"),
                                                PT[u % 2][:, 128 * hp + 64 * bb:128 * hp + 64 * bb + 64],
                                                start=True, stop=True)
                        ins.then_inc(ot_full, 1)
                    if t >= 3:
                        u = t - 3
                        pe.wait_ge(ot_read, 8 * ATT[i] + u + 1)
                        for g in range(2):
                            c = slice(128 * g, 128 * g + 128)
                            ins = pe.transpose(OR_acc[u % 2][:, c], OT[u % 2][:, c], ident)
                        ins.then_inc(acc_full, 1)
                    if i != 0 and t == 7:
                        turned_outputs(i, 0)
                    if i != 0 and t == 8:
                        project_outputs(i, 0)

            def turned_outputs(i, p):
                name = f"ot{i}.{p}"
                s = take(pe, name)
                pe.wait_ge(at_out, 8 * ATT[i] + 4 * p + 4)
                for t in range(4):
                    ins = pe.transpose(s[:, 128 * t:128 * t + 128], ON[:, 4 * p + t, :], ident)
                done(ins, name)

            def half_rows(name, x, w, p):
                s = take(pe, name)
                for t in range(4):
                    ins = pe.matmul(s[:, 128 * t:128 * t + 128], half(x, p)[:, 128 * t:128 * t + 128], w,
                                    start=True, stop=True)
                done(ins, name)

            def project_outputs(i, p):
                wait_read(pe, f"ot{i}.{p}")
                half_rows(f"out{i}.{p}", OC, weight(f"wo{i}"), p)

            def attention_out(i):
                turned_outputs(i, 1)
                project_outputs(i, 1)

            def gate_columns(name, src):
                s = take(pe, name)[0:96, 0:512].bitcast(BF16)
                for t in range(T):
                    ins = pe.transpose(s[:, 128 * t:128 * t + 128], src(t), identb)
                done(ins, name)

            def expand(name, k, gates):
                s = take(pe, name)
                for p in range(2):
                    done(pe.matmul(half(s, p), sel[:, k, :], half(gates, p), start=True, stop=True), name)

            def accumulate(x, w, first, last):
                for t in range(T):
                    ins = pe.matmul(ACC[:, 128 * t:128 * t + 128], x[:, 128 * t:128 * t + 128], w,
                                    start=first and t % 4 == 0, stop=True, skip_group_check=True)
                    if last and t == 3:
                        ins.then_inc(acc_full, 1)
                ins.then_inc(acc_full, 1)

            pe.wait_ge(cleared, 8)
            for p in range(2):
                pe.matmul(half(ACC, p), zeros[:, 0:128], zeros[:, 0:512], start=True, stop=True)
            pe.wait_ge(ld_wk1, 16)
            pe.wait_ge(ld_ctxT, 16)
            project("k1a", wk1[:, 0:128], ctxT)
            project("k1b", wk1[:, 128:256], ctxT)
            pe.wait_ge(ld_small, 48)
            for p in range(2):
                rows_to_columns(0, p)
            attention(0, XT[0], lambda p: columns_there(0, p), lambda t: causal,
                      (0, lambda: pe.wait_ge(vx_ready, 1)))
            pe.wait_ge(ld_l0, 16)

            def enter_ff0(p):
                rows_to_columns(1, p)
                s = take(pe, f"xa.{p}")
                columns_there(1, p)
                pe.matmul(s[:, 0:512], attn_w, half(XT[1], p), start=True, stop=True, skip_group_check=True)
                pe.wait_ge(xn_ready[p], 2)
                for t in range(4):
                    ins = pe.matmul(s[:, 128 * t:128 * t + 128], XN[1][:, 4 * p + t, :], ident,
                                    start=False, stop=True, skip_group_check=True)
                done(ins, f"xa.{p}")

            for t in range(T + 1):
                if t in (0, 4):
                    enter_ff0(t // 4)
                if t < T:
                    name = f"h.{t}"
                    s = take(pe, name)
                    wait_read(pe, f"xa.{t // 4}")
                    for c in range(4):
                        ins = pe.matmul(s[:, 128 * c:128 * c + 128], w1_0[:, t, 128 * c:128 * c + 128],
                                        XAT[:, 128 * t:128 * t + 128], start=True, stop=True)
                    done(ins, name)
                if t >= 1:
                    u = t - 1
                    if u == 0:
                        pe.wait_ge(at_out, 8)
                    wait_read(pe, f"h.{u}")
                    for c in range(4):
                        ins = pe.matmul(ACC[:, 128 * u:128 * u + 128], w2_0[:, u, c, :],
                                        big[:, 2 + u % 2, 128 * c:128 * c + 128], start=c == 0, stop=c == 3)
                    ins.then_inc(acc_full, 1)
                if t in (6, 8):
                    p = (t - 6) // 2
                    pe.wait_ge(acc_read, p + 1)
                    half_rows(f"nx.{p}", OC, next_w, p)
            rows_to_columns(2, 0)
            pe.wait_ge(ld_wb, 16)
            project_values(1, weight("wv1"))
            rows_to_columns(2, 1)
            for p in range(2):
                columns_there(2, p)
                project("qa", weight("wq1"), XT[0], [p])
                project("qb", weight("wq1p"), XT[0], [p])
            attention(1, QT, lambda p: pe.wait_ge(q_ready, p + 1), None, (1, lambda: wait_read(pe, "v1.1", 4)))
            attention_out(1)
            for p in range(2):
                rows_to_columns(3, p)
                s = take(pe, "rt") if p == 0 else slot("rt")
                columns_there(3, p)
                for t in range(4 * p, 4 * p + 4):
                    ins = pe.matmul(s[:, 16 * t:16 * t + 16], XT[1][:, 128 * t:128 * t + 128], weight("w_gate"),
                                    start=True, stop=True)
            done(ins, "rt")
            pe.wait_ge(ff_lo, FF_PARTS["x2"])
            pe.wait_ge(ld_sel, 16)
            for c in range(9 + L1_LAG + 1):
                if c < 9:
                    for m in range(2):
                        project_parts(f"{'GU'[m]}.{c}", (w_l1_hi[m][:, c, :], w_l1_lo[:, m, c, :]), (X_hi, X_lo))
                if c == L1_LAG:
                    pe.wait_ge(gates_ready, 1)
                    gate_columns("gt1", lambda t: G3[:, t, :])
                    wait_read(pe, "gt1")
                if L1_LAG <= c < 8 + L1_LAG:
                    expand(f"E1.{c - L1_LAG}", SEL_DUO + c - L1_LAG, GT)
                u = c - L1_LAG - 1
                if u >= 0:
                    wait_read(pe, f"E1.{u}" if u < 8 else "U.8")
                    accumulate(HID[u % 4], w_l1[:, 2, u, :], u == 0, u == 8)
            for p in range(2):
                rows_to_columns(4, p)
            s = take(pe, "s2")
            for p in range(2):
                columns_there(4, p)
                pe.matmul(half(s, p), identb, over(blocks, 4), start=True, stop=True, skip_group_check=True)
                for t in range(4 * p, 4 * p + 4):
                    c = slice(128 * t, 128 * t + 128)
                    ins = pe.matmul(s[:, c], XT[0][:, c], ctxT[:, c], start=False, stop=True,
                                    skip_group_check=True)
                done(ins, "s2")
            s = take(pe, "p2")
            for t in range(T):
                if t % 4 == 0:
                    pe.wait_ge(at_exp, 17 + t // 4)
                c = slice(128 * t, 128 * t + 128)
                ins = pe.transpose(s[:, c], PB[:, 0, c], ident)
                if t % 4 == 3:
                    done(ins, "p2")
            s = take(pe, "o2")
            pe.wait_ge(ld_ctxR, 32)
            for t in range(T):
                if t % 4 == 0:
                    wait_read(pe, "p2", t // 4 + 1)
                c = slice(128 * t, 128 * t + 128)
                ins = pe.matmul(s[:, c], PT[0][:, c], ctxR[:, t, :], start=True, stop=True)
                if t % 4 == 3:
                    done(ins, "o2")
            for p in range(2):
                rows_to_columns(5, p)
            for g in range(2):
                s = take(pe, f"gs.{g}")
                columns_there(5, g)
                for t in range(4):
                    ins = pe.matmul(s[:, 256 * t:256 * t + 256],
                                    XT[1][:, 128 * (4 * g + t):128 * (4 * g + t) + 128], weight("wsel"),
                                    start=True, stop=True)
                    if t % 2 == 1:
                        done(ins, f"gs.{g}")

            def rope2_job(hp, k):
                project_parts(f"{'qk'[k // 2]}{'ab'[k % 2]}.{hp}",
                              columns_of((w_qkv_hi[hp % 2], w_qkv_lo[hp % 2]), 128 * k, 128), (X2_hi, X2_lo))

            def scores2(hp):
                name = f"s.{hp}"
                s = take(pe, name)
                pe.wait_ge(roped, 2 * hp + 2)
                for t in range(T):
                    for b in range(2):
                        for j in range(2):
                            r, c = slice(64 * j, 64 * j + 64), slice(128 * t + 64 * b, 128 * t + 64 * b + 64)
                            ins = pe.matmul(s[r, c], QT[r, c], KT[r, c], start=True, stop=True)
                    if t % 4 == 3:
                        done(ins, name)

            def expert_values(hp, t):
                name = f"y.{hp}.{t}"
                s = take(pe, name)
                w = (w_qkv_hi[hp % 2], w_qkv_lo[hp % 2])
                for j in range(2):
                    done(in_parts(half(s, j), columns_of((X2_hi, X2_lo), 128 * t, 128),
                                  columns_of(w, 512 + 512 * j, 512)), name)

            def turned_probabilities(hp):
                name = f"pt.{hp}"
                s = take(pe, name)
                pe.wait_ge(s_norm, hp + 1)
                for t in range(T):
                    c = slice(128 * t, 128 * t + 128)
                    ins = pe.transpose(s[:, c], PB[:, hp % 2, c], ident)
                    if t % 4 == 3:
                        done(ins, name)

            def outputs2(hp):
                name = f"o.{hp}"
                s = take(pe, name)
                wait_read(pe, f"pt.{hp}", 2)
                for t in range(T):
                    pe.wait_ge(v_ready, 8 * hp + t + 1)
                    for j in range(2):
                        for b in range(2):
                            r = slice(64 * b, 64 * b + 64)
                            ins = pe.matmul(s[64 * j:64 * j + 64, 512 * b + 64 * t:512 * b + 64 * t + 64],
                                            V2[r, t, j, :], PT[0][r, 128 * t + 64 * j:128 * t + 64 * j + 64],
                                            start=True, stop=True)
                            if t == T - 1 and j == 1:
                                done(ins, name)

            def output_gates(g):
                pe.wait_ge(gates_ready, 2 if g is None else 2 * g + 3)
                gate_columns("gt2.first" if g is None else f"gt2.{g}", lambda t: G3[:, t, :])

            def project_out(hp, e):
                wait_read(pe, f"E2.{hp}.{e}")
                accumulate(AT[e % 2], w_o[hp % 2][:, 128 * e:128 * e + 128],
                           hp == 0 and e == 0, hp == HP - 1 and e == E0 - 1)

            pe.wait_ge(ff_lo, FF_PARTS["w3"])
            pe.wait_ge(qkv_lo, 1)
            for k in range(4):
                rope2_job(0, k)
            scores2(0)
            for t in range(T):
                expert_values(0, t)
            turned_probabilities(0)
            output_gates(None)
            outputs2(0)
            for hp in range(HP):
                if hp < HP - 1:
                    pe.wait_ge(qkv_lo, hp + 2)
                pe.wait_ge(ld_o[hp % 2], 16 * (hp // 2 + 1))
                if hp <= 1 or hp % 2 == 0:
                    wait_read(pe, f"gt2.{hp // 2}" if hp else "gt2.first")
                for k in range(E0):
                    expand(f"E2.{hp}.{k}", SEL_PAIR + 8 * (hp % 2) + k, GTh[:, hp // 2, :])
                    if hp < HP - 1:
                        if k < 2:
                            rope2_job(hp + 1, 2 * k)
                            rope2_job(hp + 1, 2 * k + 1)
                        expert_values(hp + 1, k)
                        if k == 7:
                            turned_probabilities(hp + 1)
                    if k >= 1:
                        project_out(hp, k - 1)
                    if hp < HP - 1 and k == 4:
                        scores2(hp + 1)
                project_out(hp, E0 - 1)
                if hp < HP - 1:
                    if hp == 0 or hp % 2 == 1:
                        output_gates((hp + 1) // 2)
                    outputs2(hp + 1)
            project("k3", weight("wk3"), ctxT)
            project_values(3, weight("wv3"))
            W1 = [weight("W1")[:, 128 * c:128 * c + 128] for c in range(4)]
            for p in range(2):
                rows_to_columns(6, p)
            for p in range(2):
                columns_there(6, p)
                for c in range(2):
                    project(f"f.{c}", W1[c], XT[0], [p])
            for c in range(2, 4):
                project(f"f.{c}", W1[c], XT[0])
            for c in range(4):
                wait_read(pe, f"f.{c}")
            for t in range(T):
                for c in range(4):
                    ins = pe.matmul(ACC[:, 128 * t:128 * t + 128], big[:, c, 128 * t:128 * t + 128],
                                    weight("W2")[:, 128 * c:128 * c + 128], start=c == 0, stop=c == 3)
                if t % 4 == 3:
                    ins.then_inc(acc_full, 1)
            for p in range(2):
                rows_to_columns(7, p)
            for p in range(2):
                columns_there(7, p)
                project("q3", weight("wq3"), XT[1], [p])
            pe.wait_ge(mask_ready, 1)
            attention(3, QT, lambda p: wait_read(pe, "q3", p + 1), lambda t: maskB[:, t, :],
                      (0, lambda: wait_read(pe, "v3.1", 4)))
            attention_out(3)
            for p in range(2):
                rows_to_columns(8, p)
                s = take(pe, "lg") if p == 0 else slot("lg")
                columns_there(8, p)
                for t in range(4 * p, 4 * p + 4):
                    ins = pe.matmul(s[:, 0:128], weight("wg_pad")[:, 112 - 16 * t:240 - 16 * t],
                                    XT[0][:, 128 * t:128 * t + 128], start=t == 0, stop=t == T - 1)
            done(ins, "lg")
            pe.wait_ge(ff_lo, FF_PARTS["end"])
            w3 = lambda m, e: (w_l3_hi[m][:, e, :], w_l3_lo[:, m, e, :])
            project_parts("h1.0", w3(0, 0), (X_hi, X_lo))
            for e in range(16 + L3_LAG + 1):
                if e < 15:
                    project_parts(f"h1.{e + 1}", w3(0, e + 1), (X_hi, X_lo))
                if e < 16:
                    pe.wait_ge(a1_parts, e + 1)
                    project_parts(f"h2.{e}", w3(1, e), (A1_hi[e % 2], A1_lo[e % 2]))
                if e == L3_LAG:
                    s = take(pe, "vt")
                    pe.wait_ge(l3_val, 1)
                    done(pe.transpose(s[:, 0:128], small[:, 0:128], ident), "vt")
                    pe.wait_ge(gates_ready, 10)
                    gate_columns("gt3", lambda t: G3[:, t, :])
                    wait_read(pe, "gt3")
                if L3_LAG <= e < 16 + L3_LAG:
                    expand(f"E3.{e - L3_LAG}", SEL_ONE + e - L3_LAG, GT)
                u = e - L3_LAG - 1
                if u >= 0:
                    wait_read(pe, f"E3.{u}")
                    accumulate(A3[u % 2], w_l3[:, 2, u, :], u == 0, u == 15)


def kernel(**inputs):
    import ml_dtypes
    import numpy as np
    import concourse.bacc as bacc
    from concourse.bass_utils import run_bass_kernel_spmd as run

    a = {k: np.asarray(v) for k, v in inputs.items()}
    f32 = np.float32
    arrays = {"x": a["x"], "ctx": a["ctx_1024"], "mask": a["mask_BxSxS2_ik0"]}
    order = [b + 8 * bb for b in range(8) for bb in range(2)]
    ctx = a["ctx_1024"][order]
    arrays["ctxT"] = ctx.transpose(2, 0, 1).reshape(P, TOK)
    heads = ctx.reshape(16, S, HP, 2, 8)
    arrays["ctxV"] = heads.transpose(3, 1, 0, 2, 4).reshape(P, 2 * T, HP, 8)
    partner1 = np.array([8 * (i // 8) + (i + 4) % 8 for i in range(P)])

    def pack(sizes, parts):
        for n, size in sizes.items():
            assert parts[n].shape[1] == size, (n, parts[n].shape)
        return np.concatenate([parts[n] for n in sizes], 1)

    def column(name):
        return a[name].reshape(P, 1)

    b_kv = a["L3_xattn_b_kv"].reshape(H, 2, 8)
    W_kv = a["L3_xattn_W_kv"].reshape(P, H, 2, 8)
    arrays["cols"] = pack(COLS, dict(
        ln_scale=column("L0_ffn_ln_scale"), ln_bias=column("L0_ffn_ln_bias"), attn_b=column("L0_ffn_attn_b"),
        b1_0=a["L0_ffn_b1"].reshape(8, 4, P).transpose(2, 0, 1).reshape(P, 32),
        b2_0=a["L0_ffn_b2"].T,
        bq1=column("L1_xattn_bq"), bq1p=column("L1_xattn_bq")[partner1],
        bk1=column("L1_xattn_bk"), bk1p=column("L1_xattn_bk")[partner1],
        bk3=b_kv[:, 0].reshape(P, 1), bq3=column("L3_xattn_b_q"),
        ln1_g=column("L2_ffn_ln1_g"), ln1_b=column("L2_ffn_ln1_b"),
        b1_2=a["L2_ffn_b1"].reshape(4, P).T, bg=np.tile(a["L3_ffn_bg"], 8).reshape(P, 1)))
    arrays["rows"] = pack(ROWS, {n: v.reshape(1, -1) for n, v in dict(
        next_b=a["L0_ffn_next_b"], bv1=a["L1_xattn_bv"], bo1=a["L1_xattn_bo"], ln1_gr=a["L2_ffn_ln1_g"],
        ln1_br=a["L2_ffn_ln1_b"], b2_2=a["L2_ffn_b2"], ln2_g=a["L2_ffn_ln2_g"], ln2_b=a["L2_ffn_ln2_b"],
        bv3=b_kv[:, 1], bo3=a["L3_xattn_b_o"], b1_3=a["L3_ffn_b1"], b2_3=a["L3_ffn_b2"],
        b3_3=a["L3_ffn_b3"]).items()})[0]
    arrays["wk1"] = np.concatenate([a["L1_xattn_Wk"].T, a["L1_xattn_Wk"][partner1].T], 1)
    wg_pad = np.zeros((P, 240), f32)
    wg_pad[:, 112:128] = a["L3_ffn_Wg"]
    wsel = np.stack([a["L2_ffn_Wsel_v"], a["L2_ffn_Wsel_o"]]).transpose(3, 0, 1, 2).reshape(P, 256)
    arrays["wb"] = pack(WB, dict(
        wq1=a["L1_xattn_Wq"].T, wq1p=a["L1_xattn_Wq"][partner1].T,
        wv1=a["L1_xattn_Wv"].T, wo1=a["L1_xattn_Wo"].T,
        wk3=W_kv[:, :, 0].reshape(P, P), wv3=W_kv[:, :, 1].reshape(P, P),
        wq3=a["L3_xattn_W_q"], wo3=a["L3_xattn_W_o"], w_gate=a["L1_ffn_w_gate"].T, wsel=wsel,
        W1=a["L2_ffn_W1"], W2=a["L2_ffn_W2"].reshape(4, P, P).transpose(1, 0, 2).reshape(P, 512),
        wg_pad=wg_pad))
    arrays["w_l0"] = np.concatenate([
        a["L0_ffn_w1"].transpose(1, 0, 2).reshape(P, 4096),
        a["L0_ffn_w2"].reshape(8, 4, P, P).transpose(2, 0, 1, 3).reshape(P, 4096),
        a["L0_ffn_attn_w"].T, a["L0_ffn_next_w"].T], 1)
    arrays["w_l1"] = np.concatenate([
        a["L1_ffn_w1_e"].reshape(1024, P).T, a["L1_ffn_w1_s"].T,
        a["L1_ffn_w3_e"].reshape(1024, P).T, a["L1_ffn_w3_s"].T,
        a["L1_ffn_w2_e"].transpose(0, 2, 1).reshape(8, P, P).transpose(1, 0, 2).reshape(P, 1024),
        a["L1_ffn_w2_s"].T], 1)
    partner2 = np.array([(i + 16) % 32 if i < 32 else i for i in range(64)])
    q, k = a["L2_ffn_Wq"], a["L2_ffn_Wk"]
    four = np.stack([q, q[:, :, partner2], k, k[:, :, partner2]], 1)
    four = four.reshape(HP, 2, 4, P, 64).transpose(0, 3, 2, 1, 4).reshape(HP, P, 512)
    wv = a["L2_ffn_Wv"].reshape(HP, 2, E0, P, 64).transpose(0, 3, 1, 2, 4).reshape(HP, P, 1024)
    wo = a["L2_ffn_Wo"].reshape(HP, 2, E0, 64, P).transpose(0, 1, 3, 2, 4).reshape(HP, P, 1024)
    arrays["w_l2"] = np.concatenate([four, wv, wo], 2)
    arrays["w_l3"] = np.stack([a["L3_ffn_w1"], a["L3_ffn_w2"], a["L3_ffn_w3"]]).transpose(2, 0, 1, 3).reshape(P, L3W)

    d, s = np.arange(P), np.arange(S, dtype=f32)
    inv1 = (f32(1.0) / f32(10000.0) ** (np.arange(0, 8, 2, dtype=f32) / f32(8)))[d % 4]
    ang1 = (inv1[:, None] * s[None]).astype(f32)
    sign1 = np.where(d % 8 < 4, -1, 1)[:, None]
    inv2 = (f32(10000.0) ** (-np.arange(16, dtype=f32) / f32(16)))[d % 16]
    ang2 = (inv2[:, None] * s[None]).astype(f32)
    turned = (d % 64 < 32)[:, None]
    sign2 = np.where(d % 32 < 16, -1, 1)[:, None]
    lower = lambda n: np.tile(np.tri(n, n, -1).reshape(1, n * n), (P, 1))
    arrays["consts"] = pack(CONSTS, dict(
        ident=np.eye(P), cos1=np.cos(ang1), sin1=np.sin(ang1) * sign1,
        cos2=np.where(turned, np.cos(ang2), 1), sin2=np.where(turned, np.sin(ang2) * sign2, 0),
        lt4=lower(4), prefer=np.tile(8 - np.arange(8), (P, 1)),
        headof=(d[:, None] // 8 == np.arange(H)[None]))).astype(f32)
    bmask = np.zeros((P, 320), f32)
    bmask[:, 0:64] = np.where(s[None] <= (d % 64)[:, None], 0, MASKED)
    bmask[:, 64:192] = np.where(d[None] // 64 == d[:, None] // 64, 0, MASKED)
    bmask[:, 192:320] = np.eye(P)
    arrays["bmask"] = bmask.astype(ml_dtypes.bfloat16)
    sel = np.zeros((96, NSEL, P), f32)
    for part in range(3):
        for half in range(2):
            to = slice(64 * half, 64 * half + 64)
            for e in range(8):
                for odd in range(2):
                    sel[48 * odd + 16 * part + 8 * half + e, SEL_PAIR + 8 * odd + e, to] = 1
                sel[16 * part + 2 * e + half, SEL_DUO + e, to] = 1
        for e in range(16):
            sel[16 * part + e, SEL_ONE + e, :] = 1
    arrays["sel"] = sel.astype(ml_dtypes.bfloat16)

    nc = bacc.Bacc("TRN2", target_bir_lowering=False, num_devices=1)
    io = {}
    for name in arrays:
        arrays[name] = np.ascontiguousarray(arrays[name])
        io[name] = nc.dram_tensor(f"in_{name}", arrays[name].shape, mybir.dt.from_np(arrays[name].dtype),
                                  kind="ExternalInput").ap()
    io["y"] = nc.dram_tensor("out_y", (16, S, P), F32, kind="ExternalOutput").ap()
    build(nc, io)
    r = run(nc, [{f"in_{name}": v for name, v in arrays.items()}], core_ids=[0])
    return r.results[0]["out_y"]
```
